# Optimizing a Trainium2 kernel written in Bass

```python
import numpy as np
import jax
import jax.numpy as jnp

def _softmax(x, axis=-1):
    return jax.nn.softmax(x, axis=axis)

def _gelu(x):
    return jax.nn.gelu(x, approximate=True)

def _silu(x):
    return jax.nn.silu(x)

def _sigmoid(x):
    return jax.nn.sigmoid(x)

def _layernorm(x, axis=-1, eps=1e-05):
    m = jnp.mean(x, axis=axis, keepdims=True)
    v = jnp.var(x, axis=axis, keepdims=True)
    return (x - m) / jnp.sqrt(v + eps)

def _scatter_add(tgt, idx, src, axis=0):
    return tgt.at[idx].add(src)

def _segment_sum(src, seg, n):
    return jax.ops.segment_sum(src, seg, n)
kernel_name = 'mk_decoder_preln_d2_seqx_r4_9524b0'

def setup_inputs(seed: int=0):
    np.random.seed(seed)
    _w = jnp.asarray

    def _rec_inputs():
        import jax
        import jax.numpy as jnp
        _rk = jax.random.key(seed)
        x = -0.0002928 + 1 * jax.random.normal(jax.random.fold_in(_rk, 1), (2, 1024, 256), jnp.float32)
        _lenS = 1024 - jax.random.randint(jax.random.fold_in(_rk, 7), (2,), 0, max(1, 1024 // 4) + 1, jnp.int32)
        _lenS2 = 64 - jax.random.randint(jax.random.fold_in(_rk, 8), (2,), 0, max(1, 64 // 4) + 1, jnp.int32)
        _ctx_1024P = jax.random.normal(jax.random.fold_in(_rk, 11), (2, 16, 256), jnp.float32)
        _ctx_1024c = jax.random.dirichlet(jax.random.fold_in(_rk, 511), 0.3 * jnp.ones((16,), jnp.float32), (2, 64))
        _ctx_1024t = jnp.einsum('bsk,bkd->bsd', _ctx_1024c, _ctx_1024P)
        _ctx_1024t = _ctx_1024t * jax.lax.rsqrt(jnp.mean(jnp.square(_ctx_1024t)) + 1e-12) * 0.953939
        ctx_1024 = -1.39393e-06 + 0.999914 * (_ctx_1024t + 0.3 * jax.random.normal(jax.random.fold_in(_rk, 611), (2, 64, 256), jnp.float32))
        _validS = jnp.arange(1024)[None, :] < _lenS[:, None]
        _validS2 = jnp.arange(64)[None, :] < _lenS2[:, None]
        _causal = jnp.tril(jnp.ones((1024, 1024), dtype=bool))
        mask_1x1xSxS2_bk0 = jnp.logical_not(jnp.broadcast_to(_validS2[0:1, None, None, :], (1, 1, 1024, 64)))
        mask_Bx1x1xS2_bf1 = jnp.ones((2, 1, 1, 64), dtype=bool)
        return (x, ctx_1024, mask_1x1xSxS2_bk0, mask_Bx1x1xS2_bf1)
    x, ctx_1024, mask_1x1xSxS2_bk0, mask_Bx1x1xS2_bf1 = _rec_inputs()

    def _L0_attn_setup():
        import jax, jax.numpy as jnp
        import numpy as np
        B, T, D, H = (2, 512, 256, 16)
        key = jax.random.key(seed)
        kx, kq, kk, kv, ko = jax.random.split(key, 5)
        s = D ** (-0.5)
        return {'x': jax.random.normal(kx, (B, T, D), dtype=jnp.float32), 'Wq': jax.random.normal(kq, (D, D), dtype=jnp.float32) * s, 'Wk': jax.random.normal(kk, (D, D), dtype=jnp.float32) * s, 'Wv': jax.random.normal(kv, (D, D), dtype=jnp.float32) * s, 'Wo': jax.random.normal(ko, (D, D), dtype=jnp.float32) * s, 'quadrant_weights': jnp.array([1.0, -0.5, -0.5, 0.25], dtype=jnp.float32)}
    _L0_attn_all = _L0_attn_setup()
    _L0_attn_in = {k: v for k, v in _L0_attn_all.items() if k in ('Wq', 'Wk', 'Wv', 'Wo', 'quadrant_weights')}
    del _L0_attn_all

    def _L0_xattn_setup():
        import jax, jax.numpy as jnp
        import numpy as np
        B, S, D, H = (2, 512, 256, 16)
        DK = D // H

        def _heads(x, W, b):
            y = x @ W.T + b
            return y.reshape(x.shape[0], -1, H, DK).transpose(0, 2, 1, 3)
        key = jax.random.key(seed)
        ks = jax.random.split(key, 11)
        scale = 1.0 / np.sqrt(D)
        inp = {'q': jax.random.normal(ks[0], (B, S, D), jnp.float32), 'k': jax.random.normal(ks[1], (B, S, D), jnp.float32), 'v': jax.random.normal(ks[2], (B, S, D), jnp.float32), 'Wq': jax.random.normal(ks[3], (D, D), jnp.float32) * scale, 'bq': jnp.zeros((D,), jnp.float32), 'Wk': jax.random.normal(ks[4], (D, D), jnp.float32) * scale, 'bk': jnp.zeros((D,), jnp.float32), 'Wv': jax.random.normal(ks[5], (D, D), jnp.float32) * scale, 'bv': jnp.zeros((D,), jnp.float32), 'Wo': jax.random.normal(ks[6], (D, D), jnp.float32) * scale, 'bo': jnp.zeros((D,), jnp.float32), 'mask': jnp.tril(jnp.ones((S, S), bool))[None, None]}
        return inp
    _L0_xattn_all = _L0_xattn_setup()
    _L0_xattn_in = {k: v for k, v in _L0_xattn_all.items() if k in ('Wq', 'bq', 'Wk', 'bk', 'Wv', 'bv', 'Wo', 'bo')}
    del _L0_xattn_all

    def _L0_ffn_setup():
        import jax, jax.numpy as jnp
        import numpy as np
        import math
        DMODEL = 256
        DFF = 1024
        NUM_EXPERTS = 8
        TOPK = 2
        CAP_FACTOR = 1.25
        EPS = 1.1920929e-07

        def _trunc_normal(key, shape, fan_in, scale=1.0):
            std = scale * (1.0 / fan_in) ** 0.5
            return jax.random.truncated_normal(key, -2.0, 2.0, shape, jnp.float32) * std
        key = jax.random.key(seed)
        ks = jax.random.split(key, 5)
        return {'x': jax.random.normal(ks[0], (2, 512, DMODEL), jnp.float32), 'router_weight': _trunc_normal(ks[1], (NUM_EXPERTS, DMODEL), DMODEL), 'ff_pre_act_weight': _trunc_normal(ks[2], (NUM_EXPERTS, DFF, DMODEL), DMODEL), 'gate_weight': _trunc_normal(ks[3], (NUM_EXPERTS, DFF, DMODEL), DMODEL), 'ff_post_act_weight': _trunc_normal(ks[4], (NUM_EXPERTS, DMODEL, DFF), DFF)}
    _L0_ffn_all = _L0_ffn_setup()
    _L0_ffn_in = {k: v for k, v in _L0_ffn_all.items() if k in ('router_weight', 'ff_pre_act_weight', 'gate_weight', 'ff_post_act_weight')}
    del _L0_ffn_all

    def _L1_attn_setup():
        import jax, jax.numpy as jnp
        import numpy as np
        EPS = 1e-05

        def xpos_rotate(x, offset=0, conjugate=False):
            b, s, h, dh = x.shape
            expoent = jnp.arange(0, dh, 2, dtype=jnp.float32) / dh
            angle = 10.0 ** (-4.0 * expoent)
            if conjugate:
                angle = -angle
            pos = jnp.arange(offset, s + offset, dtype=jnp.float32)
            nangle = pos[:, None] * angle[None, :]
            sin = jnp.sin(nangle)[None, :, None, :]
            cos = jnp.cos(nangle)[None, :, None, :]
            x0 = x[..., 0::2]
            x1 = x[..., 1::2]
            rot = jnp.stack([x0 * cos - x1 * sin, x0 * sin + x1 * cos], axis=-1)
            return rot.reshape(b, s, h, dh)

        def decay_mask(nseq, scale):
            idx = jnp.arange(nseq)
            diff = idx[:, None] - idx[None, :]
            mask = (diff >= 0).astype(scale.dtype)
            diff_c = jnp.maximum(diff, 0).astype(scale.dtype)
            logd = diff_c[None, :, :] * jnp.log(scale)[:, None, None]
            return jnp.exp(logd) * mask[None, :, :]

        def group_norm(R, gamma, beta, nheads):
            b, s, d = R.shape
            dh = d // nheads
            Rg = R.reshape(b, s, nheads, dh)
            mu = jnp.mean(Rg, axis=-1, keepdims=True)
            var = jnp.var(Rg, axis=-1, keepdims=True)
            Rn = (Rg - mu) * jax.lax.rsqrt(var + EPS)
            Rn = Rn * gamma.reshape(1, 1, nheads, dh) + beta.reshape(1, 1, nheads, dh)
            return Rn.reshape(b, s, d)
        key = jax.random.key(seed)
        ks = jax.random.split(key, 7)
        b, s, d, h = (2, 512, 256, 16)
        dh = d // h
        x = jax.random.normal(ks[0], (b, s, d), dtype=jnp.float32)
        std_qkv = float(np.sqrt(2.0 / (dh + d)))
        std_o = float(np.sqrt(2.0 / (d + d)))
        WQ = jax.random.normal(ks[1], (h, dh, d), dtype=jnp.float32) * std_qkv
        WK = jax.random.normal(ks[2], (h, dh, d), dtype=jnp.float32) * std_qkv
        WV = jax.random.normal(ks[3], (h, dh, d), dtype=jnp.float32) * std_qkv
        WO = jax.random.normal(ks[4], (d, d), dtype=jnp.float32) * std_o
        gamma = jnp.ones((d,), dtype=jnp.float32)
        beta = jnp.zeros((d,), dtype=jnp.float32)
        return {'x': x, 'WQ': WQ, 'WK': WK, 'WV': WV, 'WO': WO, 'gamma': gamma, 'beta': beta}
    _L1_attn_all = _L1_attn_setup()
    _L1_attn_in = {k: v for k, v in _L1_attn_all.items() if k in ('WQ', 'WK', 'WV', 'WO', 'gamma', 'beta')}
    del _L1_attn_all

    def _L1_xattn_setup():
        import jax, jax.numpy as jnp
        import numpy as np
        D_MODEL = 256
        NUM_HEADS = 16
        D_K = D_MODEL // NUM_HEADS

        def _split_heads(x):
            B, T, _ = x.shape
            return x.reshape(B, T, NUM_HEADS, D_K).transpose(0, 2, 1, 3)
        key = jax.random.key(seed)
        ks = jax.random.split(key, 12)
        B, T = (2, 512)
        s = 1.0 / np.sqrt(D_MODEL)
        inp = {'q': jax.random.normal(ks[0], (B, T, D_MODEL), jnp.float32), 'k': jax.random.normal(ks[1], (B, T, D_MODEL), jnp.float32), 'v': jax.random.normal(ks[2], (B, T, D_MODEL), jnp.float32), 'mask': jnp.ones((B, 1, 1, T), dtype=bool), 'Wq': jax.random.normal(ks[3], (D_MODEL, D_MODEL), jnp.float32) * s, 'bq': jnp.zeros((D_MODEL,), jnp.float32), 'Wk': jax.random.normal(ks[4], (D_MODEL, D_MODEL), jnp.float32) * s, 'bk': jnp.zeros((D_MODEL,), jnp.float32), 'Wv': jax.random.normal(ks[5], (D_MODEL, D_MODEL), jnp.float32) * s, 'bv': jnp.zeros((D_MODEL,), jnp.float32), 'Wo': jax.random.normal(ks[6], (D_MODEL, D_MODEL), jnp.float32) * s, 'bo': jnp.zeros((D_MODEL,), jnp.float32)}
        return inp
    _L1_xattn_all = _L1_xattn_setup()
    _L1_xattn_in = {k: v for k, v in _L1_xattn_all.items() if k in ('Wq', 'bq', 'Wk', 'bk', 'Wv', 'bv', 'Wo', 'bo')}
    del _L1_xattn_all

    def _L1_ffn_setup():
        import jax, jax.numpy as jnp
        import numpy as np
        B, S, H = (1, 512, 256)
        F = 1024
        E = 8
        K = 2
        key = jax.random.key(seed)
        ks = jax.random.split(key, 7)
        s = 0.02
        return {'x': jax.random.normal(ks[0], (B, S, H), jnp.float32), 'gate_w': jax.random.normal(ks[1], (H, E), jnp.float32) * s, 'gate_b': jnp.zeros((E,), jnp.float32), 'w1': jax.random.normal(ks[2], (E, H, F), jnp.float32) * s, 'b1': jnp.zeros((E, F), jnp.float32), 'w2': jax.random.normal(ks[3], (E, F, H), jnp.float32) * s, 'b2': jnp.zeros((E, H), jnp.float32)}
    _L1_ffn_all = _L1_ffn_setup()
    _L1_ffn_in = {k: v for k, v in _L1_ffn_all.items() if k in ('gate_w', 'gate_b', 'w1', 'b1', 'w2', 'b2')}
    del _L1_ffn_all
    return {'x': x, 'ctx_1024': ctx_1024, 'mask_1x1xSxS2_bk0': mask_1x1xSxS2_bk0, 'mask_Bx1x1xS2_bf1': mask_Bx1x1xS2_bf1, 'L0_attn_Wq': _L0_attn_in['Wq'], 'L0_attn_Wk': _L0_attn_in['Wk'], 'L0_attn_Wv': _L0_attn_in['Wv'], 'L0_attn_Wo': _L0_attn_in['Wo'], 'L0_attn_quadrant_weights': _L0_attn_in['quadrant_weights'], 'L0_xattn_Wq': _L0_xattn_in['Wq'], 'L0_xattn_bq': _L0_xattn_in['bq'], 'L0_xattn_Wk': _L0_xattn_in['Wk'], 'L0_xattn_bk': _L0_xattn_in['bk'], 'L0_xattn_Wv': _L0_xattn_in['Wv'], 'L0_xattn_bv': _L0_xattn_in['bv'], 'L0_xattn_Wo': _L0_xattn_in['Wo'], 'L0_xattn_bo': _L0_xattn_in['bo'], 'L0_ffn_router_weight': _L0_ffn_in['router_weight'], 'L0_ffn_ff_pre_act_weight': _L0_ffn_in['ff_pre_act_weight'], 'L0_ffn_gate_weight': _L0_ffn_in['gate_weight'], 'L0_ffn_ff_post_act_weight': _L0_ffn_in['ff_post_act_weight'], 'L1_attn_WQ': _L1_attn_in['WQ'], 'L1_attn_WK': _L1_attn_in['WK'], 'L1_attn_WV': _L1_attn_in['WV'], 'L1_attn_WO': _L1_attn_in['WO'], 'L1_attn_gamma': _L1_attn_in['gamma'], 'L1_attn_beta': _L1_attn_in['beta'], 'L1_xattn_Wq': _L1_xattn_in['Wq'], 'L1_xattn_bq': _L1_xattn_in['bq'], 'L1_xattn_Wk': _L1_xattn_in['Wk'], 'L1_xattn_bk': _L1_xattn_in['bk'], 'L1_xattn_Wv': _L1_xattn_in['Wv'], 'L1_xattn_bv': _L1_xattn_in['bv'], 'L1_xattn_Wo': _L1_xattn_in['Wo'], 'L1_xattn_bo': _L1_xattn_in['bo'], 'L1_ffn_gate_w': _L1_ffn_in['gate_w'], 'L1_ffn_gate_b': _L1_ffn_in['gate_b'], 'L1_ffn_w1': _L1_ffn_in['w1'], 'L1_ffn_b1': _L1_ffn_in['b1'], 'L1_ffn_w2': _L1_ffn_in['w2'], 'L1_ffn_b2': _L1_ffn_in['b2']}

def reference(x, ctx_1024, mask_1x1xSxS2_bk0, mask_Bx1x1xS2_bf1, L0_attn_Wq, L0_attn_Wk, L0_attn_Wv, L0_attn_Wo, L0_attn_quadrant_weights, L0_xattn_Wq, L0_xattn_bq, L0_xattn_Wk, L0_xattn_bk, L0_xattn_Wv, L0_xattn_bv, L0_xattn_Wo, L0_xattn_bo, L0_ffn_router_weight, L0_ffn_ff_pre_act_weight, L0_ffn_gate_weight, L0_ffn_ff_post_act_weight, L1_attn_WQ, L1_attn_WK, L1_attn_WV, L1_attn_WO, L1_attn_gamma, L1_attn_beta, L1_xattn_Wq, L1_xattn_bq, L1_xattn_Wk, L1_xattn_bk, L1_xattn_Wv, L1_xattn_bv, L1_xattn_Wo, L1_xattn_bo, L1_ffn_gate_w, L1_ffn_gate_b, L1_ffn_w1, L1_ffn_b1, L1_ffn_w2, L1_ffn_b2):
    import jax
    import jax.numpy as jnp

    def _L0_attn_ref(x, Wq, Wk, Wv, Wo, quadrant_weights):
        import jax, jax.numpy as jnp
        import numpy as np
        B, T, D, H = (2, 512, 256, 16)
        Bx, Tx, Dx = x.shape
        d = Dx // H
        h = d // 2
        scale = h ** (-0.5)
        q = (x @ Wq).reshape(Bx, Tx, H, d).transpose(0, 2, 1, 3)
        k = (x @ Wk).reshape(Bx, Tx, H, d).transpose(0, 2, 1, 3)
        v = (x @ Wv).reshape(Bx, Tx, H, d).transpose(0, 2, 1, 3)
        q1, q2 = (q[..., :h], q[..., h:])
        k1, k2 = (k[..., :h], k[..., h:])
        w = jax.nn.softmax(quadrant_weights)
        k_eff1 = w[0] * k1 + w[1] * k2
        k_eff2 = w[2] * k1 + w[3] * k2
        attn = (jnp.einsum('bhqc,bhkc->bhqk', q1, k_eff1) + jnp.einsum('bhqc,bhkc->bhqk', q2, k_eff2)) * scale
        attn = jax.nn.softmax(attn, axis=-1)
        out = jnp.einsum('bhqk,bhkd->bhqd', attn, v)
        out = out.transpose(0, 2, 1, 3).reshape(Bx, Tx, Dx)
        return out @ Wo

    def _L0_xattn_ref(q, k, v, Wq, bq, Wk, bk, Wv, bv, Wo, bo, mask):
        import jax, jax.numpy as jnp
        import numpy as np
        B, S, D, H = (2, 512, 256, 16)
        DK = D // H

        def _heads(x, W, b):
            y = x @ W.T + b
            return y.reshape(x.shape[0], -1, H, DK).transpose(0, 2, 1, 3)
        qh = _heads(q, Wq, bq)
        kh = _heads(k, Wk, bk)
        vh = _heads(v, Wv, bv)
        scores = jnp.einsum('bhsd,bhtd->bhst', qh, kh) / jnp.sqrt(jnp.float32(DK))
        scores = jnp.where(mask, scores, jnp.float32(-1000.0))
        attn = jax.nn.softmax(scores, axis=-1)
        out = jnp.einsum('bhst,bhtd->bhsd', attn, vh)
        out = out.transpose(0, 2, 1, 3).reshape(q.shape[0], -1, D)
        return out @ Wo.T + bo

    def _L0_ffn_ref(x, router_weight, ff_pre_act_weight, gate_weight, ff_post_act_weight):
        import jax, jax.numpy as jnp
        import numpy as np
        import math
        DMODEL = 256
        DFF = 1024
        NUM_EXPERTS = 8
        TOPK = 2
        CAP_FACTOR = 1.25
        EPS = 1.1920929e-07

        def _trunc_normal(key, shape, fan_in, scale=1.0):
            std = scale * (1.0 / fan_in) ** 0.5
            return jax.random.truncated_normal(key, -2.0, 2.0, shape, jnp.float32) * std
        orig_shape = x.shape
        h = x.reshape(-1, DMODEL)
        T = h.shape[0]
        logits = jnp.einsum('th,eh->te', h, router_weight)
        probs = jax.nn.softmax(logits.astype(jnp.float32), axis=-1)
        topk_probs, selected = jax.lax.top_k(probs, TOPK)
        topk_probs = topk_probs / jnp.maximum(topk_probs.sum(-1, keepdims=True), EPS)
        flat_tokens = jnp.repeat(jnp.arange(T), TOPK)
        flat_experts = selected.reshape(-1)
        flat_weights = topk_probs.reshape(-1)
        A = T * TOPK
        capacity = max(1, math.ceil(CAP_FACTOR * A / NUM_EXPERTS))
        weight_order = jnp.argsort(-flat_weights, stable=True)
        grouped_order = jnp.argsort(flat_experts[weight_order], stable=True)
        sort_order = weight_order[grouped_order]
        se = flat_experts[sort_order]
        st = flat_tokens[sort_order]
        sw = flat_weights[sort_order]
        counts = jnp.bincount(se, length=NUM_EXPERTS)
        offsets = jnp.cumsum(counts) - counts
        slot = jnp.arange(A) - offsets[se]
        keep = slot < capacity
        sw = jnp.where(keep, sw, 0.0)
        token_wsum = jnp.zeros(T, jnp.float32).at[st].add(sw)
        kept_w = sw / jnp.maximum(token_wsum[st], EPS)
        FC = NUM_EXPERTS * capacity
        dispatch = jnp.where(keep, se * capacity + slot, FC)
        expert_inputs = jnp.zeros((FC + 1, DMODEL), x.dtype).at[dispatch].set(h[st])
        expert_inputs = expert_inputs[:FC].reshape(NUM_EXPERTS, capacity, DMODEL)
        pre = jnp.einsum('ech,edh->ecd', expert_inputs, ff_pre_act_weight)
        gate = jnp.einsum('ech,edh->ecd', expert_inputs, gate_weight)
        expert_out = jnp.einsum('ecd,ehd->ech', pre * jax.nn.silu(gate), ff_post_act_weight)
        eo_flat = jnp.concatenate([expert_out.reshape(FC, DMODEL), jnp.zeros((1, DMODEL), x.dtype)], axis=0)
        updates = eo_flat[dispatch] * kept_w.astype(x.dtype)[:, None]
        out = jnp.zeros((T, DMODEL), x.dtype).at[st].add(updates)
        return out.reshape(orig_shape)

    def _L1_attn_ref(x, WQ, WK, WV, WO, gamma, beta):
        import jax, jax.numpy as jnp
        import numpy as np
        EPS = 1e-05

        def xpos_rotate(x, offset=0, conjugate=False):
            b, s, h, dh = x.shape
            expoent = jnp.arange(0, dh, 2, dtype=jnp.float32) / dh
            angle = 10.0 ** (-4.0 * expoent)
            if conjugate:
                angle = -angle
            pos = jnp.arange(offset, s + offset, dtype=jnp.float32)
            nangle = pos[:, None] * angle[None, :]
            sin = jnp.sin(nangle)[None, :, None, :]
            cos = jnp.cos(nangle)[None, :, None, :]
            x0 = x[..., 0::2]
            x1 = x[..., 1::2]
            rot = jnp.stack([x0 * cos - x1 * sin, x0 * sin + x1 * cos], axis=-1)
            return rot.reshape(b, s, h, dh)

        def decay_mask(nseq, scale):
            idx = jnp.arange(nseq)
            diff = idx[:, None] - idx[None, :]
            mask = (diff >= 0).astype(scale.dtype)
            diff_c = jnp.maximum(diff, 0).astype(scale.dtype)
            logd = diff_c[None, :, :] * jnp.log(scale)[:, None, None]
            return jnp.exp(logd) * mask[None, :, :]

        def group_norm(R, gamma, beta, nheads):
            b, s, d = R.shape
            dh = d // nheads
            Rg = R.reshape(b, s, nheads, dh)
            mu = jnp.mean(Rg, axis=-1, keepdims=True)
            var = jnp.var(Rg, axis=-1, keepdims=True)
            Rn = (Rg - mu) * jax.lax.rsqrt(var + EPS)
            Rn = Rn * gamma.reshape(1, 1, nheads, dh) + beta.reshape(1, 1, nheads, dh)
            return Rn.reshape(b, s, d)
        b, s, d = x.shape
        h, dh, _ = WQ.shape
        Q = jnp.einsum('bsd,hud->bshu', x, WQ)
        K = jnp.einsum('bsd,hud->bshu', x, WK)
        V = jnp.einsum('bsd,hud->bshu', x, WV)
        Q = xpos_rotate(Q)
        K = xpos_rotate(K)
        QK = jnp.einsum('bihd,bjhd->bhij', Q, K)
        scale = 1.0 - 2.0 ** (-5.0 - jnp.arange(h, dtype=jnp.float32))
        D = decay_mask(s, scale)
        QKD = QK * D[None]
        R = jnp.einsum('bhij,bjhd->bihd', QKD, V)
        R = R.reshape(b, s, d)
        R = group_norm(R, gamma, beta, h)
        y = R @ WO
        return y

    def _L1_xattn_ref(q, k, v, mask, Wq, bq, Wk, bk, Wv, bv, Wo, bo):
        import jax, jax.numpy as jnp
        import numpy as np
        D_MODEL = 256
        NUM_HEADS = 16
        D_K = D_MODEL // NUM_HEADS

        def _split_heads(x):
            B, T, _ = x.shape
            return x.reshape(B, T, NUM_HEADS, D_K).transpose(0, 2, 1, 3)
        B, Tq, _ = q.shape
        qh = _split_heads(q @ Wq + bq)
        kh = _split_heads(k @ Wk + bk)
        vh = _split_heads(v @ Wv + bv)
        scores = jnp.einsum('bhqd,bhkd->bhqk', qh, kh) / jnp.sqrt(jnp.float32(D_K))
        scores = jnp.where(mask, scores, -jnp.inf)
        attn = jax.nn.softmax(scores.astype(jnp.float32), axis=-1).astype(scores.dtype)
        out = jnp.einsum('bhqk,bhkd->bhqd', attn, vh)
        out = out.transpose(0, 2, 1, 3).reshape(B, Tq, D_MODEL)
        return out @ Wo + bo

    def _L1_ffn_ref(x, gate_w, gate_b, w1, b1, w2, b2):
        import jax, jax.numpy as jnp
        import numpy as np
        B, S, H = (1, 512, 256)
        F = 1024
        E = 8
        K = 2
        Bq, Sq, Hq = x.shape
        T = Bq * Sq
        xt = x.reshape(T, Hq)
        logits = xt @ gate_w + gate_b
        probs = jax.nn.softmax(logits, axis=-1)
        top_v, top_i = jax.lax.top_k(probs, K)
        top_v = top_v / jnp.sum(top_v, axis=-1, keepdims=True)
        combine = jnp.zeros((T, E), x.dtype).at[jnp.arange(T)[:, None], top_i].set(top_v)
        h = jax.nn.relu(jnp.einsum('th,ehf->etf', xt, w1) + b1[:, None, :])
        y = jnp.einsum('etf,efh->eth', h, w2) + b2[:, None, :]
        out = jnp.einsum('te,eth->th', combine, y)
        return out.reshape(Bq, Sq, Hq)
    x = x + _L0_attn_ref(_layernorm(x, axis=-1), L0_attn_Wq, L0_attn_Wk, L0_attn_Wv, L0_attn_Wo, L0_attn_quadrant_weights)
    x = x + _L0_xattn_ref(_layernorm(x, axis=-1), ctx_1024, ctx_1024, L0_xattn_Wq, L0_xattn_bq, L0_xattn_Wk, L0_xattn_bk, L0_xattn_Wv, L0_xattn_bv, L0_xattn_Wo, L0_xattn_bo, mask_1x1xSxS2_bk0)
    x = x + _L0_ffn_ref(_layernorm(x, axis=-1), L0_ffn_router_weight, L0_ffn_ff_pre_act_weight, L0_ffn_gate_weight, L0_ffn_ff_post_act_weight)
    x = x + _L1_attn_ref(_layernorm(x, axis=-1), L1_attn_WQ, L1_attn_WK, L1_attn_WV, L1_attn_WO, L1_attn_gamma, L1_attn_beta)
    x = x + _L1_xattn_ref(_layernorm(x, axis=-1), ctx_1024, ctx_1024, mask_Bx1x1xS2_bf1, L1_xattn_Wq, L1_xattn_bq, L1_xattn_Wk, L1_xattn_bk, L1_xattn_Wv, L1_xattn_bv, L1_xattn_Wo, L1_xattn_bo)
    x = x + _L1_ffn_ref(_layernorm(x, axis=-1), L1_ffn_gate_w, L1_ffn_gate_b, L1_ffn_w1, L1_ffn_b1, L1_ffn_w2, L1_ffn_b2)
    return x

_drawn_inputs = setup_inputs


def setup_inputs(seed=0):
    import zlib

    import numpy as np

    out = dict(_drawn_inputs(seed))
    spreads = {'L0_xattn_bq': (0.0, 0.1),
     'L0_xattn_bk': (0.0, 0.8),
     'L0_xattn_bv': (0.0, 0.1),
     'L0_xattn_bo': (0.0, 0.1),
     'L1_attn_gamma': (1.0, 0.2),
     'L1_attn_beta': (0.0, 0.1),
     'L1_xattn_bq': (0.0, 0.539),
     'L1_xattn_bk': (0.0, 0.8),
     'L1_xattn_bv': (0.0, 0.1),
     'L1_xattn_bo': (0.0, 0.1),
     'L1_ffn_gate_b': (0.0, 0.1),
     'L1_ffn_b1': (0.0, 0.45),
     'L1_ffn_b2': (0.0, 0.1)}
    factors = {}
    for name, (base, spread) in spreads.items():
        noise = np.random.default_rng([zlib.crc32(name.encode()), seed]).standard_normal(out[name].shape)
        drawn = base * np.exp(spread * noise) if base else spread * noise
        out[name] = jnp.asarray(drawn.astype(out[name].dtype))
    for name, factor in factors.items():
        out[name] = (out[name] * factor).astype(out[name].dtype)
    return out
```

```python
from contextlib import ExitStack, contextmanager

import numpy as np
import concourse.bass as bass
from concourse import mybir

F32 = mybir.dt.float32
BF16 = mybir.dt.bfloat16
I32 = mybir.dt.int32
U32 = mybir.dt.uint32
U8 = mybir.dt.uint8
ALU = mybir.AluOpType
ACT = mybir.ActivationFunctionType
AX = mybir.AxisListType

P = 128
B, S, D, H, DH = 2, 1024, 256, 16, 16
T = B * S
NT = T // P
NP = NT // 2
NX = 40
TB = S // P
SC = 64
E, F = 8, 1024
KC = D // P
HG = P // DH
CAP = 640
LN_EPS = 1e-5
LAG = 4


class Sig:

    def __init__(self, sem, per=1):
        self.sem, self.per, self.base = sem, per, LAG * per

    def upto(self, step, n=None):
        return self.base + self.per * step + (self.per if n is None else n)


class Chain:

    def __init__(self, eng, sem):
        self.eng, self.sem, self.n, self.loop = eng, sem, 0, None

    def __call__(self, ins):
        ins.then_inc(self.sem, 1)
        self.n += 1
        self.eng.wait_ge(self.sem, self.n if self.loop is None else self.loop * self.k + self.n)
        return ins

    @contextmanager
    def fori(self, count, k):
        with self.eng.Fori(0, count) as i:
            self.loop, self.k, before = i, k, self.n
            yield i
            assert self.n - before == k, f"{self.n - before} links in the body, not {k}"
        self.loop, self.n = None, before + count * k


def decoder(nc, x_in, ctxT, mask0, mask1, w, out):
    ctx = ExitStack()
    with ctx:
        def sb(name, shape, dt=F32):
            return ctx.enter_context(nc.sbuf_tensor(name, shape, dt))

        def sem(name):
            return ctx.enter_context(nc.semaphore(name))

        sigs = []

        def sig(name, per=1):
            s = Sig(sem(name), per)
            sigs.append(s)
            return s

        def dram(name, shape, dt=F32):
            return nc.dram_tensor(name, shape, dt, kind="Internal").ap()

        ps = ctx.enter_context(nc.psum_tensor("ps", [P, 8, 512], F32))

        xr = sb("xr", [P, NT, D])
        ident = sb("ident", [P, P])
        identb = sb("identb", [P, P], BF16)
        xn = sb("xn", [P, 2, 2, D])
        xT = sb("xT", [P, 2, KC, 2 * P])
        wide = sb("wide", [P, 16384])
        idle = sb("idle", [P, 1])
        zeros = sb("zeros", [P, 4])
        st = sb("st", [P, 2, 6])
        mv = sb("mv", [P, 2, 2])
        nv = sb("nv", [P, 4, 2])
        O_all = sb("O_all", [P, NT, D])
        lg = sb("lg", [P, NT, E])

        EPS = 1.1920929e-07
        BITS = 30
        nochoice = float(1 << 20)
        desc = sb("desc", [P, E])
        first = sb("first", [P, E])
        bits = sb("bits", [P, BITS, E], I32)
        lower = sb("lower", [P, P], BF16)
        onesb = sb("onesb", [P, P], BF16)
        lowf = sb("lowf", [P, P])
        pb = sb("pb", [P, NT, E])
        pe_ = sb("pexp", [P, NT, E])
        oh = [sb(f"oh{k}", [P, NT, E]) for k in range(2)]
        tm = sb("tm", [P, NT, E])
        tb = sb("tb", [P, NT, E], BF16)
        Wt = sb("Wt", [P, NT, E])
        Ct = sb("Ct", [P, NT, E])
        Kp = sb("Kp", [P, NT, E])
        tk = sb("tk", [P, 8, NT])
        top = [sb(f"top{k}", [P, NT]) for k in range(2)]
        gw = [sb(f"gw{k}", [P, NT]) for k in range(2)]
        thr = sb("thr", [P, E], I32)
        cand = sb("cand", [P, E], I32)
        c8 = sb("c8", [P, E])
        c8b = sb("c8b", [P, E], BF16)
        idxS = [sb(f"idxS{k}", [P, NT], U32) for k in range(2)]
        idxG = [sb(f"idxG{k}", [P, NT], U32) for k in range(2)]
        zrow = sb("zrow", [P, D])
        before_e = sb("before_e", [P, E, E])
        tile_no = sb("tile_no", [P, NX])
        m3 = sb("m3", [P, E, E])
        n8 = sb("n8", [P, E])
        n8i = sb("n8i", [P, E], I32)
        base8 = sb("base8", [P, E])
        ex = sb("ex", [P, NX, E])
        exf = sb("exf", [P, NX])
        exi = sb("exi", [P, NX], I32)

        chain_dve = sem("chain_dve")
        chain_act = sem("chain_act")
        chain_pool = sem("chain_pool")
        barrier = sem("barrier")
        loaded = sem("loaded")
        stored = sem("stored")

        qk_parts = dram("qk_parts", [3, B, 2 * D, S], BF16)
        v_heads = dram("v_heads", [B, H, P, TB, 32])
        sa = ExitStack()
        ctx.enter_context(sa)

        def sbA(name, shape, dt=F32):
            return sa.enter_context(nc.sbuf_tensor(name, shape, dt))

        wqA = sbA("wqA", [P, KC, D])
        wkA = sbA("wkA", [P, KC, D])
        wkE = sbA("wkE", [P, KC, D])
        wvA = sbA("wvA", [P, KC, D])
        qwB = sbA("qwB", [P, 4])
        qsm = sbA("qsm", [P, 4, 4])
        parts = sbA("parts", [P, 2, 3, 4, 2 * P], BF16)
        rest = sbA("rest", [P, 2, 4, 2 * P])
        vslot = sbA("vslot", [P, 2, 2, H, 32])
        QS = sbA("QS", [P, 4, S], BF16)
        KS = sbA("KS", [P, 4, S], BF16)
        VS = sbA("VS", [P, 4, TB, 32])
        PT = sbA("PT", [P, 4, 512])
        Osb = sbA("Osb", [P, 512])
        mx = sbA("mx", [P, 2, TB])
        mneg = sbA("mneg", [P, 2, TB])
        mpart = sbA("mpart", [P, 2, 3, TB], BF16)
        mrow = sbA("mrow", [24, 2, P], BF16)
        sel = sbA("sel", [P, 64])
        rec = sbA("rec", [P, 4, 2])

        a_xn = sig("a_xn")
        a_tr = sig("a_tr")
        a_xt = sig("a_xt")
        a_qk = sig("a_qk")
        a_v = sig("a_v")
        a_p1 = sig("a_p1")
        a_r = sig("a_r")
        a_p2 = sig("a_p2")
        a_p3 = sig("a_p3")
        a_vs = sig("a_vs")
        a_st = [sig(f"a_st{s}", 5 * 16) for s in range(2)]
        h_ld = [sig(f"h_ld{s}", 7 * 16) for s in range(4)]
        h_mr = [sig(f"h_mr{s}", 16) for s in range(4)]
        h_s = sig("h_s", 8)
        h_rm = sig("h_rm", 8)
        h_mp = sig("h_mp")
        h_mt = sig("h_mt")
        h_mc = sig("h_mc")
        h_st = sig("h_st", 16)
        h_e = sig("h_e", 16)
        h_pv = sig("h_pv", 16)
        h_ev = sig("h_ev")
        h_fin = sig("h_fin")
        h_no = sig("h_no")

        sa.close()

        sx = ExitStack()
        ctx.enter_context(sx)

        def sbX(name, shape, dt=F32):
            return sx.enter_context(nc.sbuf_tensor(name, shape, dt))

        xw = {n: sbX("xw_" + n, [P, KC, D]) for n in ("q", "k", "v", "o")}
        woA = sbX("woA", [P, KC, D])
        ctxs = sbX("ctxs", [P, KC, B * SC])
        ctx2 = sbX("ctx2", [P, B, KC, 2, SC])
        bq = sbX("bq", [P, KC])
        bq4 = sbX("bq4", [P, KC])
        bk = sbX("bk", [P, KC])
        bv = sbX("bv", [P, D])
        bo = sbX("bo", [P, D])
        hmask = sbX("hmask", [P, HG])
        halves = sbX("halves", [P, 2])
        kc = sbX("kc", [P, KC, B * SC])
        vd = sbX("vd", [P, B, D])
        Kbd = sbX("Kbd", [P, B, KC, HG, SC])
        Vbd = sbX("Vbd", [P, B, HG, 2, DH + 1])
        mask_u8 = sbX("mask_u8", [P, TB, SC], U8)
        mask_no = sbX("mask_no", [P, TB, SC], U8)
        mslot = sbX("mslot", [P, 2, 2, SC], U8)
        fill0 = sbX("fill0", [P, 1])
        mask1_u8 = sbX("mask1_u8", [P, B, SC], U8)
        mask1_f = sbX("mask1_f", [P, B, SC])
        rw = sbX("rw", [P, KC, E])
        rb = sbX("rb", [P, E])
        orow = sbX("orow", [P, 2, D])
        orow2 = sbX("orow2", [P, 2, D])
        oT = sbX("oT", [P, KC, 2 * P])
        oT2 = sbX("oT2", [P, KC, 2 * P])
        qT = sbX("qT", [P, KC, 2 * P])
        pr = sbX("pr", [P, 2, H, SC])
        mxx = sbX("mxx", [P, 2, H])
        prT = sbX("prT", [P, HG, P])
        recx = sbX("recx", [P, H])

        x_ld = sem("x_ld")
        x_ctx = sig("x_ctx", 2)
        x_cr = sig("x_cr", 1)
        x_or = sig("x_or", 16)
        x_ms = [sig(f"x_ms{s}", 16) for s in range(2)]
        x_res = sig("x_res")
        x_lnA, x_lnB = sig("x_lnA"), sig("x_lnB")
        x_no = sig("x_no", 2)
        x_sm = sig("x_sm", 2)
        x_rb = sig("x_rb")
        x_lg = sig("x_lg")
        x_t = [sig(f"x_t{r}") for r in range(4)]
        x_te = [sig(f"x_te{r}") for r in range(4)]
        x_oA, x_oB = sig("x_oA"), sig("x_oB")
        x_q = sig("x_q")
        x_qe = sig("x_qe")
        x_s = sig("x_s", 2)
        x_e = sig("x_e", 2)
        x_pt = sig("x_pt", 2)
        x_pe = sig("x_pe", 2)
        x_av = sig("x_av", 2)
        x_r = sig("x_r")
        x_mk, x_m1 = sem("x_mk"), sem("x_m1")
        x_xa = sig("x_xa", 16)

        sg_ = ExitStack()
        ctx.enter_context(sg_)

        def sbG(name, shape, dt=F32):
            return sg_.enter_context(nc.sbuf_tensor(name, shape, dt))

        xs0 = dram("xs0", [E * CAP, D])
        ys0 = dram("ys0", [E * CAP, D])
        xs1 = dram("xs1", [NX * P, D])
        ys1 = dram("ys1", [NX * P, D])
        xe = sbG("xe", [P, 2, 5, D])
        xTe = sbG("xTe", [P, KC, CAP])
        hTe = sbG("hTe", [P, F // P, CAP])
        sgt = sbG("sgt", [P, 2, CAP // 2])
        yrow = pr[:].rearrange("p j h k -> p (j h k)")[:, 0:5 * D].rearrange("p (r d) -> p r d", r=5)
        yg = hTe[:].rearrange("p f c -> p (f c)")[:, 0:4 * 2 * D].rearrange("p (q k d) -> p q k d", q=4, k=2)

        sg_.close()
        sr = ExitStack()
        ctx.enter_context(sr)

        def sbR(name, shape, dt=F32):
            return sr.enter_context(nc.sbuf_tensor(name, shape, dt))

        wqk = sbR("wqk", [P, KC, 2 * D])
        wvR = sbR("wvR", [P, KC, D])
        woR = sbR("woR", [P, KC, D])
        turns = sbR("turns", [P, 2, TB, DH // 2])
        decay = sbR("decay", [P, 2, H])
        causal = sbR("causal", [P, P])
        bdg = sbR("bdg", [P, KC, P])
        gP = sbR("gP", [P, KC])
        keepS = sbR("keepS", [P, NT])
        gamma = sbR("gamma", [P, KC])
        beta = sbR("beta", [P, KC])
        qkr = sbR("qkr", [P, 2, 2 * D])
        half_turn = sbR("half_turn", [P, 2 * D])
        vR = sbR("vR", [P, 2, D])
        qkT = sbR("qkT", [P, 2 * KC, P])
        qbd = sbR("qbd", [P, KC, HG, P])
        wS = sbR("wS", [P, 2, 4, P])
        State = sbR("State", [P, KC, P])
        newS = sbR("newS", [P, KC, P])
        Rr = sbR("Rr", [P, 2, D])
        Rq = sbR("Rq", [P, D])
        gmean = sbR("gmean", [P, H])
        gvar = sbR("gvar", [P, H])
        gnv = sbR("gnv", [P, 4, H])
        oTR = sbR("oTR", [P, KC, P])

        e_ld = sem("e_ld")
        e_z = sem("e_z")
        e_ln = sig("e_ln")
        e_tx = sig("e_tx")
        e_xt = sig("e_xt")
        e_qk = sig("e_qk")
        e_rot = sig("e_rot")
        e_tq = sig("e_tq")
        e_ex = sig("e_ex", 3)
        e_s = sig("e_s", 4)
        e_m = sig("e_m", 4)
        e_av = sig("e_av", 4)
        e_rv = sig("e_rv")
        e_su = sig("e_su")
        e_st = sig("e_st")
        e_gn = sig("e_gn")
        e_ot = sig("e_ot")
        e_oc = sig("e_oc")
        e_y = sig("e_y")
        e_rs = sig("e_rs")

        sr.close()
        sx.close()
        se = ExitStack()
        ctx.enter_context(se)

        def sbE(name, shape, dt=F32):
            return se.enter_context(nc.sbuf_tensor(name, shape, dt))

        w2s = sbE("w2s", [P, E, F // P, D])
        b1s = sbE("b1s", [P, E, F // P])
        b2s = sbE("b2s", [P, E, D])
        rows1 = sbE("rows1", [P, 2, D])
        xTm = sbE("xTm", [P, 2, KC, P])
        hrow = sbE("hrow", [P, 2, 512])
        hTm = sbE("hTm", [P, F // P, P])
        yrow1 = sbE("yrow1", [P, 2, D])
        zero1 = sbE("zero1", [P, 1])
        m_w = sem("m_w")
        m_w2 = sem("m_w2")
        m_x = [sig(f"m_x{s}", 16) for s in range(2)]
        m_t = sig("m_t")
        m_tc = sig("m_tc")
        m_h = sig("m_h", 2)
        m_hc = sig("m_hc", 2)
        m_ht = sig("m_ht", 2)
        m_a = sig("m_a", 2)
        m_y = sig("m_y")
        m_yc = sig("m_yc")
        m_st = [sig(f"m_st{s}", 16) for s in range(2)]
        yg1 = w2s[:].rearrange("p e g d -> p (e g d)")[:, 0:4 * 2 * D].rearrange("p (q k d) -> p q k d", q=4, k=2)

        r_sub = sem("r_sub")
        r_exp = sem("r_exp")
        r_rhs = sem("r_rhs")
        r_sum = sem("r_sum")
        r_idx = sem("r_idx")
        g_z = sem("g_z")
        g_sc = [sem("g_sc0"), sem("g_sc1")]
        f_w = [sig(f"f_w{s}", 48) for s in range(2)]
        f_x = [sig(f"f_x{s}", 16) for s in range(2)]
        f_t = sig("f_t")
        f_te = sig("f_te", 3)
        f_h = sig("f_h", 16)
        f_a = sig("f_a", 16)
        f_m = sig("f_m", 16)
        f_y = sig("f_y", 5)
        f_ye = sig("f_ye", 5)
        f_ys = sig("f_ys", 16)
        g_ld = [sem(f"g_ld{q}") for q in range(4)]
        g_use = sem("g_use")
        z_set = sem("z_set")

        q_sub, q_exp, v_set, ones_set, sa_ready, a_w = (sem(n) for n in ("q_sub", "q_exp", "v_set", "ones_set", "sa_ready", "a_w"))
        A_LOADS = 16 * 16
        NLOAD = [0]

        def load(eng, dst, src):
            eng.dma_start(dst, src).then_inc(loaded, 16)
            NLOAD[0] += 16

        def meet(eng, n):
            eng.drain().then_inc(barrier, 1)
            eng.wait_ge(barrier, 5 * n)

        block = ctx.enter_context(nc.Block())

        chunked = lambda ap: ap.rearrange("(k p) n -> p k n", p=P)

        def finish(sp):
            sp.dma_start(out.rearrange("b (t p) d -> p (b t) d", p=P), xr[:]).then_inc(stored, 16)
            sp.wait_ge(stored, 16)


        def ln_rows(v, c, u, s, xn_sig, tr_sig):
            v.memset(idle[:, 0:1], 0.0)
            for j in range(2):
                ins = v.bn_stats(st[:, j, :], xr[:, bass.ds(2 * u + j, 1), :].rearrange("p a d -> p (a d)"))
            c(ins)
            v.memset(idle[:, 0:1], 0.0)
            for j in range(2):
                ins = v.bn_aggr(mv[:, j, :], st[:, j, :])
            c(ins)
            rsqrt(v, c, nv, mv[:, :, 1], LN_EPS)
            v.wait_ge(tr_sig.sem, tr_sig.upto(u - 2))
            for j in range(2):
                ins = v.tensor_scalar(xn[:, s, j, :], xr[:, bass.ds(2 * u + j, 1), :].rearrange("p a d -> p (a d)"),
                                      mv[:, j, 0:1], nv[:, 0, j:j + 1], ALU.subtract, ALU.mult)
            ins.then_inc(xn_sig.sem, 1)

        def rsqrt(v, c, n4, var, eps):
            y, a, e, g = (n4[:, i] for i in range(4))
            c(v.tensor_scalar(e, var, float(eps), None, ALU.add))
            c(v.tensor_scalar(a.bitcast(I32), e.bitcast(I32), 1, None, ALU.logical_shift_right))
            c(v.tensor_scalar(y.bitcast(I32), a.bitcast(I32), -1.0, float(0x5F3759DF), ALU.mult, ALU.add))
            for _ in range(3):
                c(v.tensor_tensor(a, y, y, ALU.mult))
                c(v.tensor_tensor(g, a, e, ALU.mult))
                c(v.tensor_scalar(a, g, -0.5, 1.5, ALU.mult, ALU.add))
                c(v.tensor_tensor(y, y, a, ALU.mult))

        def transpose_rows(pe, u, s, bank, xn_sig, xt_sig, tr_sig):
            pe.wait_ge(xn_sig.sem, xn_sig.upto(u))
            pe.wait_ge(xt_sig.sem, xt_sig.upto(u - 2))
            for k in range(KC):
                for j in range(2):
                    ins = pe.transpose(ps[:, bank, (2 * k + j) * P:(2 * k + j + 1) * P],
                                       xn[:, s, j, k * P:(k + 1) * P], ident[:])
            ins.then_inc(tr_sig.sem, 1)

        def xname(layer, what):
            return w[f"L{layer}_xattn_{what}"]

        X_LOADS = [16 * 19, 16 * 19 + 16 * 10]

        def sp_cross_weights(sp, layer):
            def ld(dst, src):
                sp.dma_start(dst, src).then_inc(x_ld, 16)

            for n in "qkvo":
                ld(xw[n][:], chunked(xname(layer, "W" + n)))
            ld(bq[:], xname(layer, "bq"))
            ld(bk[:], xname(layer, "bk"))
            ld(bv[:], xname(layer, "bv").partition_broadcast(P))
            ld(bo[:], xname(layer, "bo").partition_broadcast(P))
            ld(rw[:], chunked(w["L0_ffn_router_weight"] if layer == 0 else w["L1_ffn_gate_w"]))
            ld(rb[:], w["L1_ffn_gate_b"].partition_broadcast(P))
            if layer == 0:
                cv = ctxT.rearrange("(k p) (b s) -> p k b s", p=P, b=B)
                ld(ctxs[:], ctxT.rearrange("(k p) s -> p k s", p=P))
                for b in range(B):
                    for e in range(2):
                        ld(ctx2[:, b, :, e, :], cv[:, :, b, :])
                ld(woA[:], chunked(w["L0_attn_Wo"]))
                ld(hmask[:], w["c_hmask"])
                ld(halves[:], w["c_halves"])
                ld(mask_u8[:], mask0.rearrange("a b (t p) s -> p (a b t) s", p=P))
            else:
                sp.dma_start(mask1_u8[:], mask1.rearrange("b x y s -> (b x y s)").partition_broadcast(P))\
                  .then_inc(x_m1, 16)

        def sp_cross(sp, layer):
            def feed(u, s):
                U = u + layer * NP
                if layer == 0:
                    sp.wait_ge(x_t[0].sem, x_t[0].upto(U - 1))
                    sp.dma_start(orow[:], O_all[:, bass.ds(2 * u, 2), :]).then_inc(x_or.sem, 16)
                    sp.wait_ge(x_sm.sem, x_sm.upto(U - 2))
                    sp.dma_start(mslot[:, s, :, :], mask_no[:, bass.ds((2 * u) % TB, 2), :])\
                      .then_inc(x_ms[s].sem, 16)

            def keep(u):
                U = u + layer * NP
                sp.wait_ge(x_lnB.sem, x_lnB.upto(U))
                sp.dma_start(O_all[:, bass.ds(2 * u, 2), :], xn[:, 1, :, :]).then_inc(x_xa.sem, 16)

            if layer == 0:
                sp.wait_ge(x_mk, 1)
            feed(0, 0)
            feed(1, 1)
            with sp.Fori(1, NP // 2) as i:
                for s in range(2):
                    feed(2 * i + s, s)
                    keep(2 * i + s - 2)
            keep(NP - 2)
            keep(NP - 1)
            sp.wait_ge(x_xa.sem, x_xa.upto(layer * NP + NP - 1))

        def steps(layer, body, eng, chain=None, links=0):
            body(-1, layer * NP - 1, 1, False, True, False)
            body(0, layer * NP, 0, True, True, False)
            loop = chain.fori(NP // 2 - 1, links) if chain else eng.Fori(0, NP // 2 - 1)
            with loop as i:
                for s in range(2):
                    u = 2 * i + 1 + s
                    body(u, u + layer * NP, 1 - s, True, True, True)
            body(NP - 1, layer * NP + NP - 1, 1, True, False, True)
            body(NP, layer * NP + NP, 0, False, False, True)

        def act_cross(act, c, layer):
            def turned(r, U, dst, free):
                act.wait_ge(x_t[r].sem, x_t[r].upto(U))
                act.wait_ge(free.sem, free.upto(U - 1))
                act.copy(dst[:], ps[:, 0, :].rearrange("p (k q) -> p k q", k=KC)).then_inc(x_te[r].sem, 1)

            def probs(U, j):
                act.wait_ge(x_sm.sem, x_sm.upto(U, j + 1))
                act.activation(pr[:, j, :, :], pr[:, j, :, :], ACT.Exp).then_inc(x_e.sem, 1)

            def probs_turned(U, j):
                act.wait_ge(x_pt.sem, x_pt.upto(U, j + 1))
                act.wait_ge(x_av.sem, x_av.upto(U, j))
                for q in range(2):
                    ins = act.copy(prT[:, 4 * q:4 * q + 4, :],
                                   ps[:, 5 + q, :].rearrange("p (g q) -> p g q", g=4))
                ins.then_inc(x_pe.sem, 1)

            def queries(U):
                act.wait_ge(x_q.sem, x_q.upto(U))
                for m in range(KC):
                    ins = act.activation(qT[:, m, :], ps[:, 2, m * 256:m * 256 + 256], ACT.Identity,
                                         bias=bq4[:, m:m + 1], scale=float(DH) ** -0.5)
                ins.then_inc(x_qe.sem, 1)

            act.wait_ge(x_cr.sem, x_cr.upto(layer))

            def body(u, U, s, mid, first, end):
                if first and layer == 0:
                    turned(0, U + 1, oT, x_oA)
                if mid:
                    probs(U, 0)
                    probs_turned(U, 0)
                if first:
                    turned(1, U + 1, xT_(0), x_q)
                if end:
                    turned(2, U - 1, oT2, x_oB)
                if first:
                    queries(U + 1)
                if mid:
                    probs(U, 1)
                if end:
                    turned(3, U - 1, xT_(1), x_r)
                if mid:
                    probs_turned(U, 1)

            steps(layer, body, act)

        def xT_(r):
            return xT[:, r, :, :]

        def dve_cross(v, c, layer):
            v.wait_ge(x_ld, X_LOADS[layer])
            c(v.tensor_scalar(bq4[:], bq[:], float(DH) ** -0.5, None, ALU.mult))
            if layer == 0:
                c(v.memset(fill0[:], -1000.0))
                v.tensor_scalar(mask_no[:], mask_u8[:], 0.0, None, ALU.is_equal).then_inc(x_mk, 1)
            else:
                v.wait_ge(x_m1, 16)
                c(v.tensor_scalar(mask1_f[:], mask1_u8[:], -1.0, 3e38, ALU.add, ALU.mult))
                c(v.tensor_scalar(mask1_f[:], mask1_f[:], 2.0, None, ALU.mult))
            v.wait_ge(x_ctx.sem, x_ctx.upto(layer, 1))
            for m in range(KC):
                c(v.tensor_scalar(kc[:, m, :], ps[:, 3, m * P:m * P + P], bk[:, m:m + 1], None, ALU.add))
            for b in range(B):
                for m in range(KC):
                    c(v.tensor_tensor(Kbd[:, b, m, :, :],
                                      kc[:, m, b * SC:b * SC + SC].unsqueeze(1).to_broadcast([P, HG, SC]),
                                      hmask[:].unsqueeze(2).to_broadcast([P, HG, SC]), ALU.mult))
            v.wait_ge(x_ctx.sem, x_ctx.upto(layer, 2))
            for b in range(B):
                c(v.tensor_tensor(vd[:, b, :], ps[:, 4, b * 256:b * 256 + 256], bv[:], ALU.add))
                for e in range(2):
                    c(v.tensor_scalar(Vbd[:, b, :, e, 0:DH],
                                      vd[:, b, :].rearrange("p (g e d) -> p g e d", g=HG, e=2)[:, :, e, :],
                                      halves[:, e:e + 1], None, ALU.mult))
                    c(v.tensor_copy(Vbd[:, b, :, e, DH:DH + 1],
                                    halves[:, e:e + 1].unsqueeze(1).to_broadcast([P, HG, 1])))
            v.memset(idle[:, 0:1], 0.0).then_inc(x_cr.sem, 1)
            v.wait_ge(x_cr.sem, x_cr.upto(layer))

            S2 = ps[:, 3:5, :].rearrange("p m (h k) -> p (m h) k", h=HG)

            def softmax(u, U, j, s):
                v.wait_ge(x_s.sem, x_s.upto(U, j + 1))
                if layer == 0:
                    v.wait_ge(x_ms[s].sem, x_ms[s].upto(half_of(u)))
                    v.memset(idle[:, 0:1], 0.0)
                    c(v.copy_predicated(out=S2, mask=mslot[:, s, j:j + 1, :].to_broadcast([P, H, SC]),
                                        data=fill0[:].unsqueeze(2).to_broadcast([P, H, SC])))
                else:
                    c(v.tensor_tensor(S2, S2, mask1_f[:, bass.ds(u // 4, 1), :].to_broadcast([P, H, SC]),
                                      ALU.add))
                c(v.tensor_reduce(mxx[:, j, :], S2, AX.X, ALU.max))
                v.wait_ge(x_pt.sem, x_pt.upto(U - 1, j + 1))
                v.tensor_tensor(pr[:, j, :, :], S2, mxx[:, j, :].unsqueeze(2).to_broadcast([P, H, SC]),
                                ALU.subtract).then_inc(x_sm.sem, 1)

            def outputs(U, j):
                v.wait_ge(x_av.sem, x_av.upto(U, j + 1))
                y = ps[:, 7, 0:H * (DH + 1)].rearrange("p (h d) -> p h d", h=H)
                c(v.reciprocal(recx[:].unsqueeze(2), y[:, :, DH:DH + 1]))
                v.wait_ge(x_t[2].sem, x_t[2].upto(U - 1))
                v.tensor_tensor(orow2[:, j, :].rearrange("p (h d) -> p h d", h=H), y[:, :, 0:DH],
                                recx[:].unsqueeze(2).to_broadcast([P, H, DH]), ALU.mult)\
                 .then_inc(x_no.sem, 1)

            def residual(u, U, out_sig, done):
                v.wait_ge(out_sig.sem, out_sig.upto(U))
                x2 = xr[:, bass.ds(2 * u, 2), :]
                v.tensor_tensor(x2, x2, ps[:, 1, :].rearrange("p (j d) -> p j d", j=2), ALU.add)\
                 .then_inc(done.sem, 1)
                v.wait_ge(done.sem, done.upto(U))

            def body(u, U, s, mid, first, end):
                if mid:
                    softmax(u, U, 0, s)
                if end:
                    outputs(U - 1, 1)
                if first:
                    if layer == 0:
                        residual(u + 1, U + 1, x_oA, x_res)
                    ln_fixed(v, c, u + 1, U + 1, 0, x_lnA, x_t[1])
                if mid:
                    softmax(u, U, 1, s)
                if end:
                    residual(u - 1, U - 1, x_oB, x_rb)
                    x2 = xr[:, bass.ds(2 * (u - 1), 2), :]
                    c(v.tensor_tensor(x2, x2, bo[:].unsqueeze(1).to_broadcast([P, 2, D]), ALU.add))
                    v.wait_ge(x_xa.sem, x_xa.upto(U - 2))
                    ln_fixed(v, c, u - 1, U - 1, 1, x_lnB, x_t[3])
                if mid:
                    outputs(U, 0)
                if end:
                    v.wait_ge(x_r.sem, x_r.upto(U - 1))
                    lo = lg[:, bass.ds(2 * (u - 1), 2), :]
                    y = ps[:, 2, 0:2 * E].rearrange("p (j e) -> p j e", j=2)
                    if layer == 0:
                        v.tensor_tensor(lo, y, zeros[:, 0:1].unsqueeze(2).to_broadcast([P, 2, E]), ALU.add).then_inc(x_lg.sem, 1)
                    else:
                        v.tensor_tensor(lo, y, rb[:].unsqueeze(1).to_broadcast([P, 2, E]),
                                        ALU.add).then_inc(x_lg.sem, 1)

            steps(layer, body, v, c, X_LINKS[layer])

        X_LINKS = [82, 82]

        def ln_fixed(v, c, u, U, r, xn_sig, tr_sig):
            v.memset(idle[:, 0:1], 0.0)
            for j in range(2):
                ins = v.bn_stats(st[:, j, :], xr[:, bass.ds(2 * u + j, 1), :].rearrange("p a d -> p (a d)"))
            c(ins)
            v.memset(idle[:, 0:1], 0.0)
            for j in range(2):
                ins = v.bn_aggr(mv[:, j, :], st[:, j, :])
            c(ins)
            rsqrt(v, c, nv, mv[:, :, 1], LN_EPS)
            v.wait_ge(tr_sig.sem, tr_sig.upto(U - 1))
            for j in range(2):
                ins = v.tensor_scalar(xn[:, r, j, :], xr[:, bass.ds(2 * u + j, 1), :].rearrange("p a d -> p (a d)"),
                                      mv[:, j, 0:1], nv[:, 0, j:j + 1], ALU.subtract, ALU.mult)
            ins.then_inc(xn_sig.sem, 1)

        def pe_cross(pe, layer):
            pe.wait_ge(x_ld, X_LOADS[layer])
            for m in range(KC):
                for k in range(KC):
                    ins = pe.matmul(ps[:, 3, m * P:m * P + P], xw["k"][:, k, m * P:m * P + P], ctxs[:, k, :],
                                    start=(k == 0), stop=(k == KC - 1))
            ins.then_inc(x_ctx.sem, 1)
            for b in range(B):
                for k in range(KC):
                    ins = pe.matmul(ps[:, 4, b * 256:b * 256 + 256],
                                    ctx2[:, b, k, :, :].rearrange("p e s -> p (e s)"), xw["v"][:, k, :],
                                    start=(k == 0), stop=(k == KC - 1))
            ins.then_inc(x_ctx.sem, 1)
            pe.wait_ge(x_cr.sem, x_cr.upto(layer))

            def turn(r, U, rows, wait, before):
                for s_, val in wait:
                    pe.wait_ge(s_.sem, val)
                for s_, val in before:
                    pe.wait_ge(s_.sem, val)
                for k in range(KC):
                    for j in range(2):
                        ins = pe.transpose(ps[:, 0, (2 * k + j) * P:(2 * k + j + 1) * P],
                                           rows[:, j, k * P:(k + 1) * P], ident[:])
                ins.then_inc(x_t[r].sem, 1)

            def out_rows(r, U, oT_, wo, used, done):
                pe.wait_ge(x_te[r].sem, x_te[r].upto(U))
                for s_, val in used:
                    pe.wait_ge(s_.sem, val)
                for j in range(2):
                    for k in range(KC):
                        ins = pe.matmul(ps[:, 1, j * 256:j * 256 + 256], oT_[:, k, j * P:j * P + P], wo[:, k, :],
                                        start=(k == 0), stop=(k == KC - 1))
                ins.then_inc(done.sem, 1)

            def queries(U):
                pe.wait_ge(x_te[1].sem, x_te[1].upto(U))
                pe.wait_ge(x_lg.sem, x_lg.upto(U - 3))
                for m in range(KC):
                    for k in range(KC):
                        ins = pe.matmul(ps[:, 2, m * 256:m * 256 + 256], xw["q"][:, k, m * P:m * P + P],
                                        xT[:, 0, k, :], start=(k == 0), stop=(k == KC - 1))
                ins.then_inc(x_q.sem, 1)

            def logits(U):
                pe.wait_ge(x_te[3].sem, x_te[3].upto(U))
                pe.wait_ge(x_qe.sem, x_qe.upto(U + 2))
                for j in range(2):
                    for k in range(KC):
                        ins = pe.matmul(ps[:, 2, j * E:j * E + E], xT[:, 1, k, j * P:j * P + P], rw[:, k, :],
                                        start=(k == 0), stop=(k == KC - 1))
                ins.then_inc(x_r.sem, 1)

            def scores(u, U, j):
                if j == 0:
                    pe.wait_ge(x_qe.sem, x_qe.upto(U))
                pe.wait_ge(x_sm.sem, x_sm.upto(U, j))
                for m in range(KC):
                    b = u // 4
                    ins = pe.matmul(ps[:, 3 + m, :], qT[:, m, j * P:j * P + P],
                                    Kbd[:, bass.ds(b, 1), m, :, :].rearrange("p b h k -> p (b h k)"),
                                    start=True, stop=True)
                ins.then_inc(x_s.sem, 1)

            def turn_probs(U, j):
                pe.wait_ge(x_e.sem, x_e.upto(U, j + 1))
                pe.wait_ge(x_pe.sem, x_pe.upto(U, j))
                for g in range(HG):
                    ins = pe.transpose(ps[:, 5 + g // 4, (g % 4) * P:(g % 4) * P + P],
                                       pr[:, j, 2 * g:2 * g + 2, :].rearrange("p e k -> p (e k)"), ident[:])
                ins.then_inc(x_pt.sem, 1)

            def weigh(u, U, j):
                pe.wait_ge(x_pe.sem, x_pe.upto(U, j + 1))
                pe.wait_ge(x_no.sem, x_no.upto(U, j))
                n = 2 * (DH + 1)
                for g in range(HG):
                    ins = pe.matmul(ps[:, 7, g * n:g * n + n], prT[:, g, :],
                                    Vbd[:, bass.ds(u // 4, 1), g, :, :].rearrange("p b e d -> p (b e d)"),
                                    start=True, stop=True)
                ins.then_inc(x_av.sem, 1)

            def body(u, U, s, mid, first, end):
                if mid:
                    scores(u, U, 0)
                if end:
                    weigh(u - 1, U - 1, 1)
                if first and layer == 0:
                    turn(0, U + 1, orow, [(x_or, x_or.upto(U + 1))], [(x_te[3], x_te[3].upto(U - 2))])
                    out_rows(0, U + 1, oT, woA, [(x_rb, x_rb.upto(U - 2))], x_oA)
                if mid:
                    turn_probs(U, 0)
                    scores(u, U, 1)
                if first:
                    turn(1, U + 1, xn[:, 0, :, :], [(x_lnA, x_lnA.upto(U + 1))],
                         [(x_te[0], x_te[0].upto(U + 1))] if layer == 0 else [(x_te[3], x_te[3].upto(U - 2))])
                if end:
                    turn(2, U - 1, orow2, [(x_no, x_no.upto(U - 1))],
                         [(x_te[1], x_te[1].upto(U + 1))] if first else [(x_te[3], x_te[3].upto(U - 2))])
                    out_rows(2, U - 1, oT2, xw["o"], [(x_res, x_res.upto(U + 1))] if first and layer == 0
                             else [(x_rb, x_rb.upto(U - 2))], x_oB)
                if mid:
                    weigh(u, U, 0)
                if first:
                    queries(U + 1)
                if end:
                    turn(3, U - 1, xn[:, 1, :, :], [(x_lnB, x_lnB.upto(U - 1))], [(x_te[2], x_te[2].upto(U - 1))])
                if mid:
                    turn_probs(U, 1)
                if end:
                    logits(U - 1) if first else logits_last(U)

            def logits_last(U):
                pe.wait_ge(x_te[3].sem, x_te[3].upto(U - 1))
                pe.wait_ge(x_qe.sem, x_qe.upto(layer * NP + NP - 1))
                pe.wait_ge(x_lg.sem, x_lg.upto(U - 2))
                for j in range(2):
                    for k in range(KC):
                        ins = pe.matmul(ps[:, 2, j * E:j * E + E], xT[:, 1, k, j * P:j * P + P], rw[:, k, :],
                                        start=(k == 0), stop=(k == KC - 1))
                ins.then_inc(x_r.sem, 1)

            steps(layer, body, pe)

        def half_of(u):
            return u // 2

        def dve_top2(v, c, layer):
            bc = lambda m: m.unsqueeze(2).to_broadcast([P, NT, E])
            t2 = lambda q: tk[:, q, :]
            c(v.tensor_reduce(t2(0), lg[:], AX.X, ALU.max))
            v.tensor_tensor(pe_[:], lg[:], bc(t2(0)), ALU.subtract).then_inc(r_sub, 1)
            v.wait_ge(r_exp, layer + 1)
            c(v.tensor_reduce(t2(0), pe_[:], AX.X, ALU.add))
            c(v.reciprocal(t2(1), t2(0)))
            c(v.tensor_tensor(pb[:], pe_[:], bc(t2(1)), ALU.mult))
            for k in range(2):
                c(v.tensor_reduce(top[k][:], pb[:], AX.X, ALU.max))
                c(v.tensor_tensor(tm[:], pb[:], bc(top[k][:]), ALU.is_equal))
                c(v.tensor_tensor(tm[:], tm[:], desc[:].unsqueeze(1).to_broadcast([P, NT, E]), ALU.mult))
                c(v.tensor_reduce(t2(2), tm[:], AX.X, ALU.max))
                c(v.tensor_tensor(oh[k][:], tm[:], bc(t2(2)), ALU.is_equal))
                if k == 0:
                    c(v.scalar_tensor_tensor(out=pb[:], in0=oh[0][:], scalar=-2.0, in1=pb[:],
                                             op0=ALU.mult, op1=ALU.add))
            c(v.tensor_tensor(t2(0), top[0][:], top[1][:], ALU.add))
            if layer == 0:
                c(v.tensor_scalar(t2(0), t2(0), EPS, None, ALU.max))
            c(v.reciprocal(t2(1), t2(0)))
            for k in range(2):
                c(v.tensor_tensor(gw[k][:], top[k][:], t2(1), ALU.mult))

        def over_experts(v, c, out_, a, b):
            c(v.tensor_tensor(tm[:], a, b, ALU.mult))
            c(v.tensor_reduce(out_, tm[:], AX.X, ALU.add))

        flat = lambda m: m[:].rearrange("p t e -> p (t e)")
        RS = [0]

        def dve_sum(v, ins):
            ins.then_inc(r_rhs, 1)
            RS[0] += 1
            v.wait_ge(r_sum, RS[0])

        def dve_route0(v, c):
            bc = lambda m: m.unsqueeze(2).to_broadcast([P, NT, E])
            be = lambda m: m.unsqueeze(1).to_broadcast([P, NT, E])
            dve_top2(v, c, 0)
            c(v.tensor_tensor(Wt[:], oh[0][:], bc(gw[0][:]), ALU.mult))
            c(v.tensor_tensor(tm[:], oh[1][:], bc(gw[1][:]), ALU.mult))
            c(v.tensor_tensor(Wt[:], Wt[:], tm[:], ALU.add))
            c(v.tensor_tensor(Kp[:], oh[0][:], oh[1][:], ALU.add))
            c(v.tensor_tensor(Ct[:], Wt[:], Kp[:], ALU.add))
            c(v.tensor_scalar(Ct[:], Ct[:], -1.0, None, ALU.add))
            c(v.memset(thr[:], 0))
            with c.fori(BITS, 4) as i:
                c(v.tensor_tensor(cand[:].unsqueeze(1), thr[:].unsqueeze(1), bits[:, bass.ds(i, 1), :],
                                  ALU.bitwise_or))
                c(v.tensor_tensor(tm[:], Ct[:], be(cand[:].bitcast(F32)), ALU.is_ge))
                with nc.allow_low_precision(reason="counts up to 16 are exact"):
                    ins = v.tensor_reduce(c8b[:], tm[:].rearrange("p t e -> p e t"), AX.X, ALU.add)
                ins.then_inc(r_rhs, 1)
                v.wait_ge(r_sum, i + 1)
                c(v.scalar_tensor_tensor(out=c8[:], in0=ps[:, 0, 0:E], scalar=CAP - 0.5,
                                         in1=cand[:].bitcast(F32), op0=ALU.is_ge, op1=ALU.mult))
                c(v.tensor_tensor(thr[:].bitcast(F32), thr[:].bitcast(F32), c8[:], ALU.max))
            RS[0] += BITS
            T8 = be(thr[:].bitcast(F32))
            c(v.tensor_tensor(Kp[:], Ct[:], T8, ALU.is_gt))
            with nc.allow_low_precision(reason="counts up to 16 are exact"):
                ins = v.tensor_reduce(c8b[:], Kp[:].rearrange("p t e -> p e t"), AX.X, ALU.add)
            dve_sum(v, ins)
            c(v.tensor_scalar(c8[:], ps[:, 0, 0:E], -1.0, float(CAP), ALU.mult, ALU.add))
            c(v.tensor_tensor(pb[:], Ct[:], T8, ALU.is_equal))
            dve_sum(v, v.tensor_copy(tb[:], pb[:]))
            y = ps[:, 0, 0:NT * E].rearrange("p (t e) -> p t e", t=NT)
            c(v.tensor_tensor(tm[:], y, be(c8[:]), ALU.is_lt))
            c(v.tensor_tensor(tm[:], tm[:], pb[:], ALU.mult))
            c(v.tensor_tensor(Kp[:], Kp[:], tm[:], ALU.add))
            dve_sum(v, v.tensor_copy(tb[:], Kp[:]))
            c(v.tensor_tensor(Ct[:], y, be(first[:]), ALU.add))
            c(v.tensor_tensor(Wt[:], Wt[:], Kp[:], ALU.mult))
            c(v.tensor_reduce(tk[:, 0, :], Wt[:], AX.X, ALU.add))
            c(v.tensor_scalar(tk[:, 0, :], tk[:, 0, :], EPS, None, ALU.max))
            c(v.reciprocal(tk[:, 1, :], tk[:, 0, :]))
            c(v.tensor_tensor(Wt[:], Wt[:], bc(tk[:, 1, :]), ALU.mult))
            for k in range(2):
                over_experts(v, c, gw[k][:], Wt[:], oh[k][:])
                over_experts(v, c, tk[:, 2, :], Kp[:], oh[k][:])
                over_experts(v, c, tk[:, 3, :], Ct[:], oh[k][:])
                c(v.tensor_scalar(tk[:, 4, :], tk[:, 2, :], -nochoice, nochoice, ALU.mult, ALU.add))
                c(v.tensor_tensor(tk[:, 5, :], tk[:, 3, :], tk[:, 4, :], ALU.add))
                c(v.tensor_copy(idxS[k][:], tk[:, 5, :]))
                c(v.tensor_tensor(tk[:, 6, :], tk[:, 3, :], tk[:, 2, :], ALU.mult))
                c(v.tensor_copy(idxG[k][:], tk[:, 6, :]))
            v.memset(idle[:], 0.0).then_inc(r_idx, 1)

        def pe_count(pe, n):
            pe.wait_ge(r_rhs, n)
            pe.matmul(ps[:, 0, 0:E], onesb[:], c8b[:], start=True, stop=True).then_inc(r_sum, 1)

        def pe_before(pe, n):
            pe.wait_ge(r_rhs, n)
            w_ = NT * E
            pe.matmul(ps[:, 0, 0:w_], lower[:], flat(tb), start=True, stop=False)
            for t in range(1, NT):
                ins = pe.matmul(ps[:, 0, t * E:w_], onesb[:], flat(tb)[:, 0:w_ - t * E], start=False,
                                stop=(t == NT - 1))
            ins.then_inc(r_sum, 1)

        def pe_route0(pe):
            with pe.Fori(1, BITS + 1) as i:
                pe_count(pe, i)
            pe_count(pe, BITS + 1)
            pe_before(pe, BITS + 2)
            pe_before(pe, BITS + 3)

        def pool_scatter(pool, c, layer, xs, rows):
            pool.wait_ge(r_idx, layer + 1)
            pool.wait_ge(g_z, 32)
            for t in range(NT):
                for k in range(2):
                    pool.indirect_dma_start(
                        out=xs, out_offset=bass.IndirectOffsetOnAxis(ap=idxS[k][:, t:t + 1], axis=0),
                        in_=O_all[:, t, :], in_offset=None, bounds_check=rows - 1, oob_is_err=False,
                    ).then_inc(g_sc[layer], 16)

        def pool_gather(pool, c, layer, ys, rows, ready):
            for s_, val in ready:
                pool.wait_ge(s_, val)
            for t in range(NT):
                if t >= 4:
                    pool.wait_ge(g_use, layer * NT + t - 3)
                for k in range(2):
                    pool.indirect_dma_start(
                        out=(yg, yg1)[layer][:, t % 4, k, :], out_offset=None, in_=ys,
                        in_offset=bass.IndirectOffsetOnAxis(ap=idxG[k][:, t:t + 1], axis=0),
                        bounds_check=rows - 1, oob_is_err=False,
                    ).then_inc(g_ld[t % 4], 16)

        def dve_combine(v, c, layer):
            for t in range(NT):
                v.wait_ge(g_ld[t % 4], (layer * 4 + t // 4 + 1) * 32)
                c(v.scalar_tensor_tensor(out=xr[:, t, :], in0=(yg, yg1)[layer][:, t % 4, 0, :], scalar=gw[0][:, t:t + 1],
                                         in1=xr[:, t, :], op0=ALU.mult, op1=ALU.add))
                v.scalar_tensor_tensor(out=xr[:, t, :], in0=(yg, yg1)[layer][:, t % 4, 1, :], scalar=gw[1][:, t:t + 1],
                                       in1=xr[:, t, :], op0=ALU.mult, op1=ALU.add).then_inc(g_use, 1)

        WE = 3 * KC * F
        gate_w = lambda s: wide[:, s * WE:s * WE + KC * F].rearrange("p (k f) -> p k f", k=KC)
        pre_w = lambda s: wide[:, s * WE + KC * F:s * WE + 2 * KC * F].rearrange("p (k f) -> p k f", k=KC)
        post_w = lambda s: wide[:, s * WE + 2 * KC * F:(s + 1) * WE].rearrange("p (g d) -> p g d", d=D)
        HC = CAP // 2

        def sp_weights0(sp, e, s):
            sp.wait_ge(f_y.sem, f_y.upto(e - 2))
            for dst, src in ((gate_w(s), w["L0_ffn_gate_weight"]), (pre_w(s), w["L0_ffn_ff_pre_act_weight"]),
                             (post_w(s), w["L0_ffn_ff_post_act_weight"])):
                sp.dma_start(dst, src[bass.ds(e, 1), :, :].rearrange("e (k p) n -> p (e k) n", p=P))\
                  .then_inc(f_w[s].sem, 16)

        def sp_experts0(sp):
            sp.wait_ge(g_sc[0], 2 * NT * 16)

            def rows_in(e, s):
                sp.wait_ge(f_t.sem, f_t.upto(e - 2))
                sp.dma_start(xe[:, s, :, :], xs0[bass.ds(e * CAP, CAP), :].rearrange("(r p) d -> p r d", p=P))\
                  .then_inc(f_x[s].sem, 16)

            def rows_out(e):
                sp.wait_ge(f_ye.sem, f_ye.upto(e))
                sp.dma_start(ys0[bass.ds(e * CAP, CAP), :].rearrange("(r p) d -> p r d", p=P), yrow)\
                  .then_inc(f_ys.sem, 16)

            rows_in(0, 0)
            rows_in(1, 1)
            with sp.Fori(1, E // 2) as i:
                for s in range(2):
                    rows_out(2 * i + s - 2)
                    sp_weights0(sp, 2 * i + s, s)
                    rows_in(2 * i + s, s)
            rows_out(E - 2)
            rows_out(E - 1)

        def pe_experts0(pe):
            def turn(e, s):
                pe.wait_ge(f_x[s].sem, f_x[s].upto(e // 2))
                pe.wait_ge(f_te.sem, f_te.upto(e - 1))
                for k in range(KC):
                    for r in range(5):
                        o = ps[:, k, r * P:r * P + P] if r < 4 else ps[:, 2, k * P:k * P + P]
                        ins = pe.transpose(o, xe[:, s, r, k * P:k * P + P], ident[:])
                ins.then_inc(f_t.sem, 1)

            def hidden(e, s):
                pe.wait_ge(f_w[s].sem, f_w[s].upto(e // 2))
                pe.wait_ge(f_te.sem, f_te.upto(e))
                for q in range(16):
                    hf, f = q // 8, q % 8
                    pe.wait_ge(f_m.sem, f_m.upto(e, q - 1))
                    if q == 1:
                        pe.wait_ge(f_ye.sem, f_ye.upto(e - 1))
                    for n, wt in enumerate((gate_w(s), pre_w(s))):
                        for k in range(KC):
                            ins = pe.matmul(ps[:, 3 + 2 * (q % 2) + n, 0:HC], wt[:, k, f * P:f * P + P],
                                            xTe[:, k, hf * HC:hf * HC + HC], start=(k == 0), stop=(k == KC - 1))
                    ins.then_inc(f_h.sem, 1)

            def output(e, s, r):
                pe.wait_ge(f_m.sem, f_m.upto(e))
                pe.wait_ge(f_ye.sem, f_ye.upto(e, r - 1))
                for g in range(F // P):
                    ins = pe.matmul(ps[:, 7 - r % 2, 0:D], hTe[:, g, r * P:r * P + P], post_w(s)[:, g, :],
                                    start=(g == 0), stop=(g == F // P - 1))
                ins.then_inc(f_y.sem, 1)

            def expert(e, s, last=False):
                hidden(e, s)
                for r in range(5):
                    output(e, s, r)
                    if r == 2 and not last:
                        turn(e + 1, 1 - s)

            turn(0, 0)
            with pe.Fori(0, E // 2 - 1) as i:
                for s in range(2):
                    expert(2 * i + s, s)
            expert(E - 2, 0)
            expert(E - 1, 1, True)

        def act_experts0(act):
            with act.Fori(0, E // 2) as i:
                for s in range(2):
                    e = 2 * i + s
                    act.wait_ge(f_t.sem, f_t.upto(e))
                    for k in range(KC):
                        act.copy(xTe[:, k, 0:512], ps[:, k, :]).then_inc(f_te.sem, 1)
                    act.copy(xTe[:, :, 512:CAP], ps[:, 2, 0:256].rearrange("p (k q) -> p k q", k=KC))\
                       .then_inc(f_te.sem, 1)
                    for q in range(16):
                        act.wait_ge(f_h.sem, f_h.upto(e, q + 1))
                        act.wait_ge(f_m.sem, f_m.upto(e, q - 1))
                        act.activation(sgt[:, q % 2, :], ps[:, 3 + 2 * (q % 2), 0:HC], ACT.Silu)\
                           .then_inc(f_a.sem, 1)

        def dve_experts0(v, c):
            with c.fori(E // 2, 0) as i:
                for s in range(2):
                    e = 2 * i + s
                    for q in range(16):
                        hf, f = q // 8, q % 8
                        v.wait_ge(f_a.sem, f_a.upto(e, q + 1))
                        v.tensor_tensor(hTe[:, f, hf * HC:hf * HC + HC], sgt[:, q % 2, :],
                                        ps[:, 4 + 2 * (q % 2), 0:HC], ALU.mult).then_inc(f_m.sem, 1)
                    for r in range(5):
                        v.wait_ge(f_y.sem, f_y.upto(e, r + 1))
                        if r == 0:
                            v.wait_ge(f_ys.sem, f_ys.upto(e - 1))
                        v.tensor_copy(yrow[:, r, :], ps[:, 7 - r % 2, 0:D]).then_inc(f_ye.sem, 1)

        def dve_route1(v, c):
            be = lambda m: m.unsqueeze(1).to_broadcast([P, NT, E])
            dve_top2(v, c, 1)
            c(v.tensor_tensor(Kp[:], oh[0][:], oh[1][:], ALU.add))
            with nc.allow_low_precision(reason="counts up to 16 are exact"):
                ins = v.tensor_reduce(c8b[:], Kp[:].rearrange("p t e -> p e t"), AX.X, ALU.add)
            dve_sum(v, ins)
            c(v.tensor_scalar(n8[:], ps[:, 0, 0:E], float(P - 1), None, ALU.add))
            c(v.tensor_copy(n8i[:], n8[:]))
            c(v.tensor_scalar(n8i[:], n8i[:], 7, None, ALU.logical_shift_right))
            c(v.tensor_copy(n8[:], n8i[:]))
            c(v.tensor_tensor(m3[:], before_e[:], n8[:].unsqueeze(1).to_broadcast([P, E, E]), ALU.mult))
            c(v.tensor_reduce(base8[:], m3[:], AX.X, ALU.add))
            c(v.tensor_tensor(n8[:], base8[:], n8[:], ALU.add))
            c(v.tensor_scalar(base8[:], base8[:], float(P), None, ALU.mult))
            dve_sum(v, v.tensor_copy(tb[:], Kp[:]))
            y = ps[:, 0, 0:NT * E].rearrange("p (t e) -> p t e", t=NT)
            c(v.tensor_tensor(Ct[:], y, be(base8[:]), ALU.add))
            for k in range(2):
                over_experts(v, c, tk[:, 3, :], Ct[:], oh[k][:])
                c(v.tensor_copy(idxS[k][:], tk[:, 3, :]))
                c(v.tensor_copy(idxG[k][:], tk[:, 3, :]))
            c(v.tensor_tensor(ex[:], n8[:].unsqueeze(1).to_broadcast([P, NX, E]),
                              tile_no[:].unsqueeze(2).to_broadcast([P, NX, E]), ALU.is_le))
            c(v.tensor_reduce(exf[:], ex[:], AX.X, ALU.add))
            c(v.tensor_scalar(exf[:], exf[:], float(E - 1), None, ALU.min))
            c(v.tensor_copy(exi[:], exf[:]))
            v.memset(idle[:], 0.0).then_inc(r_idx, 1)

        w1s = wide[:].rearrange("p (e k f) -> p e k f", e=E, k=KC)

        def sp_experts1(sp):
            sp.dma_start(w2s[:].rearrange("p e g d -> p (e g) d"),
                         w["L1_ffn_w2"].rearrange("e (g p) d -> p (e g) d", p=P)).then_inc(m_w2, 16)
            sp.dma_start(b1s[:], w["L1_ffn_b1"]).then_inc(m_w2, 16)
            sp.dma_start(b2s[:], w["L1_ffn_b2"].partition_broadcast(P)).then_inc(m_w2, 16)
            sp.wait_ge(g_sc[1], 2 * NT * 16)

            def rows_in(j, s):
                sp.wait_ge(m_t.sem, m_t.upto(j - 2))
                sp.dma_start(rows1[:, s, :], xs1[bass.ds(j * P, P), :]).then_inc(m_x[s].sem, 16)

            def rows_out(j, s):
                sp.wait_ge(m_yc.sem, m_yc.upto(j))
                sp.dma_start(ys1[bass.ds(j * P, P), :], yrow1[:, s, :]).then_inc(m_st[s].sem, 16)

            rows_in(0, 0)
            rows_in(1, 1)
            with sp.Fori(1, NX // 2) as i:
                for s in range(2):
                    rows_in(2 * i + s, s)
                    rows_out(2 * i + s - 2, s)
            for s in range(2):
                rows_out(NX - 2 + s, s)

        def steps1(body, eng):
            body(-2, 0, False, False, True)
            body(-1, 1, False, True, True)
            with eng.Fori(0, NX // 2 - 1) as i:
                for s in range(2):
                    body(2 * i + s, s, True, True, True)
            body(NX - 2, 0, True, True, False)
            body(NX - 1, 1, True, False, False)

        def expert_of(eng, j):
            return eng.value_load(exi[0:1, bass.ds(j, 1)], min_val=0, max_val=E - 1)

        def pe_experts1(pe):
            def body(j, s, out_, hid, turn):
                if out_:
                    for q in range(2):
                        pe.wait_ge(m_hc.sem, m_hc.upto(j, q + 1))
                        pe.wait_ge(m_a.sem, m_a.upto(j - 1, q + 1))
                        for g in range(4):
                            ins = pe.transpose(ps[:, 3 + q, g * P:g * P + P], hrow[:, q, g * P:g * P + P], ident[:])
                        ins.then_inc(m_ht.sem, 1)
                if hid:
                    pe.wait_ge(m_tc.sem, m_tc.upto(j + 1))
                    e = expert_of(pe, j + 1)
                    for q in range(2):
                        pe.wait_ge(m_hc.sem, m_hc.upto(j, q + 1))
                        for k in range(KC):
                            ins = pe.matmul(ps[:, 1 + q, :], xTm[:, 1 - s, k, :],
                                            w1s[:, bass.ds(e, 1), k, q * 512:q * 512 + 512]
                                            .rearrange("p e f -> p (e f)"),
                                            start=(k == 0), stop=(k == KC - 1))
                        ins.then_inc(m_h.sem, 1)
                if turn:
                    pe.wait_ge(m_x[s].sem, m_x[s].upto(half_of(j + 2)))
                    pe.wait_ge(m_tc.sem, m_tc.upto(j + 1))
                    for k in range(KC):
                        ins = pe.transpose(ps[:, 0, k * P:k * P + P], rows1[:, s, k * P:k * P + P], ident[:])
                    ins.then_inc(m_t.sem, 1)
                if out_:
                    e = expert_of(pe, j)
                    pe.wait_ge(m_yc.sem, m_yc.upto(j - 2))
                    for g in range(F // P):
                        if g % 4 == 0:
                            pe.wait_ge(m_a.sem, m_a.upto(j, g // 4 + 1))
                        ins = pe.matmul(ps[:, 5 + s, 0:D], hTm[:, g, :],
                                        w2s[:, bass.ds(e, 1), g, :].rearrange("p e d -> p (e d)"),
                                        start=(g == 0), stop=(g == F // P - 1))
                    ins.then_inc(m_y.sem, 1)

            pe.wait_ge(r_idx, 2)
            pe.wait_ge(m_w, 16)
            pe.wait_ge(m_w2, 48)
            steps1(body, pe)

        def act_experts1(act):
            def body(j, s, out_, hid, turn):
                if hid:
                    for q in range(2):
                        act.wait_ge(m_h.sem, m_h.upto(j + 1, q + 1))
                        act.wait_ge(m_ht.sem, m_ht.upto(j, q + 1))
                        act.copy(hrow[:, q, :], ps[:, 1 + q, :]).then_inc(m_hc.sem, 1)
                if turn:
                    act.wait_ge(m_t.sem, m_t.upto(j + 2))
                    act.wait_ge(m_h.sem, m_h.upto(j))
                    act.copy(xTm[:, s, :, :], ps[:, 0, 0:2 * P].rearrange("p (k q) -> p k q", k=KC))\
                       .then_inc(m_tc.sem, 1)

            steps1(body, act)

        def dve_experts1(v, c):
            def body(j, s):
                e = expert_of(v, j)
                for q in range(2):
                    v.wait_ge(m_ht.sem, m_ht.upto(j, q + 1))
                    v.wait_ge(m_y.sem, m_y.upto(j - 1))
                    h3 = hTm[:, 4 * q:4 * q + 4, :]
                    b = b1s[:, bass.ds(e, 1), 4 * q:4 * q + 4].rearrange("p e g -> p (e g)")
                    c(v.tensor_tensor(h3, ps[:, 3 + q, :].rearrange("p (g t) -> p g t", g=4),
                                      b.unsqueeze(2).to_broadcast([P, 4, P]), ALU.add))
                    v.tensor_scalar(h3, h3, 0.0, None, ALU.max).then_inc(m_a.sem, 1)
                v.wait_ge(m_y.sem, m_y.upto(j))
                v.wait_ge(m_st[s].sem, m_st[s].upto(half_of(j) - 1))
                v.tensor_tensor(yrow1[:, s, :], ps[:, 5 + s, 0:D],
                                b2s[:, bass.ds(e, 1), :].rearrange("p e d -> p (e d)"), ALU.add)\
                 .then_inc(m_yc.sem, 1)

            v.wait_ge(m_w2, 48)
            with c.fori(NX // 2, 4) as i:
                for s in range(2):
                    body(2 * i + s, s)

        def sp_retention(sp):
            for dst, src in ((wqk[:, :, 0:D], chunked(w["L1_attn_WQ"])), (wqk[:, :, D:2 * D], chunked(w["L1_attn_WK"])),
                             (wvR[:], chunked(w["L1_attn_WV"])), (woR[:], chunked(w["L1_attn_WO"])),
                             (turns[:], w["c_turns"]), (decay[:], w["c_decay"]), (causal[:], w["c_causal"]),
                             (bdg[:], w["c_bdg"]), (gP[:], w["c_gP"]), (keepS[:], w["c_keep"]),
                             (gamma[:], w["L1_attn_gamma"]), (beta[:], w["L1_attn_beta"])):
                sp.dma_start(dst, src).then_inc(e_ld, 16)

        def steps_r(body, eng, chain=None, links=0):
            body(-1, 1, False, True, False, False)
            body(0, 0, True, True, False, False)
            body(1, 1, True, True, True, False)
            loop = chain.fori(NT // 2 - 2, links) if chain else eng.Fori(0, NT // 2 - 2)
            with loop as i:
                for s in range(2):
                    body(2 * i + 2 + s, s, True, True, True, True)
            body(NT - 2, 0, True, True, True, True)
            body(NT - 1, 1, True, False, True, True)
            body(NT, 0, False, False, True, True)
            body(NT + 1, 1, False, False, False, True)

        E_LOADS = 12 * 16
        E_LINKS = 82

        def pe_retention(pe):
            def body(t, s, mid, first, end, res):
                def scores(g):
                    m = g // 2
                    pe.wait_ge(e_ex.sem, e_ex.upto(t, m + 2))
                    pe.wait_ge(e_m.sem, e_m.upto(t, g - 1))
                    pe.matmul(ps[:, 3 + g % 2, :], qkT[:, KC + m, :],
                              qbd[:, m, 4 * (g % 2):4 * (g % 2) + 4, :].rearrange("p h q -> p (h q)"),
                              start=True, stop=True).then_inc(e_s.sem, 1)

                def weigh(g):
                    pe.wait_ge(e_m.sem, e_m.upto(t, g + 1))
                    for h in range(4):
                        d = (4 * g + h) * DH
                        ins = pe.matmul(ps[:, 5, d:d + DH], wS[:, g % 2, h, :], vR[:, s, d:d + DH],
                                        start=False, stop=(g == 3 and h == 3))
                    ins.then_inc(e_av.sem, 1)

                if mid:
                    scores(0)
                    scores(1)
                    pe.wait_ge(e_st.sem, e_st.upto(t - 1))
                    pe.wait_ge(e_rv.sem, e_rv.upto(t - 1))
                    for m in range(KC):
                        pe.matmul(ps[:, 5, m * P:m * P + P], qkT[:, m, :], State[:, m, :], start=(m == 0), stop=False)
                    weigh(0)
                    scores(2)
                    weigh(1)
                    scores(3)
                if first:
                    pe.wait_ge(e_ln.sem, e_ln.upto(t + 1))
                    pe.wait_ge(e_ex.sem, e_ex.upto(t, 1))
                    for k in range(KC):
                        ins = pe.transpose(ps[:, 0, k * P:k * P + P], xn[:, 0, 0, k * P:k * P + P], ident[:])
                    ins.then_inc(e_tx.sem, 1)
                if mid:
                    weigh(2)
                if first:
                    pe.wait_ge(e_xt.sem, e_xt.upto(t + 1))
                    pe.wait_ge(e_rot.sem, e_rot.upto(t))
                    for wt, bank, n in ((wqk, 1, 2 * D), (wvR, 2, D)):
                        for k in range(KC):
                            ins = pe.matmul(ps[:, bank, 0:n], xT[:, 0, k, 0:P], wt[:, k, :],
                                            start=(k == 0), stop=(k == KC - 1))
                    ins.then_inc(e_qk.sem, 1)
                if mid:
                    weigh(3)
                    pe.wait_ge(e_st.sem, e_st.upto(t - 1))
                    for m in range(KC):
                        ins = pe.matmul(ps[:, 6, m * P:m * P + P], qkr[:, s, D + m * P:D + m * P + P],
                                        vR[:, s, m * P:m * P + P], start=True, stop=True)
                    ins.then_inc(e_su.sem, 1)
                if end:
                    pe.wait_ge(e_gn.sem, e_gn.upto(t - 1))
                    pe.wait_ge(e_rs.sem, e_rs.upto(t - 2))
                    for k in range(KC):
                        ins = pe.transpose(ps[:, 7, k * P:k * P + P], Rq[:, k * P:k * P + P], ident[:])
                    ins.then_inc(e_ot.sem, 1)
                if first:
                    pe.wait_ge(e_rot.sem, e_rot.upto(t + 1))
                    for k in range(2 * KC):
                        ins = pe.transpose(ps[:, 0, k * P:k * P + P], qkr[:, 1 - s, k * P:k * P + P], ident[:])
                    ins.then_inc(e_tq.sem, 1)
                if end:
                    pe.wait_ge(e_oc.sem, e_oc.upto(t - 1))
                    for k in range(KC):
                        ins = pe.matmul(ps[:, 7, 0:D], oTR[:, k, :], woR[:, k, :], start=(k == 0), stop=(k == KC - 1))
                    ins.then_inc(e_y.sem, 1)

            pe.wait_ge(e_ld, E_LOADS)
            pe.wait_ge(e_z, 1)
            steps_r(body, pe)

        def act_retention(act):
            def body(t, s, mid, first, end, res):
                if first:
                    act.wait_ge(e_tx.sem, e_tx.upto(t + 1))
                    act.copy(xT[:, 0, :, 0:P], ps[:, 0, 0:2 * P].rearrange("p (k q) -> p k q", k=KC))\
                       .then_inc(e_xt.sem, 1)
                if end:
                    act.wait_ge(e_ot.sem, e_ot.upto(t - 1))
                    for k in range(KC):
                        ins = act.activation(oTR[:, k, :], ps[:, 7, k * P:k * P + P], ACT.Identity,
                                             bias=beta[:, k:k + 1], scale=gamma[:, k:k + 1])
                    ins.then_inc(e_oc.sem, 1)
                if first:
                    act.wait_ge(e_tq.sem, e_tq.upto(t + 1))
                    act.copy(qkT[:], ps[:, 0, :].rearrange("p (k q) -> p k q", k=2 * KC)).then_inc(e_ex.sem, 1)
                    act.wait_ge(e_ex.sem, e_ex.upto(t + 1, 1))
                    for m in range(KC):
                        for g in range(HG):
                            ins = act.activation(qbd[:, m, g, :], qkT[:, m, :], ACT.Copy, scale=hmask[:, g:g + 1])
                        ins.then_inc(e_ex.sem, 1)

            act.wait_ge(e_ld, E_LOADS)
            steps_r(body, act)

        def dve_retention(v, c):
            def body(t, s, mid, first, end, res):
                def causal_scores(g):
                    v.wait_ge(e_s.sem, e_s.upto(t, g + 1))
                    v.wait_ge(e_av.sem, e_av.upto(t, g - 1))
                    v.tensor_tensor(wS[:, g % 2, :, :], ps[:, 3 + g % 2, :].rearrange("p (h q) -> p h q", h=4),
                                    causal[:].unsqueeze(1).to_broadcast([P, 4, P]), ALU.mult).then_inc(e_m.sem, 1)

                if mid:
                    causal_scores(0)
                    causal_scores(1)
                if first:
                    x1 = xr[:, bass.ds(t + 1, 1), :].rearrange("p a d -> p (a d)")
                    v.memset(idle[:, 0:1], 0.0)
                    c(v.bn_stats(st[:, 0, :], x1))
                    v.memset(idle[:, 0:1], 0.0)
                    c(v.bn_aggr(mv[:, 0, :], st[:, 0, :]))
                    rsqrt(v, c, nv[:, :, 0:1], mv[:, 0, 1:2], LN_EPS)
                    v.wait_ge(e_tx.sem, e_tx.upto(t))
                    v.tensor_scalar(xn[:, 0, 0, :], x1, mv[:, 0, 0:1], nv[:, 0, 0:1], ALU.subtract,
                                    ALU.mult).then_inc(e_ln.sem, 1)
                if mid:
                    causal_scores(2)
                if res:
                    v.wait_ge(e_y.sem, e_y.upto(t - 2))
                    x2 = xr[:, bass.ds(t - 2, 1), :].rearrange("p a d -> p (a d)")
                    v.tensor_tensor(x2, x2, ps[:, 7, 0:D], ALU.add).then_inc(e_rs.sem, 1)
                if mid:
                    causal_scores(3)
                if end:
                    R3 = Rr[:, 1 - s, :].rearrange("p (h d) -> p h d", h=H)
                    Q3 = Rq[:].rearrange("p (h d) -> p h d", h=H)
                    gb = lambda a: a.unsqueeze(2).to_broadcast([P, H, DH])
                    v.wait_ge(e_rv.sem, e_rv.upto(t - 1))
                    c(v.tensor_reduce(gmean[:], R3, AX.X, ALU.add))
                    c(v.tensor_scalar(gmean[:], gmean[:], 1.0 / DH, None, ALU.mult))
                    c(v.tensor_tensor(R3, R3, gb(gmean[:]), ALU.subtract))
                    v.wait_ge(e_ot.sem, e_ot.upto(t - 2))
                    c(v.tensor_tensor(Q3, R3, R3, ALU.mult))
                    c(v.tensor_reduce(gvar[:], Q3, AX.X, ALU.add))
                    c(v.tensor_scalar(gvar[:], gvar[:], 1.0 / DH, None, ALU.mult))
                    rsqrt(v, c, gnv, gvar[:], LN_EPS)
                    v.tensor_tensor(Q3, R3, gb(gnv[:, 0, :]), ALU.mult).then_inc(e_gn.sem, 1)
                if first:
                    v.wait_ge(e_qk.sem, e_qk.upto(t + 1))
                    v.tensor_tensor(vR[:, 1 - s, :].rearrange("p (h d) -> p h d", h=H),
                                    ps[:, 2, 0:D].rearrange("p (h d) -> p h d", h=H),
                                    decay[:, 1, :].unsqueeze(2).to_broadcast([P, H, DH]), ALU.mult)
                    b4 = lambda a: a.rearrange("p (g r e) -> p g r e", r=DH // 2, e=2)
                    tb_ = (t + 1) % TB
                    cs = [turns[:, q, bass.ds(tb_, 1), :] for q in range(2)]
                    raw, rot, hf = b4(ps[:, 1, :]), b4(qkr[:, 1 - s, :]), b4(half_turn[:])
                    v.tensor_tensor(rot, raw, cs[0].unsqueeze(3).to_broadcast([P, 2 * H, DH // 2, 2]), ALU.mult)
                    sn = cs[1].to_broadcast([P, 2 * H, DH // 2])
                    for e in range(2):
                        ins = v.tensor_tensor(hf[:, :, :, e], raw[:, :, :, 1 - e], sn, ALU.mult)
                    c(ins)
                    v.tensor_tensor(rot[:, :, :, 0], rot[:, :, :, 0], hf[:, :, :, 0], ALU.subtract)
                    v.tensor_tensor(rot[:, :, :, 1], rot[:, :, :, 1], hf[:, :, :, 1], ALU.add)\
                     .then_inc(e_rot.sem, 1)
                if mid:
                    v.wait_ge(e_av.sem, e_av.upto(t))
                    v.tensor_tensor(Rr[:, s, :].rearrange("p (h d) -> p h d", h=H),
                                    ps[:, 5, 0:D].rearrange("p (h d) -> p h d", h=H),
                                    decay[:, 0, :].unsqueeze(2).to_broadcast([P, H, DH]), ALU.mult)\
                     .then_inc(e_rv.sem, 1)
                    v.wait_ge(e_su.sem, e_su.upto(t))
                    c(v.tensor_tensor(newS[:], ps[:, 6, 0:2 * P].rearrange("p (m q) -> p m q", m=KC), bdg[:],
                                      ALU.mult))
                    for m in range(KC):
                        ins = v.scalar_tensor_tensor(out=newS[:, m, :], in0=State[:, m, :], scalar=gP[:, m:m + 1],
                                                     in1=newS[:, m, :], op0=ALU.mult, op1=ALU.add)
                    c(ins)
                    v.tensor_scalar(State[:], newS[:], keepS[:, bass.ds(t, 1)], None, ALU.mult)\
                     .then_inc(e_st.sem, 1)
                    v.wait_ge(e_st.sem, e_st.upto(t))

            v.wait_ge(e_ld, E_LOADS)
            v.memset(State[:], 0.0).then_inc(e_z, 1)
            v.wait_ge(e_z, 1)
            steps_r(body, v, c, E_LINKS)

        @block.sync
        def _(sp):
            xv = x_in.rearrange("b (t p) d -> p (b t) d", p=P)
            for q in range(4):
                load(sp, xr[:, 4 * q:4 * q + 4, :], xv[:, 4 * q:4 * q + 4, :])
            load(sp, ident[:], w["c_ident"])
            load(sp, sel[:], w["c_sel"])
            load(sp, wqA[:], chunked(w["L0_attn_Wq"]))
            load(sp, wkA[:], chunked(w["L0_attn_Wk"]))
            load(sp, wvA[:], chunked(w["L0_attn_Wv"]))
            load(sp, qwB[:], w["L0_attn_quadrant_weights"].partition_broadcast(P))
            load(sp, desc[:], w["c_desc"])
            load(sp, first[:], w["c_first"])
            load(sp, bits[:], w["c_bits"])
            load(sp, lowf[:], w["c_lower"])
            load(sp, before_e[:], w["c_before"])
            load(sp, tile_no[:], w["c_tiles"])
            sp.wait_ge(z_set, 1)
            for xs in (xs0, xs1):
                sp.dma_start(xs.rearrange("(r p) d -> p r d", p=P),
                             zrow[:].unsqueeze(1).to_broadcast([P, NX, D])).then_inc(g_z, 16)
            for e in range(2):
                sp_weights0(sp, e, e)

            with sp.Fori(0, NP // 2) as i:
                for s in range(2):
                    u = 2 * i + s
                    b, t0 = u // 4, (u % 4) * 2
                    sp.wait_ge(a_p1.sem, a_p1.upto(u))
                    sp.wait_ge(a_p2.sem, a_p2.upto(u))
                    sp.wait_ge(a_p3.sem, a_p3.upto(u))
                    for a in range(3):
                        dst = qk_parts[a, bass.ds(b, 1), :, bass.ds(t0 * P, 2 * P)]
                        sp.dma_start(dst.rearrange("b (m p) s -> p (b m) s", p=P),
                                     parts[:, s, a, :, :]).then_inc(a_st[s].sem, 16)
                    sp.wait_ge(a_vs.sem, a_vs.upto(u))
                    dst = v_heads[bass.ds(b, 1), :, :, bass.ds(t0, 2), :]
                    for j in range(2):
                        sp.dma_start(dst[:, :, :, j, :].rearrange("b h p c -> p (b h) c"),
                                     vslot[:, s, j, :, :]).then_inc(a_st[s].sem, 16)
            for s in range(2):
                sp.wait_ge(a_st[s].sem, a_st[s].upto(NP // 2 - 1))

            def fetch(n, sl):
                b, r = n // H, (n % H) * DH
                for part, count, row in ((0, 3, 0), (1, 2, 48), (2, 1, 80)):
                    src = qk_parts[part, bass.ds(b, 1), bass.ds(r, DH), :].rearrange("b r s -> (b r) s")
                    sp.dma_start(QS[row:row + count * DH, sl, :], src.partition_broadcast(count))\
                      .then_inc(h_ld[sl].sem, 16)
                    src = qk_parts[0:count, bass.ds(b, 1), bass.ds(r + D, DH), :]
                    sp.dma_start(KS[row:row + count * DH, sl, :], src.rearrange("a b r s -> (a b) r s"))\
                      .then_inc(h_ld[sl].sem, 16)
                src = v_heads[bass.ds(b, 1), bass.ds(n % H, 1), :, :, :]
                sp.dma_start(VS[:, sl, :, :], src.rearrange("b h p t c -> p (b h t) c")).then_inc(h_ld[sl].sem, 16)

            def rows(n, sl):
                sp.wait_ge(h_mc.sem, h_mc.upto(n))
                sp.dma_start(QS[96:99, sl, :], mrow[:, sl % 2, :]).then_inc(h_mr[sl].sem, 16)

            for n in range(3):
                fetch(n, n)
            rows(0, 0)

            def head(n, hh, last=False):
                if not last or hh < 1:
                    sp.wait_ge(h_pv.sem, h_pv.upto(n - 1))
                    fetch(n + 3, (hh + 3) % 4)
                if not last or hh < 3:
                    rows(n + 1, (hh + 1) % 4)

            with sp.Fori(0, B * H // 4 - 1) as i:
                for hh in range(4):
                    head(4 * i + hh, hh)
            for hh in range(4):
                head(B * H - 4 + hh, hh, True)
            meet(sp, 1)
            sp_cross_weights(sp, 0)
            sp_cross(sp, 0)
            meet(sp, 2)
            sp_experts0(sp)
            meet(sp, 3)
            sp_retention(sp)
            sp_cross_weights(sp, 1)
            sp.dma_start(wide[:].rearrange("p (g f) -> p g f", f=F),
                         w["L1_ffn_w1"].rearrange("e (k p) f -> p (e k) f", p=P)).then_inc(m_w, 16)
            meet(sp, 4)
            sp_cross(sp, 1)
            meet(sp, 5)
            sp_experts1(sp)
            meet(sp, 6)
            finish(sp)

        @block.gpsimd
        def _(pool):
            for s in sigs:
                pool.sem_inc(s.sem, LAG * s.per)
            c = Chain(pool, chain_pool)
            c(pool.memset(zeros[:], 0.0))
            c(pool.memset(onesb[:], 1.0))
            pool.memset(zrow[:], 0.0).then_inc(z_set, 1)
            pool.wait_ge(z_set, 1)
            c(pool.memset(vslot[:], 0.0))
            pool.memset(KS[96:99, :, :], 1.0).then_inc(ones_set, 1)
            pool.wait_ge(ones_set, 1)
            pool.memset(vslot[:, :, :, :, DH:DH + 1], 1.0).then_inc(v_set, 1)
            pool.wait_ge(v_set, 1)

            with pool.Fori(0, NP // 2) as i:
                for s in range(2):
                    u = 2 * i + s
                    pool.wait_ge(a_r.sem, a_r.upto(u))
                    pool.wait_ge(a_st[s].sem, a_st[s].upto(i - 1))
                    pool.tensor_tensor(parts[:, s, 1, :, :], rest[:, s, :, :], zeros[:].unsqueeze(2).to_broadcast([P, 4, 2 * P]), ALU.add).then_inc(a_p2.sem, 1)
                    pool.wait_ge(a_p2.sem, a_p2.upto(u))
                    pool.tensor_tensor(parts[:, s, 2, :, :], rest[:, s, :, :], parts[:, s, 1, :, :],
                                       ALU.subtract).then_inc(a_p3.sem, 1)
            meet(pool, 1)
            meet(pool, 2)
            pool_scatter(pool, c, 0, xs0, E * CAP)
            pool_gather(pool, c, 0, ys0, E * CAP, [(f_ys.sem, f_ys.upto(E - 1))])
            meet(pool, 3)
            meet(pool, 4)
            meet(pool, 5)
            pool_scatter(pool, c, 1, xs1, NX * P)
            pool_gather(pool, c, 1, ys1, NX * P, [(s.sem, s.upto(NX // 2 - 1)) for s in m_st])
            meet(pool, 6)

        @block.scalar
        def _(act):
            c = Chain(act, chain_act)
            act.wait_ge(q_sub, 1)
            act.activation(qsm[:, 2, :], qsm[:, 1, :], ACT.Exp).then_inc(q_exp, 1)
            act.wait_ge(v_set, 1)
            with act.Fori(0, NP // 2) as i:
                for s in range(2):
                    u = 2 * i + s
                    act.wait_ge(a_tr.sem, a_tr.upto(u))
                    act.wait_ge(a_v.sem, a_v.upto(u - 2))
                    act.copy(xT[:, s, :, :], ps[:, s, :].rearrange("p (k q) -> p k q", k=KC))\
                       .then_inc(a_xt.sem, 1)
                    act.wait_ge(a_qk.sem, a_qk.upto(u))
                    act.wait_ge(a_st[s].sem, a_st[s].upto(i - 1))
                    act.copy(parts[:, s, 0, :, :],
                             ps[:, 2 + 2 * s:4 + 2 * s, :].rearrange("p m (n q) -> p (m n) q", n=2))\
                       .then_inc(a_p1.sem, 1)
                    act.wait_ge(a_v.sem, a_v.upto(u))
                    act.copy(vslot[:, s, :, :, 0:DH],
                             ps[:, 6 + s, :].rearrange("p (j h d) -> p j h d", j=2, h=H))\
                       .then_inc(a_vs.sem, 1)

            def exps(n, q0, q1):
                for q in range(q0, q1):
                    act.wait_ge(h_st.sem, h_st.upto(n, q + 1))
                    act.wait_ge(h_pv.sem, h_pv.upto(n, q - 3))
                    act.activation(PT[:, q % 4, :], ps[:, 4 + q % 2, :], ACT.Exp).then_inc(h_e.sem, 1)

            def evac(n):
                act.wait_ge(h_pv.sem, h_pv.upto(n))
                act.wait_ge(h_fin.sem, h_fin.upto(n - 1))
                act.copy(Osb[:], ps[:, 6, :]).then_inc(h_ev.sem, 1)

            def head(n, first=False):
                exps(n, 0, 2)
                if not first:
                    evac(n - 1)
                exps(n, 2, 16)

            for n in range(4):
                head(n, n == 0)
            with act.Fori(1, B * H // 4) as i:
                for hh in range(4):
                    head(4 * i + hh)
            evac(B * H - 1)
            meet(act, 1)
            act_cross(act, c, 0)
            meet(act, 2)
            act.wait_ge(r_sub, 1)
            act.activation(pe_[:], pe_[:], ACT.Exp).then_inc(r_exp, 1)
            act_experts0(act)
            meet(act, 3)
            act_retention(act)
            meet(act, 4)
            act_cross(act, c, 1)
            meet(act, 5)
            act.wait_ge(r_sub, 2)
            act.activation(pe_[:], pe_[:], ACT.Exp).then_inc(r_exp, 1)
            act_experts1(act)
            meet(act, 6)

        @block.vector
        def _(v):
            c = Chain(v, chain_dve)
            v.wait_ge(loaded, A_LOADS)
            c(v.tensor_copy(identb[:], ident[:]))
            c(v.tensor_copy(lower[:], lowf[:]))
            c(v.tensor_reduce(qsm[:, 0, 0:1], qwB[:], AX.X, ALU.max))
            v.tensor_scalar(qsm[:, 1, :], qwB[:], qsm[:, 0, 0:1], None, ALU.subtract).then_inc(q_sub, 1)
            v.wait_ge(q_exp, 1)
            c(v.tensor_reduce(qsm[:, 0, 0:1], qsm[:, 2, :], AX.X, ALU.add))
            c(v.reciprocal(qsm[:, 0, 1:2], qsm[:, 0, 0:1]))
            c(v.tensor_scalar(qsm[:, 3, :], qsm[:, 2, :], qsm[:, 0, 1:2], float((DH // 2) ** -0.5),
                              ALU.mult, ALU.mult))
            half = lambda m, e: m[:].rearrange("p k (h e d) -> p (k h) e d", h=H, e=2)[:, :, e, :]
            for e in range(2):
                c(v.tensor_scalar(half(wkE, e), half(wkA, 0), qsm[:, 3, 2 * e:2 * e + 1], None, ALU.mult))
                ins = v.scalar_tensor_tensor(out=half(wkE, e), in0=half(wkA, 1),
                                             scalar=qsm[:, 3, 2 * e + 1:2 * e + 2], in1=half(wkE, e),
                                             op0=ALU.mult, op1=ALU.add)
            ins.then_inc(a_w, 1)

            def qk_rest(u, s):
                v.wait_ge(a_p1.sem, a_p1.upto(u))
                v.wait_ge(a_p3.sem, a_p3.upto(u - 2))
                v.tensor_tensor(rest[:, s, :, :],
                                ps[:, 2 + 2 * s:4 + 2 * s, :].rearrange("p m (n q) -> p (m n) q", n=2),
                                parts[:, s, 0, :, :], ALU.subtract).then_inc(a_r.sem, 1)

            ln_rows(v, c, 0, 0, a_xn, a_tr)
            with c.fori(NP // 2 - 1, 34) as i:
                for s in range(2):
                    ln_rows(v, c, 2 * i + s + 1, 1 - s, a_xn, a_tr)
                    qk_rest(2 * i + s, s)
            ln_rows(v, c, NP - 1, 1, a_xn, a_tr)
            qk_rest(NP - 2, 0)
            qk_rest(NP - 1, 1)

            def maxima(n, s, t0, t1):
                for t in range(t0, t1):
                    v.wait_ge(h_s.sem, h_s.upto(n, t + 1))
                    v.tensor_reduce(mx[:, s, t:t + 1], ps[:, 2 * (t % 2):2 * (t % 2) + 2, :], AX.XY,
                                    ALU.max).then_inc(h_rm.sem, 1)

            def split_max(n, s):
                v.wait_ge(h_rm.sem, h_rm.upto(n))
                c(v.tensor_scalar(mneg[:, 0, :], mx[:, s, :], -1.0, None, ALU.mult))
                v.wait_ge(h_mt.sem, h_mt.upto(n - 2))
                c(v.tensor_copy(mpart[:, s, 0, :], mneg[:, 0, :]))
                c(v.tensor_tensor(mneg[:, 1, :], mneg[:, 0, :], mpart[:, s, 0, :], ALU.subtract))
                c(v.tensor_copy(mpart[:, s, 1, :], mneg[:, 1, :]))
                v.tensor_tensor(mpart[:, s, 2, :], mneg[:, 1, :], mpart[:, s, 1, :], ALU.subtract)\
                 .then_inc(h_mp.sem, 1)

            def copy_max(n, s, sl, step):
                v.wait_ge(h_mt.sem, h_mt.upto(n))
                v.wait_ge(h_mr[sl].sem, h_mr[sl].upto(step - 1) if sl >= 2 else h_mr[sl].upto(step - 1))
                v.tensor_copy(mrow[:, s, :], ps[0:24, 7, 0:P // 2].bitcast(BF16)).then_inc(h_mc.sem, 1)

            def normalise(n):
                v.wait_ge(h_fin.sem, h_fin.upto(n))
                y = ps[:, 7, 0:256].rearrange("p (j c d) -> p j c d", j=4, c=2)
                c(v.reciprocal(rec[:].unsqueeze(3), y[:, :, :, DH:DH + 1]))
                o = O_all[:, bass.ds((n // H) * TB, TB), bass.ds((n % H) * DH, DH)]\
                    .rearrange("p (c j) d -> p j c d", c=2)
                v.tensor_tensor(o, y[:, :, :, 0:DH], rec[:].unsqueeze(3).to_broadcast([P, 4, 2, DH]),
                                ALU.mult).then_inc(h_no.sem, 1)

            def head(n, hh, i, first=False, last=False):
                split_max(n + 1, (hh + 1) % 2) if not (last and hh == 3) else None
                if not (last and hh >= 2):
                    maxima(n + 2, hh % 2, 0, 3)
                if not first:
                    normalise(n - 1)
                if not (last and hh >= 2):
                    maxima(n + 2, hh % 2, 3, 6)
                if not (last and hh == 3):
                    copy_max(n + 1, (hh + 1) % 2, (hh + 1) % 4, i + (hh + 1) // 4)
                if not (last and hh >= 2):
                    maxima(n + 2, hh % 2, 6, 8)

            maxima(0, 0, 0, 8)
            split_max(0, 0)
            maxima(1, 1, 0, 6)
            copy_max(0, 0, 0, 0)
            maxima(1, 1, 6, 8)
            for n in range(4):
                head(n, n, 0, n == 0)
            with c.fori(B * H // 4 - 2, 4 * 5) as i:
                for hh in range(4):
                    head(4 * i + 4 + hh, hh, i + 1)
            for hh in range(4):
                head(B * H - 4 + hh, hh, B * H // 4 - 1, False, True)
            normalise(B * H - 1)
            meet(v, 1)
            dve_cross(v, c, 0)
            meet(v, 2)
            dve_route0(v, c)
            dve_experts0(v, c)
            dve_combine(v, c, 0)
            meet(v, 3)
            dve_retention(v, c)
            meet(v, 4)
            dve_cross(v, c, 1)
            meet(v, 5)
            dve_route1(v, c)
            dve_experts1(v, c)
            dve_combine(v, c, 1)
            meet(v, 6)

        @block.tensor
        def _(pe):
            def project(u, s):
                pe.wait_ge(a_xt.sem, a_xt.upto(u))
                pe.wait_ge(a_r.sem, a_r.upto(u - 2))
                for m in range(4):
                    wm = (wqA, wkE)[m // 2]
                    for k in range(KC):
                        ins = pe.matmul(ps[:, 2 + 2 * s + m // 2, (m % 2) * 256:(m % 2) * 256 + 256],
                                        wm[:, k, (m % 2) * P:(m % 2) * P + P], xT[:, s, k, :],
                                        start=(k == 0), stop=(k == KC - 1))
                ins.then_inc(a_qk.sem, 1)
                pe.wait_ge(a_vs.sem, a_vs.upto(u - 2))
                for j in range(2):
                    for k in range(KC):
                        ins = pe.matmul(ps[:, 6 + s, j * 256:j * 256 + 256], xT[:, s, k, j * P:j * P + P],
                                        wvA[:, k, :], start=(k == 0), stop=(k == KC - 1))
                ins.then_inc(a_v.sem, 1)

            pe.wait_ge(loaded, A_LOADS)
            transpose_rows(pe, 0, 0, 0, a_xn, a_xt, a_tr)
            pe.wait_ge(a_w, 1)
            with pe.Fori(0, NP // 2 - 1) as i:
                for s in range(2):
                    transpose_rows(pe, 2 * i + s + 1, 1 - s, 1 - s, a_xn, a_xt, a_tr)
                    project(2 * i + s, s)
            transpose_rows(pe, NP - 1, 1, 1, a_xn, a_xt, a_tr)
            project(NP - 2, 0)
            project(NP - 1, 1)

            for s_ in (a_xt, a_r, a_vs):
                pe.wait_ge(s_.sem, s_.upto(NP - 1))

            def scores(n, sl, t):
                pe.wait_ge(h_rm.sem, h_rm.upto(n, t - 1))
                for q in range(2):
                    ins = pe.matmul(ps[:, 2 * (t % 2) + q, :], QS[0:96, sl, t * P:t * P + P],
                                    KS[0:96, sl, q * 512:q * 512 + 512], start=True, stop=True)
                ins.then_inc(h_s.sem, 1)

            def scores_t(n, sl, t):
                for q in range(2):
                    pe.wait_ge(h_e.sem, h_e.upto(n, 2 * t + q - 1))
                    pe.matmul(ps[:, 4 + q, :], KS[0:99, sl, t * P:t * P + P],
                              QS[0:99, sl, q * 512:q * 512 + 512], start=True, stop=True)\
                      .then_inc(h_st.sem, 1)

            def weigh(n, sl, t):
                for q in range(2):
                    g = 32 * (2 * (t % 2) + q)
                    pe.wait_ge(h_e.sem, h_e.upto(n, 2 * t + q + 1))
                    pe.matmul(ps[g:g + 32, 6, :], VS[:, sl, t, :], PT[:, (2 * t + q) % 4, :],
                              start=(t < 2), stop=(t >= 6)).then_inc(h_pv.sem, 1)

            def sum_tiles(n):
                pe.wait_ge(h_ev.sem, h_ev.upto(n))
                pe.wait_ge(h_mc.sem, h_mc.upto(n + 1))
                for j in range(4):
                    ins = pe.matmul(ps[:, 7, j * 64:j * 64 + 64], Osb[:, j * P:j * P + P], sel[:],
                                    start=True, stop=True)
                ins.then_inc(h_fin.sem, 1)

            def turn_max(n, s):
                pe.wait_ge(h_mp.sem, h_mp.upto(n))
                pe.wait_ge(h_no.sem, h_no.upto(n - 2))
                pe.transpose(ps[0:24, 7, 0:P // 2].bitcast(BF16),
                             mpart[:, s, :, :].rearrange("p a t -> p (a t)"), identb[:])\
                  .then_inc(h_mt.sem, 1)

            def head(n, hh, i, first=False, last=False):
                sl, s2 = hh, (hh + 2) % 4
                ahead = not (last and hh >= 2)
                pe.wait_ge(h_mr[sl].sem, h_mr[sl].upto(i))
                if ahead:
                    pe.wait_ge(h_ld[s2].sem, h_ld[s2].upto(i + (hh + 2) // 4))
                for t in range(TB):
                    scores_t(n, sl, t)
                    if ahead:
                        scores(n + 2, s2, t)
                    if t > 0:
                        if t == 1:
                            pe.wait_ge(h_ev.sem, h_ev.upto(n - 1))
                        weigh(n, sl, t - 1)
                    elif not first:
                        weigh(n - 1, (sl + 3) % 4, TB - 1)
                    if t == 2 and not first:
                        sum_tiles(n - 1)
                    if t == 4 and not (last and hh == 3):
                        turn_max(n + 1, (hh + 1) % 2)

            pe.wait_ge(ones_set, 1)
            for n in range(2):
                pe.wait_ge(h_ld[n].sem, h_ld[n].upto(0))
                for t in range(TB):
                    scores(n, n, t)
                    if n == 1 and t == 4:
                        turn_max(0, 0)
            for n in range(4):
                head(n, n, 0, n == 0)
            with pe.Fori(1, B * H // 4 - 1) as i:
                for hh in range(4):
                    head(4 * i + hh, hh, i)
            for hh in range(4):
                head(B * H - 4 + hh, hh, B * H // 4 - 1, False, True)
            weigh(B * H - 1, 3, TB - 1)
            pe.wait_ge(h_ev.sem, h_ev.upto(B * H - 1))
            pe.wait_ge(h_no.sem, h_no.upto(B * H - 2))
            for j in range(4):
                ins = pe.matmul(ps[:, 7, j * 64:j * 64 + 64], Osb[:, j * P:j * P + P], sel[:],
                                start=True, stop=True)
            ins.then_inc(h_fin.sem, 1)
            meet(pe, 1)
            pe_cross(pe, 0)
            meet(pe, 2)
            pe_route0(pe)
            pe_experts0(pe)
            meet(pe, 3)
            pe_retention(pe)
            meet(pe, 4)
            pe_cross(pe, 1)
            meet(pe, 5)
            pe_count(pe, BITS + 4)
            pe_before(pe, BITS + 5)
            pe_experts1(pe)
            meet(pe, 6)


_NAMES = ["x", "ctx_1024", "mask_1x1xSxS2_bk0", "mask_Bx1x1xS2_bf1"]


def kernel(**inputs):
    import concourse.bacc as _bacc
    from concourse.bass_utils import run_bass_kernel_spmd as _run

    nc = _bacc.Bacc("TRN2", target_bir_lowering=False, num_devices=1)
    arrays, aps = {}, {}

    def give(name, a):
        a = np.ascontiguousarray(a)
        arrays["in_" + name] = a
        aps[name] = nc.dram_tensor("in_" + name, a.shape, mybir.dt.from_np(a.dtype), kind="ExternalInput").ap()

    give("c_ident", np.eye(P, dtype=np.float32))
    rows = np.arange(P)
    give("c_sel", (rows[:, None] % 64 == np.arange(64)[None, :]).astype(np.float32))
    give("c_desc", np.tile(E - np.arange(E, dtype=np.float32), (P, 1)))
    give("c_first", np.tile(CAP * np.arange(E, dtype=np.float32), (P, 1)))
    give("c_before", np.tile(np.tri(E, E, -1, dtype=np.float32)[None], (P, 1, 1)))
    give("c_tiles", np.tile(np.arange(NX, dtype=np.float32), (P, 1)))
    give("c_bits", np.tile((1 << np.arange(29, -1, -1))[None, :, None], (P, 1, E)).astype(np.int32))
    give("c_lower", (rows[:, None] < rows[None, :]).astype(np.float32))
    give("c_hmask", (rows[:, None] // DH == np.arange(HG)[None, :]).astype(np.float32))
    give("c_halves", (rows[:, None] // SC == np.arange(2)[None, :]).astype(np.float32))
    g = 1.0 - 2.0 ** (-5.0 - np.arange(H))
    spot = np.arange(P)[:, None] + 1
    give("c_decay", np.stack([g ** spot, g ** -spot], 1).astype(np.float32))
    gd = (g ** P).reshape(KC, HG).repeat(DH, 1)
    give("c_gP", gd.T.astype(np.float32))
    give("c_bdg", ((rows[:, None, None] // DH == rows[None, None, :] // DH) * gd.T[:, :, None]).astype(np.float32))
    give("c_causal", (rows[:, None] <= rows[None, :]).astype(np.float32))
    give("c_keep", np.tile((np.arange(NT) % TB != TB - 1).astype(np.float32), (P, 1)))
    rate = (10.0 ** (-4.0 * np.arange(0, DH, 2, dtype=np.float32) / DH)).astype(np.float32)
    turn = (np.arange(S, dtype=np.float32)[:, None] * rate[None, :]).astype(np.float64)
    give("c_turns", np.stack([np.cos(turn), np.sin(turn)]).reshape(2, TB, P, DH // 2)
         .transpose(2, 0, 1, 3).astype(np.float32))
    for name, a in inputs.items():
        a = np.asarray(a)
        if name == "ctx_1024":
            a = a.reshape(B * SC, D).T
        elif name.startswith("L0_xattn_W"):
            a = a.T
        elif name in ("L1_attn_WQ", "L1_attn_WK", "L1_attn_WV"):
            a = a.reshape(D, D).T
        elif name in ("L0_ffn_ff_pre_act_weight", "L0_ffn_gate_weight", "L0_ffn_ff_post_act_weight"):
            a = a.transpose(0, 2, 1)
        elif name in ("L1_attn_gamma", "L1_attn_beta", "L0_xattn_bq", "L0_xattn_bk", "L1_xattn_bq", "L1_xattn_bk"):
            a = a.reshape(KC, P).T
        elif name == "L1_ffn_b1":
            a = a.reshape(E, F // P, P).transpose(2, 0, 1)
        elif name == "L0_ffn_router_weight":
            a = a.T
        give(name, a)
    out = nc.dram_tensor("out_0", (B, S, D), F32, kind="ExternalOutput").ap()
    decoder(nc, aps["x"], aps["ctx_1024"], aps["mask_1x1xSxS2_bk0"], aps["mask_Bx1x1xS2_bf1"], aps, out)
    r = _run(nc, [arrays], core_ids=[0])
    return r.results[0]["out_0"]
```

```python
from contextlib import ExitStack, contextmanager

import numpy as np
import concourse.bass as bass
from concourse import mybir

F32 = mybir.dt.float32
BF16 = mybir.dt.bfloat16
I32 = mybir.dt.int32
U32 = mybir.dt.uint32
U8 = mybir.dt.uint8
ALU = mybir.AluOpType
ACT = mybir.ActivationFunctionType
AX = mybir.AxisListType

P = 128
B, S, D, H, DH = 2, 1024, 256, 16, 16
T = B * S
NT = T // P
NP = NT // 2
NX = 40
TB = S // P
SC = 64
E, F = 8, 1024
KC = D // P
HG = P // DH
CAP = 640
LN_EPS = 1e-5
LAG = 4


class Sig:

    def __init__(self, sem, per=1):
        self.sem, self.per, self.base = sem, per, LAG * per

    def upto(self, step, n=None):
        return self.base + self.per * step + (self.per if n is None else n)


class Chain:

    def __init__(self, eng, sem):
        self.eng, self.sem, self.n, self.loop = eng, sem, 0, None

    def __call__(self, ins):
        ins.then_inc(self.sem, 1)
        self.n += 1
        self.eng.wait_ge(self.sem, self.n if self.loop is None else self.loop * self.k + self.n)
        return ins

    @contextmanager
    def fori(self, count, k):
        with self.eng.Fori(0, count) as i:
            self.loop, self.k, before = i, k, self.n
            yield i
            assert self.n - before == k, f"{self.n - before} links in the body, not {k}"
        self.loop, self.n = None, before + count * k


def decoder(nc, x_in, ctxT, mask0, mask1, w, out):
    ctx = ExitStack()
    with ctx:
        def sb(name, shape, dt=F32):
            return ctx.enter_context(nc.sbuf_tensor(name, shape, dt))

        def sem(name):
            return ctx.enter_context(nc.semaphore(name))

        sigs = []

        def sig(name, per=1):
            s = Sig(sem(name), per)
            sigs.append(s)
            return s

        def dram(name, shape, dt=F32):
            return nc.dram_tensor(name, shape, dt, kind="Internal").ap()

        ps = ctx.enter_context(nc.psum_tensor("ps", [P, 8, 512], F32))

        xr = sb("xr", [P, NT, D])
        ident = sb("ident", [P, P])
        identb = sb("identb", [P, P], BF16)
        xn = sb("xn", [P, 2, 2, D])
        xT = sb("xT", [P, 2, KC, 2 * P])
        wide = sb("wide", [P, 16384])
        idle = sb("idle", [P, 1])
        zeros = sb("zeros", [P, 4])
        stats = sb("stats", [P, NT, 6])
        mv = sb("mv", [P, NT, 2])
        nv = sb("nv", [P, 4, NT])
        O_all = sb("O_all", [P, NT, D])
        lg = sb("lg", [P, NT, E])

        xw_all = sb("xw_all", [P, 5, KC * D])
        part_of = lambda n: xw_all[:, n, :].rearrange("p (k d) -> p k d", k=KC)
        xw = {n: part_of(i) for i, n in enumerate("qkvo")}
        woA = part_of(4)
        ctxs = sb("ctxs", [P, KC, B * SC])
        ctx2 = sb("ctx2", [P, B, KC, 2, SC])
        rw = sb("rw", [P, KC, E])
        hmask = sb("hmask", [P, HG])
        halves = sb("halves", [P, 2])
        mask_u8 = sb("mask_u8", [P, TB, SC], U8)
        bq = sb("bq", [P, KC])
        bk = sb("bk", [P, KC])
        bv = sb("bv", [P, D])
        bo = sb("bo", [P, D])
        rb = sb("rb", [P, E])

        EPS = 1.1920929e-07
        BITS = 30
        nochoice = float(1 << 20)
        desc = sb("desc", [P, E])
        first = sb("first", [P, E])
        bits = sb("bits", [P, BITS, E], I32)
        lower = sb("lower", [P, P], BF16)
        onesb = sb("onesb", [P, P], BF16)
        lowf = sb("lowf", [P, P])
        pb = sb("pb", [P, NT, E])
        pe_ = sb("pexp", [P, NT, E])
        oh = [sb(f"oh{k}", [P, NT, E]) for k in range(2)]
        tm = sb("tm", [P, NT, E])
        tb = sb("tb", [P, NT, E], BF16)
        Wt = sb("Wt", [P, NT, E])
        Ct = sb("Ct", [P, NT, E])
        Kp = sb("Kp", [P, NT, E])
        tk = sb("tk", [P, 8, NT])
        top = [sb(f"top{k}", [P, NT]) for k in range(2)]
        gw = [sb(f"gw{k}", [P, NT]) for k in range(2)]
        thr = sb("thr", [P, E], I32)
        cand = sb("cand", [P, E], I32)
        c8 = sb("c8", [P, E])
        c8b = sb("c8b", [P, E], BF16)
        idxS = [sb(f"idxS{k}", [P, NT], U32) for k in range(2)]
        idxG = [sb(f"idxG{k}", [P, NT], U32) for k in range(2)]
        zrow = sb("zrow", [P, D])
        before_e = sb("before_e", [P, E, E])
        tile_no = sb("tile_no", [P, NX])
        m3 = sb("m3", [P, E, E])
        n8 = sb("n8", [P, E])
        n8i = sb("n8i", [P, E], I32)
        base8 = sb("base8", [P, E])
        ex = sb("ex", [P, NX, E])
        exf = sb("exf", [P, NX])
        exi = sb("exi", [P, NX], I32)

        chain_dve = sem("chain_dve")
        chain_act = sem("chain_act")
        chain_pool = sem("chain_pool")
        barrier = sem("barrier")
        loaded = sem("loaded")
        stored = sem("stored")

        qk_parts = dram("qk_parts", [3, B, 2 * D, S], BF16)
        v_heads = dram("v_heads", [B, H, P, TB, 32])
        sa = ExitStack()
        ctx.enter_context(sa)

        def sbA(name, shape, dt=F32):
            return sa.enter_context(nc.sbuf_tensor(name, shape, dt))

        wqA = sbA("wqA", [P, KC, D])
        wkA = sbA("wkA", [P, KC, D])
        wkE = sbA("wkE", [P, KC, D])
        wvA = sbA("wvA", [P, KC, D])
        qwB = sbA("qwB", [P, 4])
        qsm = sbA("qsm", [P, 4, 4])
        parts = sbA("parts", [P, 2, 3, 4, 2 * P], BF16)
        rest = sbA("rest", [P, 2, 4, 2 * P])
        vslot = sbA("vslot", [P, 2, 2, H, 32])
        QS = sbA("QS", [P, 4, S], BF16)
        KS = sbA("KS", [P, 4, S], BF16)
        VS = sbA("VS", [P, 4, TB, 32])
        PT = sbA("PT", [P, 4, 512])
        Osb = sbA("Osb", [P, 512])
        mx = sbA("mx", [P, 2, TB])
        mneg = sbA("mneg", [P, 2, TB])
        mpart = sbA("mpart", [P, 2, 3, TB], BF16)
        mrow = sbA("mrow", [24, 2, P], BF16)
        sel = sbA("sel", [P, 64])
        rec = sbA("rec", [P, 4, 2])

        a_xn = sig("a_xn")
        a_tr = sig("a_tr")
        a_xt = sig("a_xt")
        a_qk = sig("a_qk")
        a_v = sig("a_v")
        a_p1 = sig("a_p1")
        a_r = sig("a_r")
        a_p2 = sig("a_p2")
        a_p3 = sig("a_p3")
        a_vs = sig("a_vs")
        a_st = [sig(f"a_st{s}", 5 * 16) for s in range(2)]
        h_ld = [sig(f"h_ld{s}", 7 * 16) for s in range(4)]
        h_mr = [sig(f"h_mr{s}", 16) for s in range(4)]
        h_s = sig("h_s", 8)
        h_rm = sig("h_rm", 8)
        h_mp = sig("h_mp")
        h_mt = sig("h_mt")
        h_mc = sig("h_mc")
        h_st = sig("h_st", 16)
        h_e = sig("h_e", 16)
        h_pv = sig("h_pv", 16)
        h_ev = sig("h_ev")
        h_fin = sig("h_fin")
        h_no = sig("h_no")

        sa.close()

        sx = ExitStack()
        ctx.enter_context(sx)

        def sbX(name, shape, dt=F32):
            return sx.enter_context(nc.sbuf_tensor(name, shape, dt))

        bq4 = sbX("bq4", [P, KC])
        kc = sbX("kc", [P, KC, B * SC])
        vd = sbX("vd", [P, B, D])
        Kbd = sbX("Kbd", [P, B, KC, HG, SC])
        Vbd = sbX("Vbd", [P, B, HG, 2, DH + 1])
        mask_no = sbX("mask_no", [P, TB, SC], U8)
        mslot = sbX("mslot", [P, 2, 2, SC], U8)
        fill0 = sbX("fill0", [P, 1])
        mask1_u8 = sbX("mask1_u8", [P, B, SC], U8)
        mask1_f = sbX("mask1_f", [P, B, SC])
        orow = sbX("orow", [P, 2, D])
        orow2 = sbX("orow2", [P, 2, D])
        oT = sbX("oT", [P, 2, KC, 2 * P])
        qT = sbX("qT", [P, 2, KC, 2 * P])
        pr = sbX("pr", [P, 2, H, SC])
        mxx = sbX("mxx", [P, 2, H])
        prT = sbX("prT", [P, HG, P])
        recx = sbX("recx", [P, H])

        x_ld = sem("x_ld")
        x_ctx = sig("x_ctx", 2)
        x_cr = sig("x_cr", 1)
        x_or = [sig(f"x_or{s}", 16) for s in range(2)]
        x_ms = [sig(f"x_ms{s}", 16) for s in range(2)]
        x_res = sig("x_res")
        x_lnA, x_lnB = sig("x_lnA"), sig("x_lnB")
        x_no = sig("x_no", 2)
        x_sm = sig("x_sm", 2)
        x_rb = sig("x_rb")
        x_sta = sig("x_sta")
        x_lg = sig("x_lg")
        x_t = [sig(f"x_t{r}") for r in range(4)]
        x_te = [sig(f"x_te{r}") for r in range(4)]
        x_oA, x_oB = sig("x_oA"), sig("x_oB")
        x_q = sig("x_q")
        x_qe = sig("x_qe")
        x_s = sig("x_s", 2)
        x_e = sig("x_e", 2)
        x_pt = sig("x_pt", 2)
        x_pe = sig("x_pe", 2)
        x_av = sig("x_av", 2)
        x_r = sig("x_r")
        x_mk, x_m1 = sem("x_mk"), sem("x_m1")
        x_xa = sig("x_xa", 16)

        sg_ = ExitStack()
        ctx.enter_context(sg_)

        def sbG(name, shape, dt=F32):
            return sg_.enter_context(nc.sbuf_tensor(name, shape, dt))

        xs0 = dram("xs0", [E * CAP, D])
        ys0 = dram("ys0", [E * CAP, D])
        xs1 = dram("xs1", [NX * P, D])
        ys1 = dram("ys1", [NX * P, D])
        xe = sbG("xe", [P, 2, 5, D])
        xTe = sbG("xTe", [P, KC, CAP])
        hTe = sbG("hTe", [P, F // P, CAP])
        sgt = prT[:].rearrange("p h q -> p (h q)")[:, 0:CAP].rearrange("p (s q) -> p s q", s=2)
        yrow = pr[:].rearrange("p j h k -> p (j h k)")[:, 0:5 * D].rearrange("p (r d) -> p r d", r=5)
        yg = hTe[:].rearrange("p f c -> p (f c)")[:, 0:4 * 2 * D].rearrange("p (q k d) -> p q k d", q=4, k=2)

        sg_.close()
        sr = ExitStack()
        ctx.enter_context(sr)

        def sbR(name, shape, dt=F32):
            return sr.enter_context(nc.sbuf_tensor(name, shape, dt))

        place = [2 * 3 * KC * F]

        def behind(*shape):
            n = int(np.prod(shape))
            flat_ = wide[:, place[0]:place[0] + n]
            place[0] += n
            names = "abc"[:len(shape)]
            return flat_.rearrange(f"p ({' '.join(names)}) -> p {' '.join(names)}", **dict(zip(names, shape)))

        wqk = behind(KC, 2 * D)
        wvR = behind(KC, D)
        woR = behind(KC, D)
        turns = behind(2, TB, DH // 2)
        decay = behind(2, H)
        causal = behind(P)
        bdg = behind(KC, P)
        gP = behind(KC)
        keepS = behind(NT)
        gamma = behind(KC)
        beta = behind(KC)
        qkr = sbR("qkr", [P, 2, 2 * D])
        half_turn = sbR("half_turn", [P, 2 * D])
        vR = sbR("vR", [P, 2, D])
        qkT = sbR("qkT", [P, 2 * KC, P])
        qbd = O_all[:].rearrange("p t d -> p (t d)")[:, 0:KC * HG * P].rearrange("p (m h q) -> p m h q", m=KC, h=HG)
        wS = sbR("wS", [P, 2, 4, P])
        State = sbR("State", [P, KC, P])
        newS = sbR("newS", [P, KC, P])
        Rr = sbR("Rr", [P, 2, D])
        Rq = sbR("Rq", [P, D])
        gmean = sbR("gmean", [P, H])
        gvar = sbR("gvar", [P, H])
        gnv = sbR("gnv", [P, 4, H])
        three_halves = sbR("three_halves", [P, H])
        oTR = sbR("oTR", [P, KC, P])

        e_ld = sem("e_ld")
        e_z = sem("e_z")
        e_ln = sig("e_ln")
        e_tx = sig("e_tx")
        e_xt = sig("e_xt")
        e_qk = sig("e_qk")
        e_rot = sig("e_rot")
        e_tq = sig("e_tq")
        e_ex = sig("e_ex", 2)
        e_ex1 = sig("e_ex1")
        e_s = sig("e_s", 4)
        e_m = sig("e_m", 4)
        e_av = sig("e_av", 4)
        e_rv = sig("e_rv")
        e_su = sig("e_su")
        e_st = sig("e_st")
        e_gv = sig("e_gv")
        e_gr = sig("e_gr")
        e_gn = sig("e_gn")
        e_ot = sig("e_ot")
        e_oc = sig("e_oc")
        e_y = sig("e_y")
        e_rs = sig("e_rs")

        sr.close()
        sx.close()
        se = ExitStack()
        ctx.enter_context(se)

        def sbE(name, shape, dt=F32):
            return se.enter_context(nc.sbuf_tensor(name, shape, dt))

        w2s = sbE("w2s", [P, E, F // P, D])
        b1s = sbE("b1s", [P, E, F // P])
        b2s = sbE("b2s", [P, E, D])
        small = xw_all[:].rearrange("p n f -> p (n f)")
        rows1 = small[:, 0:512].rearrange("p (s d) -> p s d", s=2)
        xTm = small[:, 512:1024].rearrange("p (s k q) -> p s k q", s=2, k=KC)
        hrow = xn[:].rearrange("p s j d -> p s (j d)")
        hTm = small[:, 1024:2048].rearrange("p (g q) -> p g q", q=P)
        yrow1 = small[:, 2048:2560].rearrange("p (s d) -> p s d", s=2)
        m_w = sem("m_w")
        m_w2 = sem("m_w2")
        m_x = [sig(f"m_x{s}", 16) for s in range(2)]
        m_t = sig("m_t")
        m_tc = sig("m_tc")
        m_h = sig("m_h", 2)
        m_hc = sig("m_hc", 2)
        m_ht = sig("m_ht", 2)
        m_a = sig("m_a", 2)
        m_y = sig("m_y")
        m_yc = sig("m_yc")
        m_st = [sig(f"m_st{s}", 16) for s in range(2)]
        yg1 = w2s[:].rearrange("p e g d -> p (e g d)")[:, 0:4 * 2 * D].rearrange("p (q k d) -> p q k d", q=4, k=2)

        r_sub = sem("r_sub")
        r_exp = sem("r_exp")
        r_rhs = sem("r_rhs")
        r_sum = sem("r_sum")
        r_idx = sem("r_idx")
        g_z = sem("g_z")
        g_sc = [sem("g_sc0"), sem("g_sc1")]
        f_w = [sig(f"f_w{s}", 48) for s in range(2)]
        f_x = [sig(f"f_x{s}", 16) for s in range(2)]
        f_t = sig("f_t")
        f_te = sig("f_te", 3)
        f_h = sig("f_h", 16)
        f_a = sig("f_a", 16)
        f_m = sig("f_m", 16)
        f_y = sig("f_y", 5)
        f_ye = sig("f_ye", 5)
        f_ys = sig("f_ys", 16)
        g_ld = [sem(f"g_ld{q}") for q in range(4)]
        g_use = sem("g_use")
        z_set = sem("z_set")

        q_sub, q_exp, v_set, ones_set, sa_ready, a_w = (sem(n) for n in ("q_sub", "q_exp", "v_set", "ones_set", "sa_ready", "a_w"))
        A_LOADS = 16 * 16
        NLOAD = [0]

        def load(eng, dst, src):
            eng.dma_start(dst, src).then_inc(loaded, 16)
            NLOAD[0] += 16

        def meet(eng, n):
            eng.drain().then_inc(barrier, 1)
            eng.wait_ge(barrier, 5 * n)

        block = ctx.enter_context(nc.Block())

        chunked = lambda ap: ap.rearrange("(k p) n -> p k n", p=P)

        def finish(sp):
            sp.dma_start(out.rearrange("b (t p) d -> p (b t) d", p=P), xr[:]).then_inc(stored, 16)
            sp.wait_ge(stored, 16)


        def row_stats(v, t, n=1):
            for j in range(n):
                ins = v.bn_stats(stats[:, bass.ds(t + j, 1), :].rearrange("p a s -> p (a s)"),
                                 xr[:, bass.ds(t + j, 1), :].rearrange("p a d -> p (a d)"))
            return ins

        def norm_factors(v, c):
            for t in range(NT):
                ins = v.bn_aggr(mv[:, t, :], stats[:, t, :])
            c(ins)
            rsqrt(v, c, nv, mv[:, :, 1], LN_EPS)

        def norm_rows(v, out_, t):
            return v.tensor_scalar(out_, xr[:, bass.ds(t, 1), :].rearrange("p a d -> p (a d)"),
                                   mv[:, bass.ds(t, 1), 0:1].rearrange("p a b -> p (a b)"),
                                   nv[:, 0, bass.ds(t, 1)], ALU.subtract, ALU.mult)

        def ln_rows(v, u, s, xn_sig, tr_sig):
            v.wait_ge(tr_sig.sem, tr_sig.upto(u - 2))
            for j in range(2):
                ins = norm_rows(v, xn[:, s, j, :], 2 * u + j)
            ins.then_inc(xn_sig.sem, 1)

        def rsqrt(v, c, n4, var, eps):
            y, a, e, g = (n4[:, i] for i in range(4))
            c(v.tensor_scalar(e, var, float(eps), None, ALU.add))
            c(v.tensor_scalar(a.bitcast(I32), e.bitcast(I32), 1, None, ALU.logical_shift_right))
            c(v.tensor_scalar(y.bitcast(I32), a.bitcast(I32), -1.0, float(0x5F3759DF), ALU.mult, ALU.add))
            for _ in range(3):
                c(v.tensor_tensor(a, y, y, ALU.mult))
                c(v.scalar_tensor_tensor(out=g, in0=a, scalar=-0.5, in1=e, op0=ALU.mult, op1=ALU.mult))
                c(v.scalar_tensor_tensor(out=y, in0=g, scalar=1.5, in1=y, op0=ALU.add, op1=ALU.mult))

        POOL_LINKS = 11

        def newton(v, c, n4):
            y, a, e, g = (n4[:, i] for i in range(4))
            for i in range(3):
                c(v.tensor_tensor(a, y, y, ALU.mult))
                c(v.tensor_tensor(g, a, e, ALU.mult))
                c(v.tensor_tensor(a, g, three_halves[:], ALU.add))
                if i < 2:
                    c(v.tensor_tensor(y, y, a, ALU.mult))

        def transpose_rows(pe, u, s, bank, xn_sig, xt_sig, tr_sig):
            pe.wait_ge(xn_sig.sem, xn_sig.upto(u))
            pe.wait_ge(xt_sig.sem, xt_sig.upto(u - 2))
            for k in range(KC):
                for j in range(2):
                    ins = pe.transpose(ps[:, bank, (2 * k + j) * P:(2 * k + j + 1) * P],
                                       xn[:, s, j, k * P:(k + 1) * P], ident[:])
            ins.then_inc(tr_sig.sem, 1)

        def xname(layer, what):
            return w[f"L{layer}_xattn_{what}"]

        X_LOADS = [16 * 19, 16 * 19 + 16 * 10]

        def sp_cross_weights(sp, layer):
            def ld(dst, src):
                sp.dma_start(dst, src).then_inc(x_ld, 16)

            for n in "qkvo":
                ld(xw[n][:], chunked(xname(layer, "W" + n)))
            ld(bq[:], xname(layer, "bq"))
            ld(bk[:], xname(layer, "bk"))
            ld(bv[:], xname(layer, "bv").partition_broadcast(P))
            ld(bo[:], xname(layer, "bo").partition_broadcast(P))
            ld(rw[:], chunked(w["L0_ffn_router_weight"] if layer == 0 else w["L1_ffn_gate_w"]))
            ld(rb[:], w["L1_ffn_gate_b"].partition_broadcast(P))
            if layer == 0:
                cv = ctxT.rearrange("(k p) (b s) -> p k b s", p=P, b=B)
                ld(ctxs[:], ctxT.rearrange("(k p) s -> p k s", p=P))
                for b in range(B):
                    for e in range(2):
                        ld(ctx2[:, b, :, e, :], cv[:, :, b, :])
                ld(woA[:], chunked(w["L0_attn_Wo"]))
                ld(hmask[:], w["c_hmask"])
                ld(halves[:], w["c_halves"])
                ld(mask_u8[:], mask0.rearrange("a b (t p) s -> p (a b t) s", p=P))
            else:
                sp.dma_start(mask1_u8[:], mask1.rearrange("b x y s -> (b x y s)").partition_broadcast(P))\
                  .then_inc(x_m1, 16)

        def sp_cross(sp, layer):
            if layer == 0:
                def rows_in(u, s):
                    sp.wait_ge(x_t[0].sem, x_t[0].upto(u - 2))
                    sp.dma_start((orow, orow2)[s][:], O_all[:, bass.ds(2 * u, 2), :]).then_inc(x_or[s].sem, 16)

                def mask_in(u, s):
                    sp.wait_ge(x_sm.sem, x_sm.upto(u - 2))
                    sp.dma_start(mslot[:, s, :, :], mask_no[:, bass.ds((2 * u) % TB, 2), :])\
                      .then_inc(x_ms[s].sem, 16)

                for step, enable in ((rows_in, None), (mask_in, x_mk)):
                    if enable is not None:
                        sp.wait_ge(enable, 1)
                    with sp.Fori(0, NP // 2) as i:
                        for s in range(2):
                            step(2 * i + s, s)

            with sp.Fori(0, NP // 2) as i:
                for s in range(2):
                    u = 2 * i + s
                    U = u + layer * NP
                    sp.wait_ge(x_lnB.sem, x_lnB.upto(U))
                    sp.wait_ge(x_xa.sem, x_xa.upto(U - 1))
                    sp.dma_start(O_all[:, bass.ds(2 * u, 2), :], xn[:, s, :, :]).then_inc(x_xa.sem, 16)
            sp.wait_ge(x_xa.sem, x_xa.upto(layer * NP + NP - 1))

        def steps(layer, body, eng, chain=None, links=0):
            body(-1, layer * NP - 1, 1, False, True, False)
            body(0, layer * NP, 0, True, True, False)
            loop = chain.fori(NP // 2 - 1, links) if chain else eng.Fori(0, NP // 2 - 1)
            with loop as i:
                for s in range(2):
                    u = 2 * i + 1 + s
                    body(u, u + layer * NP, 1 - s, True, True, True)
            body(NP - 1, layer * NP + NP - 1, 1, True, False, True)
            body(NP, layer * NP + NP, 0, False, False, True)

        def pairs(eng, layer, body):
            with eng.Fori(0, NP // 2) as i:
                for s in range(2):
                    body(2 * i + s, 2 * i + s + layer * NP, s)

        turn_bank, row_bank = (0, 5), (1, 6)
        by_chunk = lambda b: ps[:, b, :].rearrange("p (k q) -> p k q", k=KC)

        def act_cross(act, c, layer):
            def first_pass(u, U, s):
                act.wait_ge(x_t[0].sem, x_t[0].upto(U))
                act.wait_ge(x_oA.sem, x_oA.upto(U - 2))
                act.copy(oT[:, s, :, :], by_chunk(turn_bank[s])).then_inc(x_te[0].sem, 1)

            def last_pass(u, U, s):
                act.wait_ge(x_t[3].sem, x_t[3].upto(U))
                act.wait_ge(x_r.sem, x_r.upto(U - 2))
                act.copy(xT[:, s, :, :], by_chunk(turn_bank[s])).then_inc(x_te[3].sem, 1)

            def probs(U, j):
                act.wait_ge(x_sm.sem, x_sm.upto(U, j + 1))
                act.activation(pr[:, j, :, :], pr[:, j, :, :], ACT.Exp).then_inc(x_e.sem, 1)

            def probs_turned(U, j):
                act.wait_ge(x_pt.sem, x_pt.upto(U, j + 1))
                act.wait_ge(x_av.sem, x_av.upto(U, j))
                for q in range(2):
                    ins = act.copy(prT[:, 4 * q:4 * q + 4, :],
                                   ps[:, 5 + q, :].rearrange("p (g q) -> p g q", g=4))
                ins.then_inc(x_pe.sem, 1)

            def queries(U, s):
                act.wait_ge(x_q.sem, x_q.upto(U))
                for m in range(KC):
                    ins = act.activation(qT[:, s, m, :], ps[:, 2, m * 256:m * 256 + 256], ACT.Identity,
                                         bias=bq4[:, m:m + 1], scale=float(DH) ** -0.5)
                ins.then_inc(x_qe.sem, 1)

            def body(u, U, s, mid, first, end):
                if first:
                    act.wait_ge(x_t[1].sem, x_t[1].upto(U + 1))
                    act.wait_ge(x_q.sem, x_q.upto(U))
                    act.copy(xT[:, 0, :, :], by_chunk(0)).then_inc(x_te[1].sem, 1)
                if mid:
                    probs(U, 0)
                if first:
                    queries(U + 1, 1 - s)
                if mid:
                    probs_turned(U, 0)
                if end:
                    act.wait_ge(x_t[2].sem, x_t[2].upto(U - 1))
                    act.wait_ge(x_oB.sem, x_oB.upto(U - 2))
                    act.copy(oT[:, 0, :, :], by_chunk(0)).then_inc(x_te[2].sem, 1)
                if mid:
                    probs(U, 1)
                    probs_turned(U, 1)

            if layer == 0:
                pairs(act, layer, first_pass)
            act.wait_ge(x_cr.sem, x_cr.upto(layer))
            steps(layer, body, act)
            pairs(act, layer, last_pass)

        def dve_cross(v, c, layer):
            v.wait_ge(x_ld, X_LOADS[layer])
            c(v.tensor_scalar(bq4[:], bq[:], float(DH) ** -0.5, None, ALU.mult))
            if layer == 0:
                c(v.memset(fill0[:], -1000.0))
                v.tensor_scalar(mask_no[:], mask_u8[:], 0.0, None, ALU.is_equal).then_inc(x_mk, 1)
            else:
                v.wait_ge(x_m1, 16)
                c(v.tensor_scalar(mask1_f[:], mask1_u8[:], -1.0, 3e38, ALU.add, ALU.mult))
                c(v.tensor_scalar(mask1_f[:], mask1_f[:], 2.0, None, ALU.mult))
            v.wait_ge(x_ctx.sem, x_ctx.upto(layer, 1))
            for m in range(KC):
                c(v.tensor_scalar(kc[:, m, :], ps[:, 3, m * P:m * P + P], bk[:, m:m + 1], None, ALU.add))
            for b in range(B):
                for m in range(KC):
                    c(v.tensor_tensor(Kbd[:, b, m, :, :],
                                      kc[:, m, b * SC:b * SC + SC].unsqueeze(1).to_broadcast([P, HG, SC]),
                                      hmask[:].unsqueeze(2).to_broadcast([P, HG, SC]), ALU.mult))
            v.wait_ge(x_ctx.sem, x_ctx.upto(layer, 2))
            for b in range(B):
                c(v.tensor_tensor(vd[:, b, :], ps[:, 4, b * 256:b * 256 + 256], bv[:], ALU.add))
                for e in range(2):
                    c(v.tensor_scalar(Vbd[:, b, :, e, 0:DH],
                                      vd[:, b, :].rearrange("p (g e d) -> p g e d", g=HG, e=2)[:, :, e, :],
                                      halves[:, e:e + 1], None, ALU.mult))
                    c(v.tensor_copy(Vbd[:, b, :, e, DH:DH + 1],
                                    halves[:, e:e + 1].unsqueeze(1).to_broadcast([P, HG, 1])))
            v.memset(idle[:, 0:1], 0.0).then_inc(x_cr.sem, 1)
            v.wait_ge(x_cr.sem, x_cr.upto(layer))

            def first_pass(u, U, s):
                v.wait_ge(x_oA.sem, x_oA.upto(U))
                x2 = xr[:, bass.ds(2 * u, 2), :]
                v.tensor_tensor(x2, x2, ps[:, row_bank[s], :].rearrange("p (j d) -> p j d", j=2), ALU.add)\
                 .then_inc(x_res.sem, 1)
                v.wait_ge(x_res.sem, x_res.upto(U))
                v.memset(idle[:, 0:1], 0.0)
                row_stats(v, 2 * u, 2).then_inc(x_sta.sem, 1)
                v.wait_ge(x_sta.sem, x_sta.upto(U))

            def last_pass(u, U, s):
                v.wait_ge(x_xa.sem, x_xa.upto(U - 2))
                v.wait_ge(x_t[3].sem, x_t[3].upto(U - 2))
                for j in range(2):
                    ins = norm_rows(v, xn[:, s, j, :], 2 * u + j)
                ins.then_inc(x_lnB.sem, 1)

            def keep_logits(u, U, s):
                v.wait_ge(x_r.sem, x_r.upto(U))
                y = ps[:, (2, 7)[s], 0:2 * E].rearrange("p (j e) -> p j e", j=2)
                b = rb[:].unsqueeze(1) if layer else zeros[:, 0:1].unsqueeze(2)
                v.tensor_tensor(lg[:, bass.ds(2 * u, 2), :], y, b.to_broadcast([P, 2, E]), ALU.add)\
                 .then_inc(x_lg.sem, 1)

            S2 = ps[:, 3:5, :].rearrange("p m (h k) -> p (m h) k", h=HG)

            def softmax(u, U, j, s):
                v.wait_ge(x_s.sem, x_s.upto(U, j + 1))
                if layer == 0:
                    v.wait_ge(x_ms[s].sem, x_ms[s].upto(half_of(u)))
                    v.memset(idle[:, 0:1], 0.0)
                    c(v.copy_predicated(out=S2, mask=mslot[:, s, j:j + 1, :].to_broadcast([P, H, SC]),
                                        data=fill0[:].unsqueeze(2).to_broadcast([P, H, SC])))
                else:
                    c(v.tensor_tensor(S2, S2, mask1_f[:, bass.ds(u // 4, 1), :].to_broadcast([P, H, SC]),
                                      ALU.add))
                c(v.tensor_reduce(mxx[:, j, :], S2, AX.X, ALU.max))
                v.wait_ge(x_pt.sem, x_pt.upto(U - 1, j + 1))
                v.tensor_tensor(pr[:, j, :, :], S2, mxx[:, j, :].unsqueeze(2).to_broadcast([P, H, SC]),
                                ALU.subtract).then_inc(x_sm.sem, 1)

            def outputs(U, j):
                v.wait_ge(x_av.sem, x_av.upto(U, j + 1))
                y = ps[:, 7, 0:H * (DH + 1)].rearrange("p (h d) -> p h d", h=H)
                c(v.reciprocal(recx[:].unsqueeze(2), y[:, :, DH:DH + 1]))
                v.wait_ge(x_t[2].sem, x_t[2].upto(U - 1))
                v.tensor_tensor(orow2[:, j, :].rearrange("p (h d) -> p h d", h=H), y[:, :, 0:DH],
                                recx[:].unsqueeze(2).to_broadcast([P, H, DH]), ALU.mult)\
                 .then_inc(x_no.sem, 1)

            def residual(u, U):
                v.wait_ge(x_oB.sem, x_oB.upto(U))
                x2 = xr[:, bass.ds(2 * u, 2), :]
                c(v.tensor_tensor(x2, x2, bo[:].unsqueeze(1).to_broadcast([P, 2, D]), ALU.add))
                v.tensor_tensor(x2, x2, ps[:, 1, :].rearrange("p (j d) -> p j d", j=2), ALU.add)\
                 .then_inc(x_rb.sem, 1)
                v.wait_ge(x_rb.sem, x_rb.upto(U))
                v.memset(idle[:, 0:1], 0.0)
                c(row_stats(v, 2 * u, 2))

            def body(u, U, s, mid, first, end):
                if first:
                    v.wait_ge(x_t[1].sem, x_t[1].upto(U))
                    for j in range(2):
                        ins = norm_rows(v, xn[:, 0, j, :], 2 * (u + 1) + j)
                    ins.then_inc(x_lnA.sem, 1)
                if mid:
                    softmax(u, U, 0, s)
                if end:
                    outputs(U - 1, 1)
                if mid:
                    softmax(u, U, 1, s)
                if end:
                    residual(u - 1, U - 1)
                if mid:
                    outputs(U, 0)

            if layer == 0:
                pairs(v, layer, first_pass)
            norm_factors(v, c)
            steps(layer, body, v, c, X_LINKS[layer])
            norm_factors(v, c)
            last_pass(0, layer * NP, 0)
            with v.Fori(0, NP // 2 - 1) as i:
                for s in range(2):
                    last_pass(2 * i + s + 1, 2 * i + s + 1 + layer * NP, 1 - s)
                    keep_logits(2 * i + s, 2 * i + s + layer * NP, s)
            last_pass(NP - 1, layer * NP + NP - 1, 1)
            for s in range(2):
                keep_logits(NP - 2 + s, layer * NP + NP - 2 + s, s)

        X_LINKS = [16, 16]

        def pe_cross(pe, layer):
            pe.wait_ge(x_ld, X_LOADS[layer])
            for m in range(KC):
                for k in range(KC):
                    ins = pe.matmul(ps[:, 3, m * P:m * P + P], xw["k"][:, k, m * P:m * P + P], ctxs[:, k, :],
                                    start=(k == 0), stop=(k == KC - 1))
            ins.then_inc(x_ctx.sem, 1)
            for b in range(B):
                for k in range(KC):
                    ins = pe.matmul(ps[:, 4, b * 256:b * 256 + 256],
                                    ctx2[:, b, k, :, :].rearrange("p e s -> p (e s)"), xw["v"][:, k, :],
                                    start=(k == 0), stop=(k == KC - 1))
            ins.then_inc(x_ctx.sem, 1)
            def turn(r, U, rows, bank):
                for k in range(KC):
                    for j in range(2):
                        ins = pe.transpose(ps[:, bank, (2 * k + j) * P:(2 * k + j + 1) * P],
                                           rows[:, j, k * P:(k + 1) * P], ident[:])
                ins.then_inc(x_t[r].sem, 1)

            def out_rows(oT_, wo, bank, done):
                for j in range(2):
                    for k in range(KC):
                        ins = pe.matmul(ps[:, bank, j * 256:j * 256 + 256], oT_[:, k, j * P:j * P + P], wo[:, k, :],
                                        start=(k == 0), stop=(k == KC - 1))
                ins.then_inc(done.sem, 1)

            def turn_first(U, s):
                pe.wait_ge(x_or[s].sem, x_or[s].upto(half_of(U)))
                pe.wait_ge(x_te[0].sem, x_te[0].upto(U - 2))
                turn(0, U, (orow, orow2)[s], turn_bank[s])

            def project_first(U, s):
                pe.wait_ge(x_te[0].sem, x_te[0].upto(U))
                pe.wait_ge(x_res.sem, x_res.upto(U - 2))
                out_rows(oT[:, s, :, :], woA, row_bank[s], x_oA)

            def turn_last(U, s):
                pe.wait_ge(x_lnB.sem, x_lnB.upto(U))
                pe.wait_ge(x_te[3].sem, x_te[3].upto(U - 2))
                turn(3, U, xn[:, s, :, :], turn_bank[s])

            def logits(U, s):
                pe.wait_ge(x_te[3].sem, x_te[3].upto(U))
                pe.wait_ge(x_lg.sem, x_lg.upto(U - 2))
                for j in range(2):
                    for k in range(KC):
                        ins = pe.matmul(ps[:, (2, 7)[s], j * E:j * E + E], xT[:, s, k, j * P:j * P + P], rw[:, k, :],
                                        start=(k == 0), stop=(k == KC - 1))
                ins.then_inc(x_r.sem, 1)

            def two_stages(a, b):
                U0 = layer * NP
                a(U0, 0)
                with pe.Fori(0, NP // 2 - 1) as i:
                    for s in range(2):
                        a(2 * i + U0 + s + 1, 1 - s)
                        b(2 * i + U0 + s, s)
                a(U0 + NP - 1, 1)
                b(U0 + NP - 2, 0)
                b(U0 + NP - 1, 1)

            def queries(U):
                pe.wait_ge(x_te[1].sem, x_te[1].upto(U))
                pe.wait_ge(x_qe.sem, x_qe.upto(U - 1))
                for m in range(KC):
                    for k in range(KC):
                        ins = pe.matmul(ps[:, 2, m * 256:m * 256 + 256], xw["q"][:, k, m * P:m * P + P],
                                        xT[:, 0, k, :], start=(k == 0), stop=(k == KC - 1))
                ins.then_inc(x_q.sem, 1)

            def scores(u, U, j, s):
                if j == 0:
                    pe.wait_ge(x_qe.sem, x_qe.upto(U))
                pe.wait_ge(x_sm.sem, x_sm.upto(U, j))
                for m in range(KC):
                    b = u // 4
                    ins = pe.matmul(ps[:, 3 + m, :], qT[:, s, m, j * P:j * P + P],
                                    Kbd[:, bass.ds(b, 1), m, :, :].rearrange("p b h k -> p (b h k)"),
                                    start=True, stop=True)
                ins.then_inc(x_s.sem, 1)

            def turn_probs(U, j):
                pe.wait_ge(x_e.sem, x_e.upto(U, j + 1))
                pe.wait_ge(x_pe.sem, x_pe.upto(U, j))
                for g in range(HG):
                    ins = pe.transpose(ps[:, 5 + g // 4, (g % 4) * P:(g % 4) * P + P],
                                       pr[:, j, 2 * g:2 * g + 2, :].rearrange("p e k -> p (e k)"), ident[:])
                ins.then_inc(x_pt.sem, 1)

            def weigh(u, U, j):
                pe.wait_ge(x_pe.sem, x_pe.upto(U, j + 1))
                pe.wait_ge(x_no.sem, x_no.upto(U, j))
                n = 2 * (DH + 1)
                for g in range(HG):
                    ins = pe.matmul(ps[:, 7, g * n:g * n + n], prT[:, g, :],
                                    Vbd[:, bass.ds(u // 4, 1), g, :, :].rearrange("p b e d -> p (b e d)"),
                                    start=True, stop=True)
                ins.then_inc(x_av.sem, 1)

            def body(u, U, s, mid, first, end):
                if mid:
                    scores(u, U, 0, s)
                if end:
                    weigh(u - 1, U - 1, 1)
                if first:
                    pe.wait_ge(x_lnA.sem, x_lnA.upto(U + 1))
                    pe.wait_ge(x_te[2].sem, x_te[2].upto(U - 2))
                    turn(1, U + 1, xn[:, 0, :, :], 0)
                    queries(U + 1)
                if mid:
                    scores(u, U, 1, s)
                    turn_probs(U, 0)
                if end:
                    pe.wait_ge(x_no.sem, x_no.upto(U - 1))
                    if first:
                        pe.wait_ge(x_te[1].sem, x_te[1].upto(U + 1))
                    else:
                        pe.wait_ge(x_te[2].sem, x_te[2].upto(U - 2))
                    turn(2, U - 1, orow2, 0)
                if mid:
                    weigh(u, U, 0)
                if end:
                    pe.wait_ge(x_te[2].sem, x_te[2].upto(U - 1))
                    pe.wait_ge(x_rb.sem, x_rb.upto(U - 2))
                    out_rows(oT[:, 0, :, :], xw["o"], 1, x_oB)
                if mid:
                    turn_probs(U, 1)

            if layer == 0:
                two_stages(turn_first, project_first)
            pe.wait_ge(x_cr.sem, x_cr.upto(layer))
            steps(layer, body, pe)
            two_stages(turn_last, logits)

        def half_of(u):
            return u // 2

        def dve_top2(v, c, layer):
            bc = lambda m: m.unsqueeze(2).to_broadcast([P, NT, E])
            t2 = lambda q: tk[:, q, :]
            c(v.tensor_reduce(t2(0), lg[:], AX.X, ALU.max))
            v.tensor_tensor(pe_[:], lg[:], bc(t2(0)), ALU.subtract).then_inc(r_sub, 1)
            v.wait_ge(r_exp, layer + 1)
            c(v.tensor_reduce(t2(0), pe_[:], AX.X, ALU.add))
            c(v.reciprocal(t2(1), t2(0)))
            c(v.tensor_tensor(pb[:], pe_[:], bc(t2(1)), ALU.mult))
            for k in range(2):
                c(v.tensor_reduce(top[k][:], pb[:], AX.X, ALU.max))
                c(v.tensor_tensor(tm[:], pb[:], bc(top[k][:]), ALU.is_equal))
                c(v.tensor_tensor(tm[:], tm[:], desc[:].unsqueeze(1).to_broadcast([P, NT, E]), ALU.mult))
                c(v.tensor_reduce(t2(2), tm[:], AX.X, ALU.max))
                c(v.tensor_tensor(oh[k][:], tm[:], bc(t2(2)), ALU.is_equal))
                if k == 0:
                    c(v.scalar_tensor_tensor(out=pb[:], in0=oh[0][:], scalar=-2.0, in1=pb[:],
                                             op0=ALU.mult, op1=ALU.add))
            c(v.tensor_tensor(t2(0), top[0][:], top[1][:], ALU.add))
            if layer == 0:
                c(v.tensor_scalar(t2(0), t2(0), EPS, None, ALU.max))
            c(v.reciprocal(t2(1), t2(0)))
            for k in range(2):
                c(v.tensor_tensor(gw[k][:], top[k][:], t2(1), ALU.mult))

        def over_experts(v, c, out_, a, b):
            c(v.tensor_tensor(tm[:], a, b, ALU.mult))
            c(v.tensor_reduce(out_, tm[:], AX.X, ALU.add))

        flat = lambda m: m[:].rearrange("p t e -> p (t e)")
        RS = [0]

        def dve_sum(v, ins):
            ins.then_inc(r_rhs, 1)
            RS[0] += 1
            v.wait_ge(r_sum, RS[0])

        def dve_route0(v, c):
            bc = lambda m: m.unsqueeze(2).to_broadcast([P, NT, E])
            be = lambda m: m.unsqueeze(1).to_broadcast([P, NT, E])
            dve_top2(v, c, 0)
            c(v.tensor_tensor(Wt[:], oh[0][:], bc(gw[0][:]), ALU.mult))
            c(v.tensor_tensor(tm[:], oh[1][:], bc(gw[1][:]), ALU.mult))
            c(v.tensor_tensor(Wt[:], Wt[:], tm[:], ALU.add))
            c(v.tensor_tensor(Kp[:], oh[0][:], oh[1][:], ALU.add))
            c(v.tensor_tensor(Ct[:], Wt[:], Kp[:], ALU.add))
            c(v.tensor_scalar(Ct[:], Ct[:], -1.0, None, ALU.add))
            c(v.memset(thr[:], 0))
            with c.fori(BITS, 4) as i:
                c(v.tensor_tensor(cand[:].unsqueeze(1), thr[:].unsqueeze(1), bits[:, bass.ds(i, 1), :],
                                  ALU.bitwise_or))
                c(v.tensor_tensor(tm[:], Ct[:], be(cand[:].bitcast(F32)), ALU.is_ge))
                with nc.allow_low_precision(reason="counts up to 16 are exact"):
                    ins = v.tensor_reduce(c8b[:], tm[:].rearrange("p t e -> p e t"), AX.X, ALU.add)
                ins.then_inc(r_rhs, 1)
                v.wait_ge(r_sum, i + 1)
                c(v.scalar_tensor_tensor(out=c8[:], in0=ps[:, 0, 0:E], scalar=CAP - 0.5,
                                         in1=cand[:].bitcast(F32), op0=ALU.is_ge, op1=ALU.mult))
                c(v.tensor_tensor(thr[:].bitcast(F32), thr[:].bitcast(F32), c8[:], ALU.max))
            RS[0] += BITS
            T8 = be(thr[:].bitcast(F32))
            c(v.tensor_tensor(Kp[:], Ct[:], T8, ALU.is_gt))
            with nc.allow_low_precision(reason="counts up to 16 are exact"):
                ins = v.tensor_reduce(c8b[:], Kp[:].rearrange("p t e -> p e t"), AX.X, ALU.add)
            dve_sum(v, ins)
            c(v.tensor_scalar(c8[:], ps[:, 0, 0:E], -1.0, float(CAP), ALU.mult, ALU.add))
            c(v.tensor_tensor(pb[:], Ct[:], T8, ALU.is_equal))
            dve_sum(v, v.tensor_copy(tb[:], pb[:]))
            y = ps[:, 0, 0:NT * E].rearrange("p (t e) -> p t e", t=NT)
            c(v.tensor_tensor(tm[:], y, be(c8[:]), ALU.is_lt))
            c(v.tensor_tensor(tm[:], tm[:], pb[:], ALU.mult))
            c(v.tensor_tensor(Kp[:], Kp[:], tm[:], ALU.add))
            dve_sum(v, v.tensor_copy(tb[:], Kp[:]))
            c(v.tensor_tensor(Ct[:], y, be(first[:]), ALU.add))
            c(v.tensor_tensor(Wt[:], Wt[:], Kp[:], ALU.mult))
            c(v.tensor_reduce(tk[:, 0, :], Wt[:], AX.X, ALU.add))
            c(v.tensor_scalar(tk[:, 0, :], tk[:, 0, :], EPS, None, ALU.max))
            c(v.reciprocal(tk[:, 1, :], tk[:, 0, :]))
            c(v.tensor_tensor(Wt[:], Wt[:], bc(tk[:, 1, :]), ALU.mult))
            for k in range(2):
                over_experts(v, c, gw[k][:], Wt[:], oh[k][:])
                over_experts(v, c, tk[:, 2, :], Kp[:], oh[k][:])
                over_experts(v, c, tk[:, 3, :], Ct[:], oh[k][:])
                c(v.tensor_scalar(tk[:, 4, :], tk[:, 2, :], -nochoice, nochoice, ALU.mult, ALU.add))
                c(v.tensor_tensor(tk[:, 5, :], tk[:, 3, :], tk[:, 4, :], ALU.add))
                c(v.tensor_copy(idxS[k][:], tk[:, 5, :]))
                c(v.tensor_tensor(tk[:, 6, :], tk[:, 3, :], tk[:, 2, :], ALU.mult))
                c(v.tensor_copy(idxG[k][:], tk[:, 6, :]))
            v.memset(idle[:], 0.0).then_inc(r_idx, 1)

        def pe_count(pe, n):
            pe.wait_ge(r_rhs, n)
            pe.matmul(ps[:, 0, 0:E], onesb[:], c8b[:], start=True, stop=True).then_inc(r_sum, 1)

        def pe_before(pe, n):
            pe.wait_ge(r_rhs, n)
            w_ = NT * E
            pe.matmul(ps[:, 0, 0:w_], lower[:], flat(tb), start=True, stop=False)
            for t in range(1, NT):
                ins = pe.matmul(ps[:, 0, t * E:w_], onesb[:], flat(tb)[:, 0:w_ - t * E], start=False,
                                stop=(t == NT - 1))
            ins.then_inc(r_sum, 1)

        def pe_route0(pe):
            with pe.Fori(1, BITS + 1) as i:
                pe_count(pe, i)
            pe_count(pe, BITS + 1)
            pe_before(pe, BITS + 2)
            pe_before(pe, BITS + 3)

        def pool_scatter(pool, c, layer, xs, rows):
            pool.wait_ge(r_idx, layer + 1)
            pool.wait_ge(g_z, 32)
            for t in range(NT):
                for k in range(2):
                    pool.indirect_dma_start(
                        out=xs, out_offset=bass.IndirectOffsetOnAxis(ap=idxS[k][:, t:t + 1], axis=0),
                        in_=O_all[:, t, :], in_offset=None, bounds_check=rows - 1, oob_is_err=False,
                    ).then_inc(g_sc[layer], 16)

        def pool_gather(pool, c, layer, ys, rows, ready):
            for s_, val in ready:
                pool.wait_ge(s_, val)
            for t in range(NT):
                if t >= 4:
                    pool.wait_ge(g_use, layer * NT + t - 3)
                for k in range(2):
                    pool.indirect_dma_start(
                        out=(yg, yg1)[layer][:, t % 4, k, :], out_offset=None, in_=ys,
                        in_offset=bass.IndirectOffsetOnAxis(ap=idxG[k][:, t:t + 1], axis=0),
                        bounds_check=rows - 1, oob_is_err=False,
                    ).then_inc(g_ld[t % 4], 16)

        def dve_combine(v, c, layer):
            for t in range(NT):
                v.wait_ge(g_ld[t % 4], (layer * 4 + t // 4 + 1) * 32)
                c(v.scalar_tensor_tensor(out=xr[:, t, :], in0=(yg, yg1)[layer][:, t % 4, 0, :], scalar=gw[0][:, t:t + 1],
                                         in1=xr[:, t, :], op0=ALU.mult, op1=ALU.add))
                v.scalar_tensor_tensor(out=xr[:, t, :], in0=(yg, yg1)[layer][:, t % 4, 1, :], scalar=gw[1][:, t:t + 1],
                                       in1=xr[:, t, :], op0=ALU.mult, op1=ALU.add).then_inc(g_use, 1)
                if layer == 0:
                    v.wait_ge(g_use, t + 1)
                    v.memset(idle[:, 0:1], 0.0)
                    c(v.bn_stats(stats[:, t, :], xr[:, t, :]))

        WE = 3 * KC * F
        gate_w = lambda s: wide[:, s * WE:s * WE + KC * F].rearrange("p (k f) -> p k f", k=KC)
        pre_w = lambda s: wide[:, s * WE + KC * F:s * WE + 2 * KC * F].rearrange("p (k f) -> p k f", k=KC)
        post_w = lambda s: wide[:, s * WE + 2 * KC * F:(s + 1) * WE].rearrange("p (g d) -> p g d", d=D)
        HC = CAP // 2

        def sp_weights0(sp, e, s, which=range(3)):
            sp.wait_ge(f_y.sem, f_y.upto(e - 2))
            pieces = ((gate_w(s), w["L0_ffn_gate_weight"]), (pre_w(s), w["L0_ffn_ff_pre_act_weight"]),
                      (post_w(s), w["L0_ffn_ff_post_act_weight"]))
            for q in which:
                dst, src = pieces[q]
                sp.dma_start(dst, src[bass.ds(e, 1), :, :].rearrange("e (k p) n -> p (e k) n", p=P))\
                  .then_inc(f_w[s].sem, 16)

        def sp_experts0(sp):
            sp.wait_ge(g_sc[0], 2 * NT * 16)

            def rows_in(e, s):
                sp.wait_ge(f_t.sem, f_t.upto(e - 2))
                sp.dma_start(xe[:, s, :, :], xs0[bass.ds(e * CAP, CAP), :].rearrange("(r p) d -> p r d", p=P))\
                  .then_inc(f_x[s].sem, 16)

            def rows_out(e):
                sp.wait_ge(f_ye.sem, f_ye.upto(e))
                sp.dma_start(ys0[bass.ds(e * CAP, CAP), :].rearrange("(r p) d -> p r d", p=P), yrow)\
                  .then_inc(f_ys.sem, 16)

            rows_in(0, 0)
            rows_in(1, 1)
            with sp.Fori(1, E // 2) as i:
                for s in range(2):
                    rows_out(2 * i + s - 2)
                    sp_weights0(sp, 2 * i + s, s)
                    rows_in(2 * i + s, s)
            rows_out(E - 2)
            rows_out(E - 1)

        def pe_experts0(pe):
            def turn(e, s):
                pe.wait_ge(f_x[s].sem, f_x[s].upto(e // 2))
                pe.wait_ge(f_te.sem, f_te.upto(e - 1))
                for k in range(KC):
                    for r in range(5):
                        o = ps[:, k, r * P:r * P + P] if r < 4 else ps[:, 2, k * P:k * P + P]
                        ins = pe.transpose(o, xe[:, s, r, k * P:k * P + P], ident[:])
                ins.then_inc(f_t.sem, 1)

            def hidden(e, s):
                pe.wait_ge(f_w[s].sem, f_w[s].upto(e // 2))
                pe.wait_ge(f_te.sem, f_te.upto(e))
                for q in range(16):
                    hf, f = q // 8, q % 8
                    pe.wait_ge(f_m.sem, f_m.upto(e, q - 1))
                    if q == 1:
                        pe.wait_ge(f_ye.sem, f_ye.upto(e - 1))
                    for n, wt in enumerate((gate_w(s), pre_w(s))):
                        for k in range(KC):
                            ins = pe.matmul(ps[:, 3 + 2 * (q % 2) + n, 0:HC], wt[:, k, f * P:f * P + P],
                                            xTe[:, k, hf * HC:hf * HC + HC], start=(k == 0), stop=(k == KC - 1))
                    ins.then_inc(f_h.sem, 1)

            def output(e, s, r):
                pe.wait_ge(f_m.sem, f_m.upto(e))
                pe.wait_ge(f_ye.sem, f_ye.upto(e, r - 1))
                for g in range(F // P):
                    ins = pe.matmul(ps[:, 7 - r % 2, 0:D], hTe[:, g, r * P:r * P + P], post_w(s)[:, g, :],
                                    start=(g == 0), stop=(g == F // P - 1))
                ins.then_inc(f_y.sem, 1)

            def expert(e, s, last=False):
                hidden(e, s)
                for r in range(5):
                    output(e, s, r)
                    if r == 2 and not last:
                        turn(e + 1, 1 - s)

            turn(0, 0)
            with pe.Fori(0, E // 2 - 1) as i:
                for s in range(2):
                    expert(2 * i + s, s)
            expert(E - 2, 0)
            expert(E - 1, 1, True)

        def act_experts0(act):
            with act.Fori(0, E // 2) as i:
                for s in range(2):
                    e = 2 * i + s
                    act.wait_ge(f_t.sem, f_t.upto(e))
                    for k in range(KC):
                        act.copy(xTe[:, k, 0:512], ps[:, k, :]).then_inc(f_te.sem, 1)
                    act.copy(xTe[:, :, 512:CAP], ps[:, 2, 0:256].rearrange("p (k q) -> p k q", k=KC))\
                       .then_inc(f_te.sem, 1)
                    for q in range(16):
                        act.wait_ge(f_h.sem, f_h.upto(e, q + 1))
                        act.wait_ge(f_m.sem, f_m.upto(e, q - 1))
                        act.activation(sgt[:, q % 2, :], ps[:, 3 + 2 * (q % 2), 0:HC], ACT.Silu)\
                           .then_inc(f_a.sem, 1)

        def dve_experts0(v, c):
            with c.fori(E // 2, 0) as i:
                for s in range(2):
                    e = 2 * i + s
                    for q in range(16):
                        hf, f = q // 8, q % 8
                        v.wait_ge(f_a.sem, f_a.upto(e, q + 1))
                        v.tensor_tensor(hTe[:, f, hf * HC:hf * HC + HC], sgt[:, q % 2, :],
                                        ps[:, 4 + 2 * (q % 2), 0:HC], ALU.mult).then_inc(f_m.sem, 1)
                    for r in range(5):
                        v.wait_ge(f_y.sem, f_y.upto(e, r + 1))
                        if r == 0:
                            v.wait_ge(f_ys.sem, f_ys.upto(e - 1))
                        v.tensor_copy(yrow[:, r, :], ps[:, 7 - r % 2, 0:D]).then_inc(f_ye.sem, 1)

        def dve_route1(v, c):
            be = lambda m: m.unsqueeze(1).to_broadcast([P, NT, E])
            dve_top2(v, c, 1)
            c(v.tensor_tensor(Kp[:], oh[0][:], oh[1][:], ALU.add))
            with nc.allow_low_precision(reason="counts up to 16 are exact"):
                ins = v.tensor_reduce(c8b[:], Kp[:].rearrange("p t e -> p e t"), AX.X, ALU.add)
            dve_sum(v, ins)
            c(v.tensor_scalar(n8[:], ps[:, 0, 0:E], float(P - 1), None, ALU.add))
            c(v.tensor_copy(n8i[:], n8[:]))
            c(v.tensor_scalar(n8i[:], n8i[:], 7, None, ALU.logical_shift_right))
            c(v.tensor_copy(n8[:], n8i[:]))
            c(v.tensor_tensor(m3[:], before_e[:], n8[:].unsqueeze(1).to_broadcast([P, E, E]), ALU.mult))
            c(v.tensor_reduce(base8[:], m3[:], AX.X, ALU.add))
            c(v.tensor_tensor(n8[:], base8[:], n8[:], ALU.add))
            c(v.tensor_scalar(base8[:], base8[:], float(P), None, ALU.mult))
            dve_sum(v, v.tensor_copy(tb[:], Kp[:]))
            y = ps[:, 0, 0:NT * E].rearrange("p (t e) -> p t e", t=NT)
            c(v.tensor_tensor(Ct[:], y, be(base8[:]), ALU.add))
            for k in range(2):
                over_experts(v, c, tk[:, 3, :], Ct[:], oh[k][:])
                c(v.tensor_copy(idxS[k][:], tk[:, 3, :]))
                c(v.tensor_copy(idxG[k][:], tk[:, 3, :]))
            c(v.tensor_tensor(ex[:], n8[:].unsqueeze(1).to_broadcast([P, NX, E]),
                              tile_no[:].unsqueeze(2).to_broadcast([P, NX, E]), ALU.is_le))
            c(v.tensor_reduce(exf[:], ex[:], AX.X, ALU.add))
            c(v.tensor_scalar(exf[:], exf[:], float(E - 1), None, ALU.min))
            c(v.tensor_copy(exi[:], exf[:]))
            v.memset(idle[:], 0.0).then_inc(r_idx, 1)

        w1s = wide[:].rearrange("p (e k f) -> p e k f", e=E, k=KC)

        def sp_experts1(sp):
            sp.dma_start(w2s[:].rearrange("p e g d -> p (e g) d"),
                         w["L1_ffn_w2"].rearrange("e (g p) d -> p (e g) d", p=P)).then_inc(m_w2, 16)
            sp.dma_start(b1s[:], w["L1_ffn_b1"]).then_inc(m_w2, 16)
            sp.dma_start(b2s[:], w["L1_ffn_b2"].partition_broadcast(P)).then_inc(m_w2, 16)
            sp.wait_ge(g_sc[1], 2 * NT * 16)

            def rows_in(j, s):
                sp.wait_ge(m_t.sem, m_t.upto(j - 2))
                sp.dma_start(rows1[:, s, :], xs1[bass.ds(j * P, P), :]).then_inc(m_x[s].sem, 16)

            def rows_out(j, s):
                sp.wait_ge(m_yc.sem, m_yc.upto(j))
                sp.dma_start(ys1[bass.ds(j * P, P), :], yrow1[:, s, :]).then_inc(m_st[s].sem, 16)

            rows_in(0, 0)
            rows_in(1, 1)
            with sp.Fori(1, NX // 2) as i:
                for s in range(2):
                    rows_in(2 * i + s, s)
                    rows_out(2 * i + s - 2, s)
            for s in range(2):
                rows_out(NX - 2 + s, s)

        def steps1(body, eng):
            body(-2, 0, False, False, True)
            body(-1, 1, False, True, True)
            with eng.Fori(0, NX // 2 - 1) as i:
                for s in range(2):
                    body(2 * i + s, s, True, True, True)
            body(NX - 2, 0, True, True, False)
            body(NX - 1, 1, True, False, False)

        def expert_of(eng, j):
            return eng.value_load(exi[0:1, bass.ds(j, 1)], min_val=0, max_val=E - 1)

        def pe_experts1(pe):
            def body(j, s, out_, hid, turn):
                if out_:
                    for q in range(2):
                        pe.wait_ge(m_hc.sem, m_hc.upto(j, q + 1))
                        pe.wait_ge(m_a.sem, m_a.upto(j - 1, q + 1))
                        for g in range(4):
                            ins = pe.transpose(ps[:, 3 + q, g * P:g * P + P], hrow[:, q, g * P:g * P + P], ident[:])
                        ins.then_inc(m_ht.sem, 1)
                if hid:
                    pe.wait_ge(m_tc.sem, m_tc.upto(j + 1))
                    e = expert_of(pe, j + 1)
                    for q in range(2):
                        pe.wait_ge(m_hc.sem, m_hc.upto(j, q + 1))
                        for k in range(KC):
                            ins = pe.matmul(ps[:, 1 + q, :], xTm[:, 1 - s, k, :],
                                            w1s[:, bass.ds(e, 1), k, q * 512:q * 512 + 512]
                                            .rearrange("p e f -> p (e f)"),
                                            start=(k == 0), stop=(k == KC - 1))
                        ins.then_inc(m_h.sem, 1)
                if turn:
                    pe.wait_ge(m_x[s].sem, m_x[s].upto(half_of(j + 2)))
                    pe.wait_ge(m_tc.sem, m_tc.upto(j + 1))
                    for k in range(KC):
                        ins = pe.transpose(ps[:, 0, k * P:k * P + P], rows1[:, s, k * P:k * P + P], ident[:])
                    ins.then_inc(m_t.sem, 1)
                if out_:
                    e = expert_of(pe, j)
                    pe.wait_ge(m_yc.sem, m_yc.upto(j - 2))
                    for g in range(F // P):
                        if g % 4 == 0:
                            pe.wait_ge(m_a.sem, m_a.upto(j, g // 4 + 1))
                        ins = pe.matmul(ps[:, 5 + s, 0:D], hTm[:, g, :],
                                        w2s[:, bass.ds(e, 1), g, :].rearrange("p e d -> p (e d)"),
                                        start=(g == 0), stop=(g == F // P - 1))
                    ins.then_inc(m_y.sem, 1)

            pe.wait_ge(r_idx, 2)
            pe.wait_ge(m_w, 16)
            pe.wait_ge(m_w2, 48)
            steps1(body, pe)

        def act_experts1(act):
            def body(j, s, out_, hid, turn):
                if hid:
                    for q in range(2):
                        act.wait_ge(m_h.sem, m_h.upto(j + 1, q + 1))
                        act.wait_ge(m_ht.sem, m_ht.upto(j, q + 1))
                        act.copy(hrow[:, q, :], ps[:, 1 + q, :]).then_inc(m_hc.sem, 1)
                if turn:
                    act.wait_ge(m_t.sem, m_t.upto(j + 2))
                    act.wait_ge(m_h.sem, m_h.upto(j))
                    act.copy(xTm[:, s, :, :], ps[:, 0, 0:2 * P].rearrange("p (k q) -> p k q", k=KC))\
                       .then_inc(m_tc.sem, 1)

            steps1(body, act)

        def dve_experts1(v, c):
            def body(j, s):
                e = expert_of(v, j)
                for q in range(2):
                    v.wait_ge(m_ht.sem, m_ht.upto(j, q + 1))
                    v.wait_ge(m_y.sem, m_y.upto(j - 1))
                    h3 = hTm[:, 4 * q:4 * q + 4, :]
                    b = b1s[:, bass.ds(e, 1), 4 * q:4 * q + 4].rearrange("p e g -> p (e g)")
                    c(v.tensor_tensor(h3, ps[:, 3 + q, :].rearrange("p (g t) -> p g t", g=4),
                                      b.unsqueeze(2).to_broadcast([P, 4, P]), ALU.add))
                    v.tensor_scalar(h3, h3, 0.0, None, ALU.max).then_inc(m_a.sem, 1)
                v.wait_ge(m_y.sem, m_y.upto(j))
                v.wait_ge(m_st[s].sem, m_st[s].upto(half_of(j) - 1))
                v.tensor_tensor(yrow1[:, s, :], ps[:, 5 + s, 0:D],
                                b2s[:, bass.ds(e, 1), :].rearrange("p e d -> p (e d)"), ALU.add)\
                 .then_inc(m_yc.sem, 1)

            v.wait_ge(m_w2, 48)
            with c.fori(NX // 2, 4) as i:
                for s in range(2):
                    body(2 * i + s, s)

        def sp_retention(sp):
            for dst, src in ((wqk[:, :, 0:D], chunked(w["L1_attn_WQ"])), (wqk[:, :, D:2 * D], chunked(w["L1_attn_WK"])),
                             (wvR[:], chunked(w["L1_attn_WV"])), (woR[:], chunked(w["L1_attn_WO"])),
                             (turns[:], w["c_turns"]), (decay[:], w["c_decay"]), (causal[:], w["c_causal"]),
                             (bdg[:], w["c_bdg"]), (gP[:], w["c_gP"]), (keepS[:], w["c_keep"]),
                             (gamma[:], w["L1_attn_gamma"]), (beta[:], w["L1_attn_beta"])):
                sp.dma_start(dst, src).then_inc(e_ld, 16)

        def steps_r(body, eng, chain=None, links=0):
            body(-2, 0, False, False, False, False, True)
            body(-1, 1, False, True, False, False, True)
            body(0, 0, True, True, False, False, True)
            body(1, 1, True, True, True, False, True)
            loop = chain.fori(NT // 2 - 2, links) if chain else eng.Fori(0, NT // 2 - 2)
            with loop as i:
                for s in range(2):
                    body(2 * i + 2 + s, s, True, True, True, True, True)
            body(NT - 2, 0, True, True, True, True, False)
            body(NT - 1, 1, True, False, True, True, False)
            body(NT, 0, False, False, True, True, False)
            body(NT + 1, 1, False, False, False, True, False)

        E_LOADS = 12 * 16
        E_LINKS = 24

        def pe_retention(pe):
            def body(t, s, mid, first, end, res, pre):
                def scores(g):
                    m = g // 2
                    src = (e_ex, e_ex1)[m]
                    pe.wait_ge(src.sem, src.upto(t))
                    pe.wait_ge(e_m.sem, e_m.upto(t, g - 1))
                    pe.matmul(ps[:, 3 + g % 2, :], qkT[:, KC + m, :],
                              qbd[:, m, 4 * (g % 2):4 * (g % 2) + 4, :].rearrange("p h q -> p (h q)"),
                              start=True, stop=True).then_inc(e_s.sem, 1)

                def weigh(g):
                    pe.wait_ge(e_m.sem, e_m.upto(t, g + 1))
                    for h in range(4):
                        d = (4 * g + h) * DH
                        ins = pe.matmul(ps[:, 5, d:d + DH], wS[:, g % 2, h, :], vR[:, s, d:d + DH],
                                        start=False, stop=(g == 3 and h == 3))
                    ins.then_inc(e_av.sem, 1)

                if mid:
                    scores(0)
                    scores(1)
                if first:
                    pe.wait_ge(e_xt.sem, e_xt.upto(t + 1))
                    pe.wait_ge(e_rot.sem, e_rot.upto(t))
                    for wt, bank, n in ((wqk, 1, 2 * D), (wvR, 2, D)):
                        for k in range(KC):
                            ins = pe.matmul(ps[:, bank, 0:n], xT[:, 0, k, 0:P], wt[:, k, :],
                                            start=(k == 0), stop=(k == KC - 1))
                    ins.then_inc(e_qk.sem, 1)
                if mid:
                    pe.wait_ge(e_st.sem, e_st.upto(t - 1))
                    pe.wait_ge(e_rv.sem, e_rv.upto(t - 1))
                    for m in range(KC):
                        pe.matmul(ps[:, 5, m * P:m * P + P], qkT[:, m, :], State[:, m, :], start=(m == 0), stop=False)
                    weigh(0)
                    scores(2)
                    weigh(1)
                    scores(3)
                if first:
                    pe.wait_ge(e_rot.sem, e_rot.upto(t + 1))
                    for k in range(2 * KC):
                        ins = pe.transpose(ps[:, 0, k * P:k * P + P], qkr[:, 1 - s, k * P:k * P + P], ident[:])
                    ins.then_inc(e_tq.sem, 1)
                if res:
                    pe.wait_ge(e_gn.sem, e_gn.upto(t - 2))
                    pe.wait_ge(e_rs.sem, e_rs.upto(t - 3))
                    for k in range(KC):
                        ins = pe.transpose(ps[:, 7, k * P:k * P + P], Rq[:, k * P:k * P + P], ident[:])
                    ins.then_inc(e_ot.sem, 1)
                if mid:
                    weigh(2)
                    weigh(3)
                    for m in range(KC):
                        ins = pe.matmul(ps[:, 6, m * P:m * P + P], qkr[:, s, D + m * P:D + m * P + P],
                                        vR[:, s, m * P:m * P + P], start=True, stop=True)
                    ins.then_inc(e_su.sem, 1)
                if res:
                    pe.wait_ge(e_oc.sem, e_oc.upto(t - 2))
                    for k in range(KC):
                        ins = pe.matmul(ps[:, 7, 0:D], oTR[:, k, :], woR[:, k, :], start=(k == 0), stop=(k == KC - 1))
                    ins.then_inc(e_y.sem, 1)
                if pre:
                    pe.wait_ge(e_ln.sem, e_ln.upto(t + 2))
                    pe.wait_ge(e_ex.sem, e_ex.upto(t + 1, 1))
                    for k in range(KC):
                        ins = pe.transpose(ps[:, 0, k * P:k * P + P], xn[:, 0, 0, k * P:k * P + P], ident[:])
                    ins.then_inc(e_tx.sem, 1)

            pe.wait_ge(e_ld, E_LOADS)
            pe.wait_ge(e_z, 1)
            steps_r(body, pe)

        def act_retention(act):
            def body(t, s, mid, first, end, res, pre):
                if first:
                    act.wait_ge(e_tq.sem, e_tq.upto(t + 1))
                    act.copy(qkT[:], ps[:, 0, :].rearrange("p (k q) -> p k q", k=2 * KC)).then_inc(e_ex.sem, 1)
                    act.wait_ge(e_ex.sem, e_ex.upto(t + 1, 1))
                    for g in range(HG):
                        ins = act.activation(qbd[:, 0, g, :], qkT[:, 0, :], ACT.Copy, scale=hmask[:, g:g + 1])
                    ins.then_inc(e_ex.sem, 1)
                if res:
                    act.wait_ge(e_ot.sem, e_ot.upto(t - 2))
                    for k in range(KC):
                        ins = act.activation(oTR[:, k, :], ps[:, 7, k * P:k * P + P], ACT.Identity,
                                             bias=beta[:, k:k + 1], scale=gamma[:, k:k + 1])
                    ins.then_inc(e_oc.sem, 1)
                if pre:
                    act.wait_ge(e_tx.sem, e_tx.upto(t + 2))
                    act.copy(xT[:, 0, :, 0:P], ps[:, 0, 0:2 * P].rearrange("p (k q) -> p k q", k=KC))\
                       .then_inc(e_xt.sem, 1)

            act.wait_ge(e_ld, E_LOADS)
            steps_r(body, act)

        def dve_retention(v, c):
            def body(t, s, mid, first, end, res, pre):
                def causal_scores(g):
                    v.wait_ge(e_s.sem, e_s.upto(t, g + 1))
                    v.wait_ge(e_av.sem, e_av.upto(t, g - 1))
                    v.tensor_tensor(wS[:, g % 2, :, :], ps[:, 3 + g % 2, :].rearrange("p (h q) -> p h q", h=4),
                                    causal[:].unsqueeze(1).to_broadcast([P, 4, P]), ALU.mult).then_inc(e_m.sem, 1)

                if mid:
                    causal_scores(0)
                    causal_scores(1)
                if first:
                    v.wait_ge(e_qk.sem, e_qk.upto(t + 1))
                    v.tensor_tensor(vR[:, 1 - s, :].rearrange("p (h d) -> p h d", h=H),
                                    ps[:, 2, 0:D].rearrange("p (h d) -> p h d", h=H),
                                    decay[:, 1, :].unsqueeze(2).to_broadcast([P, H, DH]), ALU.mult)
                    b4 = lambda a: a.rearrange("p (g r e) -> p g r e", r=DH // 2, e=2)
                    tb_ = (t + 1) % TB
                    cs = [turns[:, q, bass.ds(tb_, 1), :] for q in range(2)]
                    raw, rot, hf = b4(ps[:, 1, :]), b4(qkr[:, 1 - s, :]), b4(half_turn[:])
                    v.tensor_tensor(rot, raw, cs[0].unsqueeze(3).to_broadcast([P, 2 * H, DH // 2, 2]), ALU.mult)
                    sn = cs[1].to_broadcast([P, 2 * H, DH // 2])
                    for e in range(2):
                        ins = v.tensor_tensor(hf[:, :, :, e], raw[:, :, :, 1 - e], sn, ALU.mult)
                    c(ins)
                    v.tensor_tensor(rot[:, :, :, 0], rot[:, :, :, 0], hf[:, :, :, 0], ALU.subtract)
                    v.tensor_tensor(rot[:, :, :, 1], rot[:, :, :, 1], hf[:, :, :, 1], ALU.add)\
                     .then_inc(e_rot.sem, 1)
                if res:
                    v.wait_ge(e_gr.sem, e_gr.upto(t - 2))
                    v.tensor_tensor(Rq[:].rearrange("p (h d) -> p h d", h=H),
                                    Rr[:, s, :].rearrange("p (h d) -> p h d", h=H),
                                    gnv[:, 0, :].unsqueeze(2).to_broadcast([P, H, DH]), ALU.mult)\
                     .then_inc(e_gn.sem, 1)
                if mid:
                    causal_scores(2)
                    causal_scores(3)
                if pre:
                    v.wait_ge(e_tx.sem, e_tx.upto(t + 1))
                    norm_rows(v, xn[:, 0, 0, :], t + 2).then_inc(e_ln.sem, 1)
                if mid:
                    v.wait_ge(e_av.sem, e_av.upto(t))
                    v.tensor_tensor(Rr[:, s, :].rearrange("p (h d) -> p h d", h=H),
                                    ps[:, 5, 0:D].rearrange("p (h d) -> p h d", h=H),
                                    decay[:, 0, :].unsqueeze(2).to_broadcast([P, H, DH]), ALU.mult)\
                     .then_inc(e_rv.sem, 1)
                    v.wait_ge(e_su.sem, e_su.upto(t))
                    c(v.tensor_tensor(newS[:], ps[:, 6, 0:2 * P].rearrange("p (m q) -> p m q", m=KC), bdg[:],
                                      ALU.mult))
                    for m in range(KC):
                        ins = v.scalar_tensor_tensor(out=newS[:, m, :], in0=State[:, m, :], scalar=gP[:, m:m + 1],
                                                     in1=newS[:, m, :], op0=ALU.mult, op1=ALU.add)
                    c(ins)
                    v.tensor_scalar(State[:], newS[:], keepS[:, bass.ds(t, 1)], None, ALU.mult)\
                     .then_inc(e_st.sem, 1)
                    v.wait_ge(e_st.sem, e_st.upto(t))
                if res:
                    v.wait_ge(e_y.sem, e_y.upto(t - 2))
                    x2 = xr[:, bass.ds(t - 2, 1), :].rearrange("p a d -> p (a d)")
                    v.tensor_tensor(x2, x2, ps[:, 7, 0:D], ALU.add).then_inc(e_rs.sem, 1)
                    v.wait_ge(e_rs.sem, e_rs.upto(t - 2))
                    v.memset(idle[:, 0:1], 0.0)
                    c(row_stats(v, t - 2))
                if end:
                    R3 = Rr[:, 1 - s, :].rearrange("p (h d) -> p h d", h=H)
                    Q3 = Rq[:].rearrange("p (h d) -> p h d", h=H)
                    gb = lambda a: a.unsqueeze(2).to_broadcast([P, H, DH])
                    v.wait_ge(e_rv.sem, e_rv.upto(t - 1))
                    c(v.tensor_reduce(gmean[:], R3, AX.X, ALU.add))
                    c(v.tensor_scalar(gmean[:], gmean[:], 1.0 / DH, None, ALU.mult))
                    c(v.tensor_tensor(R3, R3, gb(gmean[:]), ALU.subtract))
                    v.wait_ge(e_ot.sem, e_ot.upto(t - 2))
                    c(v.tensor_tensor(Q3, R3, R3, ALU.mult))
                    c(v.tensor_reduce(gvar[:], Q3, AX.X, ALU.add))
                    v.wait_ge(e_gr.sem, e_gr.upto(t - 2))
                    c(v.tensor_scalar(gvar[:], gvar[:], 1.0 / DH, LN_EPS, ALU.mult, ALU.add))
                    c(v.tensor_scalar(gnv[:, 1, :].bitcast(I32), gvar[:].bitcast(I32), 1, None,
                                      ALU.logical_shift_right))
                    c(v.tensor_scalar(gnv[:, 0, :].bitcast(I32), gnv[:, 1, :].bitcast(I32), -1.0,
                                      float(0x5F3759DF), ALU.mult, ALU.add))
                    v.tensor_scalar(gnv[:, 2, :], gvar[:], -0.5, None, ALU.mult).then_inc(e_gv.sem, 1)

            v.wait_ge(e_ld, E_LOADS)
            v.memset(State[:], 0.0).then_inc(e_z, 1)
            v.wait_ge(e_z, 1)
            norm_factors(v, c)
            steps_r(body, v, c, E_LINKS)

        @block.sync
        def _(sp):
            xv = x_in.rearrange("b (t p) d -> p (b t) d", p=P)
            for q in range(4):
                load(sp, xr[:, 4 * q:4 * q + 4, :], xv[:, 4 * q:4 * q + 4, :])
            load(sp, ident[:], w["c_ident"])
            load(sp, sel[:], w["c_sel"])
            load(sp, wqA[:], chunked(w["L0_attn_Wq"]))
            load(sp, wkA[:], chunked(w["L0_attn_Wk"]))
            load(sp, wvA[:], chunked(w["L0_attn_Wv"]))
            load(sp, qwB[:], w["L0_attn_quadrant_weights"].partition_broadcast(P))
            load(sp, desc[:], w["c_desc"])
            load(sp, first[:], w["c_first"])
            load(sp, bits[:], w["c_bits"])
            load(sp, lowf[:], w["c_lower"])
            load(sp, before_e[:], w["c_before"])
            load(sp, tile_no[:], w["c_tiles"])
            sp.wait_ge(z_set, 1)
            for xs in (xs0, xs1):
                sp.dma_start(xs.rearrange("(r p) d -> p r d", p=P),
                             zrow[:].unsqueeze(1).to_broadcast([P, NX, D])).then_inc(g_z, 16)
            with sp.Fori(0, NP // 2) as i:
                for s in range(2):
                    u = 2 * i + s
                    b, t0 = u // 4, (u % 4) * 2
                    sp.wait_ge(a_p1.sem, a_p1.upto(u))
                    sp.wait_ge(a_p2.sem, a_p2.upto(u))
                    sp.wait_ge(a_p3.sem, a_p3.upto(u))
                    for a in range(3):
                        dst = qk_parts[a, bass.ds(b, 1), :, bass.ds(t0 * P, 2 * P)]
                        sp.dma_start(dst.rearrange("b (m p) s -> p (b m) s", p=P),
                                     parts[:, s, a, :, :]).then_inc(a_st[s].sem, 16)
                    sp.wait_ge(a_vs.sem, a_vs.upto(u))
                    dst = v_heads[bass.ds(b, 1), :, :, bass.ds(t0, 2), :]
                    for j in range(2):
                        sp.dma_start(dst[:, :, :, j, :].rearrange("b h p c -> p (b h) c"),
                                     vslot[:, s, j, :, :]).then_inc(a_st[s].sem, 16)
            for s in range(2):
                sp.wait_ge(a_st[s].sem, a_st[s].upto(NP // 2 - 1))

            def fetch(n, sl):
                b, r = n // H, (n % H) * DH
                for part, count, row in ((0, 3, 0), (1, 2, 48), (2, 1, 80)):
                    src = qk_parts[part, bass.ds(b, 1), bass.ds(r, DH), :].rearrange("b r s -> (b r) s")
                    sp.dma_start(QS[row:row + count * DH, sl, :], src.partition_broadcast(count))\
                      .then_inc(h_ld[sl].sem, 16)
                    src = qk_parts[0:count, bass.ds(b, 1), bass.ds(r + D, DH), :]
                    sp.dma_start(KS[row:row + count * DH, sl, :], src.rearrange("a b r s -> (a b) r s"))\
                      .then_inc(h_ld[sl].sem, 16)
                src = v_heads[bass.ds(b, 1), bass.ds(n % H, 1), :, :, :]
                sp.dma_start(VS[:, sl, :, :], src.rearrange("b h p t c -> p (b h t) c")).then_inc(h_ld[sl].sem, 16)

            def rows(n, sl):
                sp.wait_ge(h_mc.sem, h_mc.upto(n))
                sp.dma_start(QS[96:99, sl, :], mrow[:, sl % 2, :]).then_inc(h_mr[sl].sem, 16)

            for n in range(3):
                fetch(n, n)
            rows(0, 0)
            sp_cross_weights(sp, 0)

            def head(n, hh, last=False):
                if not last or hh < 1:
                    sp.wait_ge(h_pv.sem, h_pv.upto(n - 1))
                    fetch(n + 3, (hh + 3) % 4)
                if not last or hh < 3:
                    rows(n + 1, (hh + 1) % 4)

            with sp.Fori(0, B * H // 4 - 1) as i:
                for hh in range(4):
                    head(4 * i + hh, hh)
            for hh in range(4):
                head(B * H - 4 + hh, hh, True)
                sp_weights0(sp, hh // 2, hh // 2, (range(0, 2), range(2, 3))[hh % 2])
            sp_retention(sp)
            meet(sp, 1)
            sp_cross(sp, 0)
            meet(sp, 2)
            sp_experts0(sp)
            meet(sp, 3)
            sp_cross_weights(sp, 1)
            meet(sp, 4)
            sp.dma_start(wide[:].rearrange("p (g f) -> p g f", f=F),
                         w["L1_ffn_w1"].rearrange("e (k p) f -> p (e k) f", p=P)).then_inc(m_w, 16)
            sp_cross(sp, 1)
            meet(sp, 5)
            sp_experts1(sp)
            meet(sp, 6)
            finish(sp)

        @block.gpsimd
        def _(pool):
            for s in sigs:
                pool.sem_inc(s.sem, LAG * s.per)
            c = Chain(pool, chain_pool)
            c(pool.memset(zeros[:], 0.0))
            c(pool.memset(onesb[:], 1.0))
            pool.memset(zrow[:], 0.0).then_inc(z_set, 1)
            pool.wait_ge(z_set, 1)
            c(pool.memset(vslot[:], 0.0))
            pool.memset(KS[96:99, :, :], 1.0).then_inc(ones_set, 1)
            pool.wait_ge(ones_set, 1)
            pool.memset(vslot[:, :, :, :, DH:DH + 1], 1.0).then_inc(v_set, 1)
            pool.wait_ge(v_set, 1)

            with pool.Fori(0, NP // 2) as i:
                for s in range(2):
                    u = 2 * i + s
                    pool.wait_ge(a_r.sem, a_r.upto(u))
                    pool.wait_ge(a_st[s].sem, a_st[s].upto(i - 1))
                    pool.tensor_tensor(parts[:, s, 1, :, :], rest[:, s, :, :], zeros[:].unsqueeze(2).to_broadcast([P, 4, 2 * P]), ALU.add).then_inc(a_p2.sem, 1)
                    pool.wait_ge(a_p2.sem, a_p2.upto(u))
                    pool.tensor_tensor(parts[:, s, 2, :, :], rest[:, s, :, :], parts[:, s, 1, :, :],
                                       ALU.subtract).then_inc(a_p3.sem, 1)
            meet(pool, 1)
            meet(pool, 2)
            pool_scatter(pool, c, 0, xs0, E * CAP)
            pool_gather(pool, c, 0, ys0, E * CAP, [(f_ys.sem, f_ys.upto(E - 1))])
            meet(pool, 3)
            pool.wait_ge(e_ld, E_LOADS)

            c(pool.memset(three_halves[:], 1.5))

            def expand(t):
                pool.wait_ge(e_ex.sem, e_ex.upto(t, 1))
                pool.tensor_tensor(qbd[:, 1, :, :], qkT[:, 1:2, :].to_broadcast([P, HG, P]),
                                   hmask[:].unsqueeze(2).to_broadcast([P, HG, P]), ALU.mult).then_inc(e_ex1.sem, 1)
                pool.wait_ge(e_ex1.sem, e_ex1.upto(t))

            def group_factors(t):
                pool.wait_ge(e_gv.sem, e_gv.upto(t))
                pool.wait_ge(e_gn.sem, e_gn.upto(t - 1))
                newton(pool, c, gnv)
                pool.tensor_tensor(gnv[:, 0, :], gnv[:, 0, :], gnv[:, 1, :], ALU.mult).then_inc(e_gr.sem, 1)
                pool.wait_ge(e_gr.sem, e_gr.upto(t))

            expand(0)
            expand(1)
            with c.fori(NT - 2, POOL_LINKS) as i:
                expand(i + 2)
                group_factors(i)
            group_factors(NT - 2)
            group_factors(NT - 1)
            meet(pool, 4)
            meet(pool, 5)
            pool_scatter(pool, c, 1, xs1, NX * P)
            pool_gather(pool, c, 1, ys1, NX * P, [(s.sem, s.upto(NX // 2 - 1)) for s in m_st])
            meet(pool, 6)

        @block.scalar
        def _(act):
            c = Chain(act, chain_act)
            act.wait_ge(q_sub, 1)
            act.activation(qsm[:, 2, :], qsm[:, 1, :], ACT.Exp).then_inc(q_exp, 1)
            act.wait_ge(v_set, 1)
            with act.Fori(0, NP // 2) as i:
                for s in range(2):
                    u = 2 * i + s
                    act.wait_ge(a_tr.sem, a_tr.upto(u))
                    act.wait_ge(a_v.sem, a_v.upto(u - 2))
                    act.copy(xT[:, s, :, :], ps[:, s, :].rearrange("p (k q) -> p k q", k=KC))\
                       .then_inc(a_xt.sem, 1)
                    act.wait_ge(a_qk.sem, a_qk.upto(u))
                    act.wait_ge(a_st[s].sem, a_st[s].upto(i - 1))
                    act.copy(parts[:, s, 0, :, :],
                             ps[:, 2 + 2 * s:4 + 2 * s, :].rearrange("p m (n q) -> p (m n) q", n=2))\
                       .then_inc(a_p1.sem, 1)
                    act.wait_ge(a_v.sem, a_v.upto(u))
                    act.copy(vslot[:, s, :, :, 0:DH],
                             ps[:, 6 + s, :].rearrange("p (j h d) -> p j h d", j=2, h=H))\
                       .then_inc(a_vs.sem, 1)

            def exps(n, q0, q1):
                for q in range(q0, q1):
                    act.wait_ge(h_st.sem, h_st.upto(n, q + 1))
                    act.wait_ge(h_pv.sem, h_pv.upto(n, q - 3))
                    act.activation(PT[:, q % 4, :], ps[:, 4 + q % 2, :], ACT.Exp).then_inc(h_e.sem, 1)

            def evac(n):
                act.wait_ge(h_pv.sem, h_pv.upto(n))
                act.wait_ge(h_fin.sem, h_fin.upto(n - 1))
                act.copy(Osb[:], ps[:, 6, :]).then_inc(h_ev.sem, 1)

            def head(n, first=False):
                exps(n, 0, 2)
                if not first:
                    evac(n - 1)
                exps(n, 2, 16)

            for n in range(4):
                head(n, n == 0)
            with act.Fori(1, B * H // 4) as i:
                for hh in range(4):
                    head(4 * i + hh)
            evac(B * H - 1)
            meet(act, 1)
            act_cross(act, c, 0)
            meet(act, 2)
            act.wait_ge(r_sub, 1)
            act.activation(pe_[:], pe_[:], ACT.Exp).then_inc(r_exp, 1)
            act_experts0(act)
            meet(act, 3)
            act_retention(act)
            meet(act, 4)
            act_cross(act, c, 1)
            meet(act, 5)
            act.wait_ge(r_sub, 2)
            act.activation(pe_[:], pe_[:], ACT.Exp).then_inc(r_exp, 1)
            act_experts1(act)
            meet(act, 6)

        @block.vector
        def _(v):
            c = Chain(v, chain_dve)
            v.wait_ge(loaded, A_LOADS)
            c(v.tensor_copy(identb[:], ident[:]))
            c(v.tensor_copy(lower[:], lowf[:]))
            for t in range(NT):
                ins = v.bn_stats(stats[:, t, :], xr[:, t, :])
            c(ins)
            norm_factors(v, c)
            c(v.tensor_reduce(qsm[:, 0, 0:1], qwB[:], AX.X, ALU.max))
            v.tensor_scalar(qsm[:, 1, :], qwB[:], qsm[:, 0, 0:1], None, ALU.subtract).then_inc(q_sub, 1)
            v.wait_ge(q_exp, 1)
            c(v.tensor_reduce(qsm[:, 0, 0:1], qsm[:, 2, :], AX.X, ALU.add))
            c(v.reciprocal(qsm[:, 0, 1:2], qsm[:, 0, 0:1]))
            c(v.tensor_scalar(qsm[:, 3, :], qsm[:, 2, :], qsm[:, 0, 1:2], float((DH // 2) ** -0.5),
                              ALU.mult, ALU.mult))
            half = lambda m, e: m[:].rearrange("p k (h e d) -> p (k h) e d", h=H, e=2)[:, :, e, :]
            for e in range(2):
                c(v.tensor_scalar(half(wkE, e), half(wkA, 0), qsm[:, 3, 2 * e:2 * e + 1], None, ALU.mult))
                ins = v.scalar_tensor_tensor(out=half(wkE, e), in0=half(wkA, 1),
                                             scalar=qsm[:, 3, 2 * e + 1:2 * e + 2], in1=half(wkE, e),
                                             op0=ALU.mult, op1=ALU.add)
            ins.then_inc(a_w, 1)

            def qk_rest(u, s):
                v.wait_ge(a_p1.sem, a_p1.upto(u))
                v.wait_ge(a_p3.sem, a_p3.upto(u - 2))
                v.tensor_tensor(rest[:, s, :, :],
                                ps[:, 2 + 2 * s:4 + 2 * s, :].rearrange("p m (n q) -> p (m n) q", n=2),
                                parts[:, s, 0, :, :], ALU.subtract).then_inc(a_r.sem, 1)

            ln_rows(v, 0, 0, a_xn, a_tr)
            with v.Fori(0, NP // 2 - 1) as i:
                for s in range(2):
                    ln_rows(v, 2 * i + s + 1, 1 - s, a_xn, a_tr)
                    qk_rest(2 * i + s, s)
            ln_rows(v, NP - 1, 1, a_xn, a_tr)
            qk_rest(NP - 2, 0)
            qk_rest(NP - 1, 1)

            def maxima(n, s, t0, t1):
                for t in range(t0, t1):
                    v.wait_ge(h_s.sem, h_s.upto(n, t + 1))
                    v.tensor_reduce(mx[:, s, t:t + 1], ps[:, 2 * (t % 2):2 * (t % 2) + 2, :], AX.XY,
                                    ALU.max).then_inc(h_rm.sem, 1)

            def split_max(n, s):
                v.wait_ge(h_rm.sem, h_rm.upto(n))
                c(v.tensor_scalar(mneg[:, 0, :], mx[:, s, :], -1.0, None, ALU.mult))
                v.wait_ge(h_mt.sem, h_mt.upto(n - 2))
                c(v.tensor_copy(mpart[:, s, 0, :], mneg[:, 0, :]))
                c(v.tensor_tensor(mneg[:, 1, :], mneg[:, 0, :], mpart[:, s, 0, :], ALU.subtract))
                c(v.tensor_copy(mpart[:, s, 1, :], mneg[:, 1, :]))
                v.tensor_tensor(mpart[:, s, 2, :], mneg[:, 1, :], mpart[:, s, 1, :], ALU.subtract)\
                 .then_inc(h_mp.sem, 1)

            def copy_max(n, s, sl, step):
                v.wait_ge(h_mt.sem, h_mt.upto(n))
                v.wait_ge(h_mr[sl].sem, h_mr[sl].upto(step - 1) if sl >= 2 else h_mr[sl].upto(step - 1))
                v.tensor_copy(mrow[:, s, :], ps[0:24, 7, 0:P // 2].bitcast(BF16)).then_inc(h_mc.sem, 1)

            def normalise(n):
                v.wait_ge(h_fin.sem, h_fin.upto(n))
                y = ps[:, 7, 0:256].rearrange("p (j c d) -> p j c d", j=4, c=2)
                c(v.reciprocal(rec[:].unsqueeze(3), y[:, :, :, DH:DH + 1]))
                o = O_all[:, bass.ds((n // H) * TB, TB), bass.ds((n % H) * DH, DH)]\
                    .rearrange("p (c j) d -> p j c d", c=2)
                v.tensor_tensor(o, y[:, :, :, 0:DH], rec[:].unsqueeze(3).to_broadcast([P, 4, 2, DH]),
                                ALU.mult).then_inc(h_no.sem, 1)

            def head(n, hh, i, first=False, last=False):
                split_max(n + 1, (hh + 1) % 2) if not (last and hh == 3) else None
                if not (last and hh >= 2):
                    maxima(n + 2, hh % 2, 0, 3)
                if not first:
                    normalise(n - 1)
                if not (last and hh >= 2):
                    maxima(n + 2, hh % 2, 3, 6)
                if not (last and hh == 3):
                    copy_max(n + 1, (hh + 1) % 2, (hh + 1) % 4, i + (hh + 1) // 4)
                if not (last and hh >= 2):
                    maxima(n + 2, hh % 2, 6, 8)

            maxima(0, 0, 0, 8)
            split_max(0, 0)
            maxima(1, 1, 0, 6)
            copy_max(0, 0, 0, 0)
            maxima(1, 1, 6, 8)
            for n in range(4):
                head(n, n, 0, n == 0)
            with c.fori(B * H // 4 - 2, 4 * 5) as i:
                for hh in range(4):
                    head(4 * i + 4 + hh, hh, i + 1)
            for hh in range(4):
                head(B * H - 4 + hh, hh, B * H // 4 - 1, False, True)
            normalise(B * H - 1)
            meet(v, 1)
            dve_cross(v, c, 0)
            meet(v, 2)
            dve_route0(v, c)
            dve_experts0(v, c)
            dve_combine(v, c, 0)
            meet(v, 3)
            dve_retention(v, c)
            meet(v, 4)
            dve_cross(v, c, 1)
            meet(v, 5)
            dve_route1(v, c)
            dve_experts1(v, c)
            dve_combine(v, c, 1)
            meet(v, 6)

        @block.tensor
        def _(pe):
            def project(u, s):
                pe.wait_ge(a_xt.sem, a_xt.upto(u))
                pe.wait_ge(a_r.sem, a_r.upto(u - 2))
                for m in range(4):
                    wm = (wqA, wkE)[m // 2]
                    for k in range(KC):
                        ins = pe.matmul(ps[:, 2 + 2 * s + m // 2, (m % 2) * 256:(m % 2) * 256 + 256],
                                        wm[:, k, (m % 2) * P:(m % 2) * P + P], xT[:, s, k, :],
                                        start=(k == 0), stop=(k == KC - 1))
                ins.then_inc(a_qk.sem, 1)
                pe.wait_ge(a_vs.sem, a_vs.upto(u - 2))
                for j in range(2):
                    for k in range(KC):
                        ins = pe.matmul(ps[:, 6 + s, j * 256:j * 256 + 256], xT[:, s, k, j * P:j * P + P],
                                        wvA[:, k, :], start=(k == 0), stop=(k == KC - 1))
                ins.then_inc(a_v.sem, 1)

            pe.wait_ge(loaded, A_LOADS)
            transpose_rows(pe, 0, 0, 0, a_xn, a_xt, a_tr)
            pe.wait_ge(a_w, 1)
            with pe.Fori(0, NP // 2 - 1) as i:
                for s in range(2):
                    transpose_rows(pe, 2 * i + s + 1, 1 - s, 1 - s, a_xn, a_xt, a_tr)
                    project(2 * i + s, s)
            transpose_rows(pe, NP - 1, 1, 1, a_xn, a_xt, a_tr)
            project(NP - 2, 0)
            project(NP - 1, 1)

            for s_ in (a_xt, a_r, a_vs):
                pe.wait_ge(s_.sem, s_.upto(NP - 1))

            def scores(n, sl, t):
                pe.wait_ge(h_rm.sem, h_rm.upto(n, t - 1))
                for q in range(2):
                    ins = pe.matmul(ps[:, 2 * (t % 2) + q, :], QS[0:96, sl, t * P:t * P + P],
                                    KS[0:96, sl, q * 512:q * 512 + 512], start=True, stop=True)
                ins.then_inc(h_s.sem, 1)

            def scores_t(n, sl, t):
                for q in range(2):
                    pe.wait_ge(h_e.sem, h_e.upto(n, 2 * t + q - 1))
                    pe.matmul(ps[:, 4 + q, :], KS[0:99, sl, t * P:t * P + P],
                              QS[0:99, sl, q * 512:q * 512 + 512], start=True, stop=True)\
                      .then_inc(h_st.sem, 1)

            def weigh(n, sl, t):
                for q in range(2):
                    g = 32 * (2 * (t % 2) + q)
                    pe.wait_ge(h_e.sem, h_e.upto(n, 2 * t + q + 1))
                    pe.matmul(ps[g:g + 32, 6, :], VS[:, sl, t, :], PT[:, (2 * t + q) % 4, :],
                              start=(t < 2), stop=(t >= 6)).then_inc(h_pv.sem, 1)

            def sum_tiles(n):
                pe.wait_ge(h_ev.sem, h_ev.upto(n))
                pe.wait_ge(h_mc.sem, h_mc.upto(n + 1))
                for j in range(4):
                    ins = pe.matmul(ps[:, 7, j * 64:j * 64 + 64], Osb[:, j * P:j * P + P], sel[:],
                                    start=True, stop=True)
                ins.then_inc(h_fin.sem, 1)

            def turn_max(n, s):
                pe.wait_ge(h_mp.sem, h_mp.upto(n))
                pe.wait_ge(h_no.sem, h_no.upto(n - 2))
                pe.transpose(ps[0:24, 7, 0:P // 2].bitcast(BF16),
                             mpart[:, s, :, :].rearrange("p a t -> p (a t)"), identb[:])\
                  .then_inc(h_mt.sem, 1)

            def head(n, hh, i, first=False, last=False):
                sl, s2 = hh, (hh + 2) % 4
                ahead = not (last and hh >= 2)
                pe.wait_ge(h_mr[sl].sem, h_mr[sl].upto(i))
                if ahead:
                    pe.wait_ge(h_ld[s2].sem, h_ld[s2].upto(i + (hh + 2) // 4))
                for t in range(TB):
                    scores_t(n, sl, t)
                    if ahead:
                        scores(n + 2, s2, t)
                    if t > 0:
                        if t == 1:
                            pe.wait_ge(h_ev.sem, h_ev.upto(n - 1))
                        weigh(n, sl, t - 1)
                    elif not first:
                        weigh(n - 1, (sl + 3) % 4, TB - 1)
                    if t == 2 and not first:
                        sum_tiles(n - 1)
                    if t == 4 and not (last and hh == 3):
                        turn_max(n + 1, (hh + 1) % 2)

            pe.wait_ge(ones_set, 1)
            for n in range(2):
                pe.wait_ge(h_ld[n].sem, h_ld[n].upto(0))
                for t in range(TB):
                    scores(n, n, t)
                    if n == 1 and t == 4:
                        turn_max(0, 0)
            for n in range(4):
                head(n, n, 0, n == 0)
            with pe.Fori(1, B * H // 4 - 1) as i:
                for hh in range(4):
                    head(4 * i + hh, hh, i)
            for hh in range(4):
                head(B * H - 4 + hh, hh, B * H // 4 - 1, False, True)
            weigh(B * H - 1, 3, TB - 1)
            pe.wait_ge(h_ev.sem, h_ev.upto(B * H - 1))
            pe.wait_ge(h_no.sem, h_no.upto(B * H - 2))
            for j in range(4):
                ins = pe.matmul(ps[:, 7, j * 64:j * 64 + 64], Osb[:, j * P:j * P + P], sel[:],
                                start=True, stop=True)
            ins.then_inc(h_fin.sem, 1)
            meet(pe, 1)
            pe_cross(pe, 0)
            meet(pe, 2)
            pe_route0(pe)
            pe_experts0(pe)
            meet(pe, 3)
            pe_retention(pe)
            meet(pe, 4)
            pe_cross(pe, 1)
            meet(pe, 5)
            pe_count(pe, BITS + 4)
            pe_before(pe, BITS + 5)
            pe_experts1(pe)
            meet(pe, 6)


_NAMES = ["x", "ctx_1024", "mask_1x1xSxS2_bk0", "mask_Bx1x1xS2_bf1"]


def kernel(**inputs):
    import concourse.bacc as _bacc
    from concourse.bass_utils import run_bass_kernel_spmd as _run

    nc = _bacc.Bacc("TRN2", target_bir_lowering=False, num_devices=1)
    arrays, aps = {}, {}

    def give(name, a):
        a = np.ascontiguousarray(a)
        arrays["in_" + name] = a
        aps[name] = nc.dram_tensor("in_" + name, a.shape, mybir.dt.from_np(a.dtype), kind="ExternalInput").ap()

    give("c_ident", np.eye(P, dtype=np.float32))
    rows = np.arange(P)
    give("c_sel", (rows[:, None] % 64 == np.arange(64)[None, :]).astype(np.float32))
    give("c_desc", np.tile(E - np.arange(E, dtype=np.float32), (P, 1)))
    give("c_first", np.tile(CAP * np.arange(E, dtype=np.float32), (P, 1)))
    give("c_before", np.tile(np.tri(E, E, -1, dtype=np.float32)[None], (P, 1, 1)))
    give("c_tiles", np.tile(np.arange(NX, dtype=np.float32), (P, 1)))
    give("c_bits", np.tile((1 << np.arange(29, -1, -1))[None, :, None], (P, 1, E)).astype(np.int32))
    give("c_lower", (rows[:, None] < rows[None, :]).astype(np.float32))
    give("c_hmask", (rows[:, None] // DH == np.arange(HG)[None, :]).astype(np.float32))
    give("c_halves", (rows[:, None] // SC == np.arange(2)[None, :]).astype(np.float32))
    g = 1.0 - 2.0 ** (-5.0 - np.arange(H))
    spot = np.arange(P)[:, None] + 1
    give("c_decay", np.stack([g ** spot, g ** -spot], 1).astype(np.float32))
    gd = (g ** P).reshape(KC, HG).repeat(DH, 1)
    give("c_gP", gd.T.astype(np.float32))
    give("c_bdg", ((rows[:, None, None] // DH == rows[None, None, :] // DH) * gd.T[:, :, None]).astype(np.float32))
    give("c_causal", (rows[:, None] <= rows[None, :]).astype(np.float32))
    give("c_keep", np.tile((np.arange(NT) % TB != TB - 1).astype(np.float32), (P, 1)))
    rate = (10.0 ** (-4.0 * np.arange(0, DH, 2, dtype=np.float32) / DH)).astype(np.float32)
    turn = (np.arange(S, dtype=np.float32)[:, None] * rate[None, :]).astype(np.float64)
    give("c_turns", np.stack([np.cos(turn), np.sin(turn)]).reshape(2, TB, P, DH // 2)
         .transpose(2, 0, 1, 3).astype(np.float32))
    for name, a in inputs.items():
        a = np.asarray(a)
        if name == "ctx_1024":
            a = a.reshape(B * SC, D).T
        elif name.startswith("L0_xattn_W"):
            a = a.T
        elif name in ("L1_attn_WQ", "L1_attn_WK", "L1_attn_WV"):
            a = a.reshape(D, D).T
        elif name in ("L0_ffn_ff_pre_act_weight", "L0_ffn_gate_weight", "L0_ffn_ff_post_act_weight"):
            a = a.transpose(0, 2, 1)
        elif name in ("L1_attn_gamma", "L1_attn_beta", "L0_xattn_bq", "L0_xattn_bk", "L1_xattn_bq", "L1_xattn_bk"):
            a = a.reshape(KC, P).T
        elif name == "L1_ffn_b1":
            a = a.reshape(E, F // P, P).transpose(2, 0, 1)
        elif name == "L0_ffn_router_weight":
            a = a.T
        give(name, a)
    out = nc.dram_tensor("out_0", (B, S, D), F32, kind="ExternalOutput").ap()
    decoder(nc, aps["x"], aps["ctx_1024"], aps["mask_1x1xSxS2_bk0"], aps["mask_Bx1x1xS2_bf1"], aps, out)
    r = _run(nc, [arrays], core_ids=[0])
    return r.results[0]["out_0"]
```
